# Optimizing a Trainium2 kernel written in Bass

```python
import numpy as np
import jax
import jax.numpy as jnp

def _softmax(x, axis=-1):
    return jax.nn.softmax(x, axis=axis)

def _gelu(x):
    return jax.nn.gelu(x, approximate=True)

def _silu(x):
    return jax.nn.silu(x)

def _sigmoid(x):
    return jax.nn.sigmoid(x)

def _layernorm(x, axis=-1, eps=1e-05):
    m = jnp.mean(x, axis=axis, keepdims=True)
    v = jnp.var(x, axis=axis, keepdims=True)
    return (x - m) / jnp.sqrt(v + eps)

def _scatter_add(tgt, idx, src, axis=0):
    return tgt.at[idx].add(src)

def _segment_sum(src, seg, n):
    return jax.ops.segment_sum(src, seg, n)
kernel_name = 'mk_adaln_ffn_d2_seqx_r8_c1b74d'

def setup_inputs(seed: int=0):
    np.random.seed(seed)
    _w = jnp.asarray

    def _rec_inputs():
        import jax
        import jax.numpy as jnp
        _rk = jax.random.key(seed)
        x = -0.0002928 + 1 * jax.random.normal(jax.random.fold_in(_rk, 1), (16, 128, 128), jnp.float32)
        _lenS = 128 - jax.random.randint(jax.random.fold_in(_rk, 7), (16,), 0, max(1, 128 // 4) + 1, jnp.int32)
        _lenS2 = 128 - jax.random.randint(jax.random.fold_in(_rk, 8), (16,), 0, max(1, 128 // 4) + 1, jnp.int32)
        cond_256 = -0.0209273 + 1.04763 * jax.random.normal(jax.random.fold_in(_rk, 11), (16, 32), jnp.float32)
        return (x, cond_256)
    x, cond_256 = _rec_inputs()

    def _L0_cond_setup():
        import jax, jax.numpy as jnp
        import numpy as np
        B, S, E, H, CD = (4, 128, 128, 16, 32)
        HD = E // H
        FIELD_COHERENCE = 0.7
        COH_THRESHOLD = 0.5
        FIELD_COUPLING = 0.3

        def _layernorm(x, g, b, eps=1e-05):
            mu = x.mean(-1, keepdims=True)
            var = ((x - mu) ** 2).mean(-1, keepdims=True)
            return (x - mu) * jax.lax.rsqrt(var + eps) * g + b
        key = jax.random.key(seed)
        ks = jax.random.split(key, 10)
        s = 0.02
        f32 = jnp.float32
        return {'x': jax.random.normal(ks[0], (B, S, E), f32), 'consciousness_state': jax.random.normal(ks[1], (B, CD), f32), 'Wqkv': jax.random.normal(ks[2], (3 * E, E), f32) * s, 'bqkv': jnp.zeros((3 * E,), f32), 'Wout': jax.random.normal(ks[3], (E, E), f32) * s, 'bout': jnp.zeros((E,), f32), 'Wc1': jax.random.normal(ks[4], (E, E + CD), f32) * s, 'bc1': jnp.zeros((E,), f32), 'Wc2': jax.random.normal(ks[5], (H, E), f32) * s, 'bc2': jnp.zeros((H,), f32), 'We1': jax.random.normal(ks[6], (E, CD), f32) * s, 'be1': jnp.zeros((E,), f32), 'We2': jax.random.normal(ks[7], (E, E), f32) * s, 'be2': jnp.zeros((E,), f32), 'ln_g': jnp.ones((E,), f32), 'ln_b': jnp.zeros((E,), f32)}
    _L0_cond_all = _L0_cond_setup()
    _L0_cond_in = {k: v for k, v in _L0_cond_all.items() if k in ('Wqkv', 'bqkv', 'Wout', 'bout', 'Wc1', 'bc1', 'Wc2', 'bc2', 'We1', 'be1', 'We2', 'be2', 'ln_g', 'ln_b')}
    del _L0_cond_all

    def _L0_ffn_setup():
        import jax, jax.numpy as jnp
        import numpy as np
        H = 8
        KD = 128
        TOPK = 8
        NUM_KEYS = 32
        N_EXPERTS = NUM_KEYS * NUM_KEYS
        N_DIM = 128
        BN_EPS = 1e-05

        def gelu_new(x):
            c = jnp.sqrt(jnp.asarray(2.0 / jnp.pi, x.dtype))
            return 0.5 * x * (1.0 + jnp.tanh(c * (x + 0.044715 * x * x * x)))
        key = jax.random.key(seed)
        ks = jax.random.split(key, 5)
        b, s = (2, 128)
        x = jax.random.normal(ks[0], (b, s, N_DIM), dtype=jnp.float32)
        w_q = jax.random.normal(ks[1], (N_DIM, 2 * H * KD), dtype=jnp.float32) * 0.02
        bn_gamma = jnp.ones((2 * H * KD,), dtype=jnp.float32)
        bn_beta = jnp.zeros((2 * H * KD,), dtype=jnp.float32)
        keys = jax.random.normal(ks[2], (H, NUM_KEYS, 2, KD), dtype=jnp.float32) * 0.02
        down_embed = jax.random.normal(ks[3], (N_EXPERTS, N_DIM), dtype=jnp.float32) * 0.02
        up_embed = jax.random.normal(ks[4], (N_EXPERTS, N_DIM), dtype=jnp.float32) * 0.02
        return {'x': x, 'w_q': w_q, 'bn_gamma': bn_gamma, 'bn_beta': bn_beta, 'keys': keys, 'down_embed': down_embed, 'up_embed': up_embed}
    _L0_ffn_all = _L0_ffn_setup()
    _L0_ffn_in = {k: v for k, v in _L0_ffn_all.items() if k in ('w_q', 'bn_gamma', 'bn_beta', 'keys', 'down_embed', 'up_embed')}
    del _L0_ffn_all

    def _L1_cond_setup():
        import jax, jax.numpy as jnp
        import numpy as np
        TOP_K = 2
        EPS = 1e-06
        B, S, H, G, E, M = (2, 256, 128, 32, 8, 256)
        key = jax.random.key(seed)
        ks = jax.random.split(key, 16)
        s_h = 1.0 / np.sqrt(H)
        s_g = 1.0 / np.sqrt(G)
        s_m = 1.0 / np.sqrt(M)
        return {'x': jax.random.normal(ks[0], (B, S, H), jnp.float32), 'genre_embed': jax.random.normal(ks[1], (B, 1, G), jnp.float32), 'rms_w': jnp.ones((H,), jnp.float32), 'wg_W': jax.random.normal(ks[2], (H, E), jnp.float32) * s_h, 'wg_b': jnp.zeros((E,), jnp.float32), 'gg_W': jax.random.normal(ks[3], (G, E), jnp.float32) * s_g, 'gg_b': jnp.zeros((E,), jnp.float32), 'W1': jax.random.normal(ks[4], (E, H, M), jnp.float32) * s_h, 'b1': jnp.zeros((E, M), jnp.float32), 'W2': jax.random.normal(ks[5], (E, M, M), jnp.float32) * s_m, 'b2': jnp.zeros((E, M), jnp.float32), 'W3': jax.random.normal(ks[6], (E, M, H), jnp.float32) * s_m, 'b3': jnp.zeros((E, H), jnp.float32)}
    _L1_cond_all = _L1_cond_setup()
    _L1_cond_in = {k: v for k, v in _L1_cond_all.items() if k in ('rms_w', 'wg_W', 'wg_b', 'gg_W', 'gg_b', 'W1', 'b1', 'W2', 'b2', 'W3', 'b3')}
    del _L1_cond_all

    def _L1_ffn_setup():
        import jax, jax.numpy as jnp
        import numpy as np
        TOP_K = 2
        key = jax.random.key(seed)
        ks = jax.random.split(key, 6)
        B, L, D, E, F = (2, 256, 128, 8, 512)
        x = jax.random.normal(ks[0], (B, L, D), dtype=jnp.float32)
        Wg = jax.random.normal(ks[1], (D, E), dtype=jnp.float32) * D ** (-0.5)
        W1 = jax.random.normal(ks[2], (E, D, F), dtype=jnp.float32) * D ** (-0.5)
        b1 = jnp.zeros((E, F), dtype=jnp.float32)
        W2 = jax.random.normal(ks[3], (E, F, D), dtype=jnp.float32) * F ** (-0.5)
        b2 = jnp.zeros((E, D), dtype=jnp.float32)
        return {'x': x, 'Wg': Wg, 'W1': W1, 'b1': b1, 'W2': W2, 'b2': b2}
    _L1_ffn_all = _L1_ffn_setup()
    _L1_ffn_in = {k: v for k, v in _L1_ffn_all.items() if k in ('Wg', 'W1', 'b1', 'W2', 'b2')}
    del _L1_ffn_all
    return {'x': x, 'cond_256': cond_256, 'L0_cond_Wqkv': _L0_cond_in['Wqkv'], 'L0_cond_bqkv': _L0_cond_in['bqkv'], 'L0_cond_Wout': _L0_cond_in['Wout'], 'L0_cond_bout': _L0_cond_in['bout'], 'L0_cond_Wc1': _L0_cond_in['Wc1'], 'L0_cond_bc1': _L0_cond_in['bc1'], 'L0_cond_Wc2': _L0_cond_in['Wc2'], 'L0_cond_bc2': _L0_cond_in['bc2'], 'L0_cond_We1': _L0_cond_in['We1'], 'L0_cond_be1': _L0_cond_in['be1'], 'L0_cond_We2': _L0_cond_in['We2'], 'L0_cond_be2': _L0_cond_in['be2'], 'L0_cond_ln_g': _L0_cond_in['ln_g'], 'L0_cond_ln_b': _L0_cond_in['ln_b'], 'L0_ffn_w_q': _L0_ffn_in['w_q'], 'L0_ffn_bn_gamma': _L0_ffn_in['bn_gamma'], 'L0_ffn_bn_beta': _L0_ffn_in['bn_beta'], 'L0_ffn_keys': _L0_ffn_in['keys'], 'L0_ffn_down_embed': _L0_ffn_in['down_embed'], 'L0_ffn_up_embed': _L0_ffn_in['up_embed'], 'L1_cond_rms_w': _L1_cond_in['rms_w'], 'L1_cond_wg_W': _L1_cond_in['wg_W'], 'L1_cond_wg_b': _L1_cond_in['wg_b'], 'L1_cond_gg_W': _L1_cond_in['gg_W'], 'L1_cond_gg_b': _L1_cond_in['gg_b'], 'L1_cond_W1': _L1_cond_in['W1'], 'L1_cond_b1': _L1_cond_in['b1'], 'L1_cond_W2': _L1_cond_in['W2'], 'L1_cond_b2': _L1_cond_in['b2'], 'L1_cond_W3': _L1_cond_in['W3'], 'L1_cond_b3': _L1_cond_in['b3'], 'L1_ffn_Wg': _L1_ffn_in['Wg'], 'L1_ffn_W1': _L1_ffn_in['W1'], 'L1_ffn_b1': _L1_ffn_in['b1'], 'L1_ffn_W2': _L1_ffn_in['W2'], 'L1_ffn_b2': _L1_ffn_in['b2']}

def reference(x, cond_256, L0_cond_Wqkv, L0_cond_bqkv, L0_cond_Wout, L0_cond_bout, L0_cond_Wc1, L0_cond_bc1, L0_cond_Wc2, L0_cond_bc2, L0_cond_We1, L0_cond_be1, L0_cond_We2, L0_cond_be2, L0_cond_ln_g, L0_cond_ln_b, L0_ffn_w_q, L0_ffn_bn_gamma, L0_ffn_bn_beta, L0_ffn_keys, L0_ffn_down_embed, L0_ffn_up_embed, L1_cond_rms_w, L1_cond_wg_W, L1_cond_wg_b, L1_cond_gg_W, L1_cond_gg_b, L1_cond_W1, L1_cond_b1, L1_cond_W2, L1_cond_b2, L1_cond_W3, L1_cond_b3, L1_ffn_Wg, L1_ffn_W1, L1_ffn_b1, L1_ffn_W2, L1_ffn_b2):
    import jax
    import jax.numpy as jnp

    def _L0_cond_ref(x, consciousness_state, Wqkv, bqkv, Wout, bout, Wc1, bc1, Wc2, bc2, We1, be1, We2, be2, ln_g, ln_b):
        import jax, jax.numpy as jnp
        import numpy as np
        B, S, E, H, CD = (4, 128, 128, 16, 32)
        HD = E // H
        FIELD_COHERENCE = 0.7
        COH_THRESHOLD = 0.5
        FIELD_COUPLING = 0.3

        def _layernorm(x, g, b, eps=1e-05):
            mu = x.mean(-1, keepdims=True)
            var = ((x - mu) ** 2).mean(-1, keepdims=True)
            return (x - mu) * jax.lax.rsqrt(var + eps) * g + b
        Bb, Ss, Ee = x.shape
        qkv = (x @ Wqkv.T + bqkv).reshape(Bb, Ss, 3, H, HD).transpose(2, 0, 3, 1, 4)
        q, k, v = (qkv[0], qkv[1], qkv[2])
        attn = jax.nn.softmax(jnp.einsum('bhid,bhjd->bhij', q, k) / jnp.sqrt(jnp.float32(HD)), axis=-1)
        cs_exp = jnp.broadcast_to(consciousness_state[:, None, :], (Bb, Ss, CD))
        comb = jnp.concatenate([x, cs_exp], axis=-1)
        coh = jax.nn.sigmoid(jnp.tanh(comb @ Wc1.T + bc1) @ Wc2.T + bc2).transpose(0, 2, 1)
        mod = attn * coh[..., None]
        mod = mod / (mod.sum(-1, keepdims=True) + 1e-08)
        fp = _layernorm(jax.nn.relu(consciousness_state @ We1.T + be1) @ We2.T + be2, ln_g, ln_b)
        pos = jnp.arange(Ss, dtype=jnp.float32)
        inv = 10000.0 ** jnp.repeat(jnp.arange(0, Ee, 2, dtype=jnp.float32) / Ee, 2)
        pe = jnp.sin(pos[:, None] / inv[None, :])
        fa = jax.nn.softmax(jnp.einsum('be,se->bs', fp, pe), axis=-1)
        fi = FIELD_COUPLING * FIELD_COHERENCE
        mod = (1.0 - fi) * mod + fi * fa[:, None, :, None]
        out = jnp.einsum('bhij,bhjd->bhid', mod, v).transpose(0, 2, 1, 3).reshape(Bb, Ss, Ee)
        return out @ Wout.T + bout

    def _L0_ffn_ref(x, w_q, bn_gamma, bn_beta, keys, down_embed, up_embed):
        import jax, jax.numpy as jnp
        import numpy as np
        H = 8
        KD = 128
        TOPK = 8
        NUM_KEYS = 32
        N_EXPERTS = NUM_KEYS * NUM_KEYS
        N_DIM = 128
        BN_EPS = 1e-05

        def gelu_new(x):
            c = jnp.sqrt(jnp.asarray(2.0 / jnp.pi, x.dtype))
            return 0.5 * x * (1.0 + jnp.tanh(c * (x + 0.044715 * x * x * x)))
        b, n, d = x.shape
        q = jnp.einsum('bnd,de->bne', x, w_q)
        mean = jnp.mean(q, axis=(0, 1))
        var = jnp.var(q, axis=(0, 1))
        q = (q - mean) * jax.lax.rsqrt(var + BN_EPS) * bn_gamma + bn_beta
        q = q.reshape(b, n, 2, H, KD).transpose(2, 0, 1, 3, 4)
        sim = jnp.einsum('pbnhd,hkpd->pbnhk', q, keys)
        sx, ix = jax.lax.top_k(sim[0], TOPK)
        sy, iy = jax.lax.top_k(sim[1], TOPK)
        all_scores = (sx[..., :, None] + sy[..., None, :]).reshape(b, n, H, TOPK * TOPK)
        all_indices = (ix[..., :, None] * NUM_KEYS + iy[..., None, :]).reshape(b, n, H, TOPK * TOPK)
        scores, pk = jax.lax.top_k(all_scores, TOPK)
        indices = jnp.take_along_axis(all_indices, pk, axis=-1)
        wd = down_embed[indices]
        wu = up_embed[indices]
        h = jnp.einsum('bnd,bnhkd->bnhk', x, wd)
        h = gelu_new(h)
        h = jax.nn.softmax(scores, axis=-1) * h
        out = jnp.einsum('bnhk,bnhkd->bnd', h, wu)
        return out

    def _L1_cond_ref(x, genre_embed, rms_w, wg_W, wg_b, gg_W, gg_b, W1, b1, W2, b2, W3, b3):
        import jax, jax.numpy as jnp
        import numpy as np
        TOP_K = 2
        EPS = 1e-06
        E = W1.shape[0]
        var = jnp.mean(x * x, axis=-1, keepdims=True)
        xn = rms_w * (x * jax.lax.rsqrt(var + EPS))
        gate = xn @ wg_W + wg_b + (genre_embed @ gg_W + gg_b)
        gate_w = jax.nn.softmax(gate, axis=-1)
        topk_w, topk_i = jax.lax.top_k(gate_w, TOP_K)
        cw = jnp.sum(jax.nn.one_hot(topk_i, E, dtype=x.dtype) * topk_w[..., None], axis=-2)
        h1 = jax.nn.relu(jnp.einsum('bsh,ehm->bsem', x, W1) + b1)
        h2 = jax.nn.relu(jnp.einsum('bsem,emn->bsen', h1, W2) + b2)
        out_e = jnp.einsum('bsen,enh->bseh', h2, W3) + b3
        return jnp.einsum('bseh,bse->bsh', out_e, cw)

    def _L1_ffn_ref(x, Wg, W1, b1, W2, b2):
        import jax, jax.numpy as jnp
        import numpy as np
        TOP_K = 2
        b, l, d = x.shape
        E = Wg.shape[1]
        xt = x.reshape(b * l, d)
        N = xt.shape[0]
        S = jax.nn.sigmoid(xt @ Wg)
        G, I = jax.lax.top_k(S, TOP_K)
        h = jax.nn.gelu(jnp.einsum('nd,edf->enf', xt, W1) + b1[:, None, :])
        y = jnp.einsum('enf,efd->end', h, W2) + b2[:, None, :]
        combine = jnp.zeros((N, E), dtype=x.dtype).at[jnp.arange(N)[:, None], I].add(G)
        out = jnp.einsum('ne,end->nd', combine, y)
        return out.reshape(b, l, d)
    x = x + _L0_ffn_ref(_L0_cond_ref(x, cond_256, L0_cond_Wqkv, L0_cond_bqkv, L0_cond_Wout, L0_cond_bout, L0_cond_Wc1, L0_cond_bc1, L0_cond_Wc2, L0_cond_bc2, L0_cond_We1, L0_cond_be1, L0_cond_We2, L0_cond_be2, L0_cond_ln_g, L0_cond_ln_b), L0_ffn_w_q, L0_ffn_bn_gamma, L0_ffn_bn_beta, L0_ffn_keys, L0_ffn_down_embed, L0_ffn_up_embed)
    x = x + _L1_ffn_ref(_L1_cond_ref(x, cond_256[:, None, :], L1_cond_rms_w, L1_cond_wg_W, L1_cond_wg_b, L1_cond_gg_W, L1_cond_gg_b, L1_cond_W1, L1_cond_b1, L1_cond_W2, L1_cond_b2, L1_cond_W3, L1_cond_b3), L1_ffn_Wg, L1_ffn_W1, L1_ffn_b1, L1_ffn_W2, L1_ffn_b2)
    return x

_drawn_inputs = setup_inputs


def setup_inputs(seed=0):
    import zlib

    import numpy as np

    out = dict(_drawn_inputs(seed))
    spreads = {'L0_cond_bqkv': (0.0, 0.8),
     'L0_cond_bout': (0.0, 0.8),
     'L0_cond_bc1': (0.0, 2.0),
     'L0_cond_bc2': (0.0, 2.0),
     'L0_cond_be1': (0.0, 0.8),
     'L0_cond_be2': (0.0, 0.8),
     'L0_cond_ln_g': (1.0, 0.6),
     'L0_cond_ln_b': (0.0, 0.8),
     'L0_ffn_bn_gamma': (1.0, 0.6),
     'L0_ffn_bn_beta': (0.0, 0.8),
     'L1_cond_rms_w': (1.0, 0.2),
     'L1_cond_wg_b': (0.0, 0.1),
     'L1_cond_gg_b': (0.0, 0.27),
     'L1_cond_b1': (0.0, 0.1),
     'L1_cond_b2': (0.0, 0.1),
     'L1_cond_b3': (0.0, 0.1),
     'L1_ffn_b1': (0.0, 0.1),
     'L1_ffn_b2': (0.0, 0.1)}
    factors = {'L0_cond_Wqkv': 8.0,
     'L0_cond_Wout': 8.0,
     'L0_cond_Wc1': 64.0,
     'L0_cond_Wc2': 64.0,
     'L0_cond_We1': 8.0,
     'L0_cond_We2': 8.0,
     'L0_ffn_w_q': 8.0,
     'L0_ffn_keys': 8.0,
     'L0_ffn_down_embed': 8.0,
     'L0_ffn_up_embed': 8.0}
    for name, (base, spread) in spreads.items():
        noise = np.random.default_rng([zlib.crc32(name.encode()), seed]).standard_normal(out[name].shape)
        drawn = base * np.exp(spread * noise) if base else spread * noise
        out[name] = jnp.asarray(drawn.astype(out[name].dtype))
    for name, factor in factors.items():
        out[name] = (out[name] * factor).astype(out[name].dtype)
    return out
```

```python
from contextlib import ExitStack

import numpy as np

import concourse.bass as bass
from concourse import mybir

F32 = mybir.dt.float32
U32 = mybir.dt.uint32
ALU = mybir.AluOpType
ACT = mybir.ActivationFunctionType
AX_X = mybir.AxisListType.X

P = 128
B = 16
NH, HD = 16, 8
CD = 32
FG = 4
FIELD = 0.3 * 0.7
PH = 8
NK = 32
NE = 8
M1 = 256
FF = 512
NG = B // 2
TOK = B * P
RING = 8

COLS_A = dict(wqT=128, wkT=128, wvT=128, bq=1, bk=1, head_of=16, woT=128, wo=128, wc1T=128, wc2T=16,
              we2T=128, peT=128, ident=128, bout=1, bc1=1, be1=1, gamma=16, beta=16, keysT=512)
COLS_L = dict(b1=16, b2=16, bf=32, wgr=8, rms=1, wgf=8)
COLS_C = dict(wc1c=128, csT=16, we1T=128, ggW=8)
COLS_R = dict(bv=128, bc2=16, be2=128, ln_g=128, ln_b=128, wgb=8, ggb=8)
COLS_8 = dict(b3=128, b2f=128)


def columns(widths):
    at, n = {}, 0
    for name, w in widths.items():
        at[name] = (n, n + w)
        n += w
    return at, n


PE_SETUP = ["hid_bias", "field1", "field2", "fpT", "field_scores", "faT", "gate_bias",
            "U0", "U1", "U2", "U3"]
DVE_SETUP = ["consts", "gate_rhs", "hid_bias", "f2", "stats", "aggr", "vareps", "f3", "f4g", "f4b", "fpT",
             "field_max", "fa_recip", "fa", "faT", "gate_rows", "gate_bias", "wgr"]
ACT_SETUP = ["field1", "field_exp", "U0", "U1", "U2", "U3"]
NORM_PE = ["mean_row", "cov", "CU0", "CU1", "CU2", "CU3", "var", "weff", "sim_bias"]
NORM_DVE = ["mean_col", "mean_bc", "x1mean", "x1neg", "centred", "cov", "T0", "T1", "T2", "T3",
            "vareps", "scale", "ka", "kb", "weff", "sim_bias"]


def program(nc, xtok, xT, pA, pL, pC, pR, p8, wq, wqT, down, up, w1, w2, w3, f1, f2, out):
    A_AT, A_N = columns(COLS_A)
    L_AT, L_N = columns(COLS_L)
    C_AT, C_N = columns(COLS_C)
    R_AT, R_N = columns(COLS_R)
    E_AT, E_N = columns(COLS_8)
    ds = bass.ds

    with ExitStack() as ctx:
        def sb(name, shape, dt=F32):
            return ctx.enter_context(nc.sbuf_tensor(name, shape, dt))

        def sem(name):
            return ctx.enter_context(nc.semaphore(name))

        x_all = sb("x_all", [P, B, P])
        x1T_all = sb("x1T_all", [P, TOK])
        downT = sb("downT", [P, NK * NK])
        up_sb = sb("up_sb", [P, PH, P])
        w1_sb = sb("w1_sb", [P, NE, M1])
        w2_sb = sb("w2_sb", [P, NE, 2, M1])
        w3_sb = sb("w3_sb", [P, NE, 2, P])
        f1_sb = sb("f1_sb", [P, NE, FF])
        f2_sb = sb("f2_sb", [P, NE, 4, P])
        lpack = sb("lpack", [P, L_N])
        epack = sb("epack", [NE, E_N])
        ident = sb("ident", [P, P])
        weff = sb("weff", [P, 512])
        sim_bias = sb("sim_bias", [P, 512])
        gate_bias = sb("gate_bias", [P, B, NE])
        iota8 = sb("iota8", [P, NE])
        mhalf = sb("mhalf", [P, B])

        def L(name, a=0, b=None):
            lo, hi = L_AT[name]
            return lpack[:, lo + a:hi if b is None else lo + b]

        region = sb("region", [P, 2 * RING, 1024])
        flat = region[:, :, :].rearrange("p a n -> p (a n)")
        used = [0]

        def part(n):
            used[0] += n
            assert used[0] <= 2 * RING * 1024
            return flat[:, used[0] - n:used[0]]

        wq_sb = part(2048)
        wqT_sb = part(2048)
        U = part(2048)
        o_all = part(TOK)
        qT, kT = part(P), part(P)
        k_heads = part(2048)
        apack = part(A_N)
        v_aug = part(NH * 9)
        xTs, thT, o_s, oT = part(P), part(P), part(P), part(P)
        cpack = part(C_N)
        rows = part(R_N)
        gate_rhs, gate_rows, ones = part(P), part(NE), part(P)
        hidb, fas = part(B), part(B)
        mx4 = part(16)
        tl, ec, cden, zden, rz_att = part(NH), part(NH), part(NH), part(NH), part(NH)
        o_n = part(P)
        v_stage = part(P)
        field_a, field_b, fpT, fa = part(P), part(P), part(B), part(P)
        small = part(32)
        o_sum, x1_sum = part(B), part(B)
        mean_bc, x1neg = part(P), part(P)
        cov = part(P)
        rstd, scale_a = part(B), part(B)
        ka, kb = k_heads[:, 0:512], k_heads[:, 512:1024]

        def A(name, a=0, b=None):
            lo, hi = A_AT[name]
            return apack[:, lo + a:hi if b is None else lo + b]

        def C(name):
            lo, hi = C_AT[name]
            return cpack[0:CD, lo:hi]

        def R(name, rows_=P):
            lo, hi = R_AT[name]
            return rows[0:rows_, lo:hi]

        S = [region[:, n, :] for n in range(RING)]
        E = [region[:, RING + n, :] for n in range(RING)]

        x1s = [sb(f"x1s{a}", [P, P]) for a in range(2)]
        sim = [sb(f"sim{a}", [P, 16, NK]) for a in range(2)]
        top_keys = sb("top_keys", [P, 16, 8])
        pairs = sb("pairs", [P, PH, 8, 8])
        top = [sb(f"top{a}", [P, PH, 8]) for a in range(2)]
        neg_max = [sb(f"neg_max{a}", [P, PH]) for a in range(2)]
        dtop = sb("dtop", [P, PH, 8])
        etop = sb("etop", [P, PH, 8])
        zsum = sb("zsum", [P, PH])
        rz = [sb(f"rz{a}", [P, PH]) for a in range(2)]
        W_both = sb("W_both", [P, 2048])
        G_both = sb("G_both", [P, 2048])
        W = [W_both[:, 1024 * a:1024 * a + 1024] for a in range(2)]
        G = [G_both[:, 1024 * a:1024 * a + 1024] for a in range(2)]
        D = [W_both[:, 512 * r:512 * r + 512] for r in range(FG)]
        ET = [G_both[:, 512 * r:512 * r + 512] for r in range(FG)]
        o_c, T = W_both[:, :], G_both[:, :]
        PT = sb("PT", [P, 1024])
        x2s = [sb(f"x2s{a}", [P, P]) for a in range(2)]
        x2T = sb("x2T", [P, 2 * P])
        square = sb("square", [P, P])
        ssq = sb("ssq", [P, 2])
        msq = sb("msq", [P, 2])
        rms = sb("rms", [P, 2])
        HF = [sb(f"HF_{n}", [P, 4, 256]) for n in range(2)]
        H1 = [HF[0][:, 2 * n:2 * n + 2, :] for n in range(2)]
        H2 = [sb(f"H2_{n}", [P, 2, 256]) for n in range(2)]
        acc = sb("acc", [P, 2, P])
        cT = sb("cT", [P, 2 * P])
        acc_f = sb("acc_f", [P, 2, P])
        lg = sb("lg", [P, 2, NE])
        lmax = sb("lmax", [P, 2])
        lexp = sb("lexp", [P, 2, NE])
        lsum = sb("lsum", [P, 2])
        prob = sb("prob", [P, 2, NE])
        best = sb("best", [P, 2, 8])
        besti = sb("besti", [P, 2, 8], U32)
        bestf = sb("bestf", [P, 2, 8])
        pick = sb("pick", [P, 2, NE])
        cw = sb("cw", [P, 2, NE])
        cwT = sb("cwT", [NE, 2 * P])

        banks = ctx.enter_context(nc.psum_tensor("banks", [P, 8, 512], F32))

        def bank(n, a=0, b=512):
            return banks[:, n, a:b]

        ld_a, ld_c, ld_r, ld_x, ld_wq, ld_wqT = (sem(n) for n in ("ld_a", "ld_c", "ld_r", "ld_x", "ld_wq", "ld_wqT"))
        ld_w, ld_l, ld_xtok = sem("ld_w"), sem("ld_l"), sem("ld_xtok")
        pe_setup, dve_setup, act_setup, pool_setup = sem("pe_setup"), sem("dve_setup"), sem("act_setup"), sem("pool_setup")
        s_proj, s_v, s_hid, s_coh = sem("s_proj"), sem("s_v"), sem("s_hid"), sem("s_coh")
        s_tanh, s_tl, s_ec, s_cden = sem("s_tanh"), sem("s_tl"), sem("s_ec"), sem("s_cden")
        s_qk, s_q, s_kh = sem("s_qk"), sem("s_q"), sem("s_kh")
        s_vst, s_x = sem("s_vst"), sem("s_x")
        s_S, s_mx, s_D, s_E, s_T, s_ET, s_pv = (sem("att_" + n) for n in ("S", "mx", "D", "E", "T", "ET", "pv"))
        s_vs = sem("s_vs")
        s_zd, s_rz, s_on, s_os, s_ostore = sem("s_zd"), sem("s_rzatt"), sem("s_on"), sem("s_os"), sem("s_ostore")
        s_oTp, s_oT, s_x1p, s_x1 = sem("s_oTp"), sem("s_oT"), sem("s_x1p"), sem("s_x1")
        pe_norm, dve_norm, pool_norm = sem("pe_norm"), sem("dve_norm"), sem("pool_norm")

        t_x1s, t_simp, t_sim, t_cand = sem("t_x1s"), sem("t_simp"), sem("t_sim"), sem("t_cand")
        topk = sem("topk")
        t_top, t_ez, t_zs, t_rz, t_Hp, t_G = (sem("t_" + n) for n in ("top", "ez", "zs", "rz", "Hp", "G"))
        h_S, h_E, h_me, h_w = sem("h_S"), sem("h_E"), sem("h_me"), sem("h_w")
        t_P, t_Tp, t_PT, t_x2p, t_x2, t_xst, t_ssq, t_trp, t_x2T = (
            sem("t_" + n) for n in ("P", "Tp", "PT", "x2p", "x2", "xst", "ssq", "trp", "x2T"))
        e_h1, e_r1, e_h2, e_r2, e_hf, e_g = (sem("e_" + n) for n in ("h1", "r1", "h2", "r2", "hf", "g"))
        e_y, e_acc = sem("e_y"), sem("e_acc")
        g_msq, g_rms, g_g1p, g_lg, g_exp1, g_g2p, g_exp2 = (
            sem("g_" + n) for n in ("msq", "rms", "g1p", "lg", "exp1", "g2p", "exp2"))
        gate = sem("gate")
        g_cw, g_cwTp, g_cwT, g_bias, g_binit, g_cTp, g_cT = (
            sem("g_" + n) for n in ("cw", "cwTp", "cwT", "bias", "binit", "cTp", "cT"))
        g_out = sem("g_out")

        def wait(eng, s, value):
            if not isinstance(value, int) or value > 0:
                eng.wait_ge(s, value)

        def col(ap, i):
            return ap[:, ds(i, 1)] if not isinstance(i, int) else ap[:, i:i + 1]

        def cols(ap, i, n=P):
            return ap[:, ds(i * n, n)] if not isinstance(i, int) else ap[:, i * n:(i + 1) * n]

        def tile_of(ap, t):
            if isinstance(t, int):
                return ap[:, t, :]
            return ap[:, ds(t, 1), :].rearrange("p a n -> p (a n)")

        block = ctx.enter_context(nc.Block())

        @block.sync
        def _(sp):
            sp.dma_start(apack, pA).then_inc(ld_a, 16)
            sp.dma_start(cpack[0:CD, :], pC).then_inc(ld_c, 16)
            sp.dma_start(rows, pR.broadcast_to([P, R_N])).then_inc(ld_r, 16)
            sp.dma_start(x1T_all[:, :], xT).then_inc(ld_x, 16)
            sp.dma_start(lpack[:, :], pL).then_inc(ld_l, 16)
            sp.dma_start(ident[:, :], pA[:, A_AT["ident"][0]:A_AT["ident"][1]]).then_inc(ld_l, 16)
            sp.dma_start(epack[:, :], p8).then_inc(ld_l, 16)
            sp.dma_start(wq_sb, wq).then_inc(ld_wq, 16)
            sp.dma_start(wqT_sb, wqT).then_inc(ld_wqT, 16)
            for dst, src in ((downT[:, :], down), (x_all[:, :, :], xtok.rearrange("b s e -> s b e")),
                             (up_sb[:, :, :], up.rearrange("(c p) d -> p c d", p=P)),
                             (w1_sb[:, :, :], w1.rearrange("e h m -> h e m")),
                             (w2_sb[:, :, :, :].rearrange("p e c n -> p (e c) n"),
                              w2.rearrange("e (c p) n -> p (e c) n", p=P)),
                             (w3_sb[:, :, :, :].rearrange("p e c n -> p (e c) n"),
                              w3.rearrange("e (c p) n -> p (e c) n", p=P)),
                             (f1_sb[:, :, :], f1.rearrange("e d f -> d e f")),
                             (f2_sb[:, :, :, :].rearrange("p e c n -> p (e c) n"),
                              f2.rearrange("e (c p) n -> p (e c) n", p=P))):
                sp.dma_start(dst, src).then_inc(ld_w, 16)

            def turn(g, peer, new, old):
                if old:
                    G2 = g - 2
                    sp.wait_ge(e_acc, 16 * (G2 + 1))
                    for a in range(2):
                        sp.dma_start(out[2 * G2 + a, :, :] if isinstance(g, int) else
                                     out[ds(2 * G2 + a, 1), :, :].rearrange("a s e -> s (a e)"),
                                     acc_f[:, a, :]).then_inc(g_out, 16)

            with sp.Fori(2, NG + 2) as g:
                turn(g, True, True, True)
            sp.wait_ge(g_out, 32 * NG)

        @block.gpsimd
        def _(pool):
            pool.memset(mhalf[:, :], -0.5).then_inc(pool_setup, 1)
            pool.memset(ones, 1.0).then_inc(pool_setup, 1)
            pool.memset(v_aug, 1.0).then_inc(pool_setup, 1)
            pool.iota(iota8[:, :], [[1, NE]], base=0, channel_multiplier=0,
                      allow_small_or_imprecise_dtypes=True).then_inc(pool_setup, 1)
            pool.wait_ge(pool_setup, 4)
            pool.wait_ge(dve_setup, DVE_SETUP.index("vareps") + 1)
            pool.tensor_tensor(small[0:B, 9:10], small[0:B, 8:9], mhalf[0:B, 0:1], ALU.pow).then_inc(pool_setup, 1)
            heads = lambda ap: ap.rearrange("p (h d) -> p h d", h=NH)

            def values(b):
                pool.wait_ge(s_vst, b + 1)
                wait(pool, s_pv, FG * b)
                wait(pool, s_vs, b)
                pool.tensor_tensor(heads(v_aug)[:, :, 0:HD], heads(v_stage), heads(R("bv")), ALU.add).then_inc(s_v, 1)

            def keep_output(b):
                pool.wait_ge(s_os, b + 1)
                pool.tensor_copy(cols(o_all, b), o_s).then_inc(s_ostore, 1)

            def stage_x(b):
                wait(pool, s_proj, b)
                pool.tensor_copy(xTs, cols(x1T_all, b)).then_inc(s_x, 1)

            def head_keys(b):
                pool.wait_ge(s_q, b + 1)
                for r in range(FG):
                    wait(pool, s_S, FG * (b - 1) + r + 1)
                    pool.tensor_tensor(k_heads[:, 512 * r:512 * r + 512].rearrange("p (g n) -> p g n", g=FG),
                                       kT.unsqueeze(1).broadcast_to([P, FG, P]),
                                       A("head_of", FG * r, FG * r + FG).unsqueeze(2).broadcast_to([P, FG, P]),
                                       ALU.mult).then_inc(s_kh, 1)

            pool.wait_ge(ld_x, 16)
            stage_x(0)
            pool.wait_ge(ld_r, 16)
            pool.wait_ge(ld_a, 16)
            head_keys(0)
            values(0)
            stage_x(1)
            head_keys(1)
            stage_x(2)

            def attend(b, more):
                values(b + 1)
                head_keys(b + 2)
                keep_output(b)
                if more:
                    stage_x(b + 3)

            attend(0, True)
            with pool.Fori(1, B - 3) as b:
                attend(b, True)
            attend(B - 3, False)
            values(B - 1)
            keep_output(B - 2)
            keep_output(B - 1)
            pool.wait_ge(dve_norm, NORM_DVE.index("vareps") + 1)
            pool.tensor_tensor(rstd, small[:, 0:B], mhalf[:, :], ALU.pow).then_inc(pool_norm, 1)

            def stage_x1(t, a):
                wait(pool, t_Hp, t - 1)
                pool.tensor_copy(x1s[a][:, :], cols(x1T_all, t)).then_inc(t_x1s, 1)

            def pair_scores(t, a, h):
                hs, slot = 8 * t + h, 8 * a + h
                if h == 0:
                    pool.wait_ge(t_sim, t + 1)
                wait(pool, h_me, hs - RING + 1)
                pool.tensor_tensor(
                    S[slot % RING].rearrange("p (i j) -> p i j", i=NK),
                    sim[a][:, h, :].unsqueeze(2).broadcast_to([P, NK, NK]),
                    sim[a][:, PH + h, :].unsqueeze(1).broadcast_to([P, NK, NK]),
                    ALU.add).then_inc(h_S, 1)

            def weigh(t, a):
                pool.wait_ge(h_w, 8 * t + 8)
                pool.wait_ge(t_G, t + 1)
                pool.tensor_tensor(W[a], W[a], G[a], ALU.mult).then_inc(t_P, 1)

            def keep_x2(t, a):
                pool.wait_ge(t_x2, t + 1)
                pool.tensor_copy(tile_of(x_all, t), x2s[a][:, :]).then_inc(t_xst, 1)

            pool.wait_ge(s_x1, B)
            pool.wait_ge(dve_norm, len(NORM_DVE))
            stage_x1(0, 0)
            stage_x1(1, 1)

            def turn(g, peer, new, old):
                t = 2 * g
                if peer:
                    if isinstance(g, int) and g == 0:
                        for h in range(4):
                            pair_scores(t, 0, h)
                if new:
                    weigh(t - 1, 1)
                    keep_x2(t - 1, 1)
                if new:
                    pool.wait_ge(g_msq, g)
                    pool.tensor_tensor(rms[:, :], msq[:, :], mhalf[:, 0:2], ALU.pow).then_inc(g_rms, 1)
                if not peer:
                    return
                for h in range(4, 8):
                    pair_scores(t, 0, h)
                for h in range(3):
                    pair_scores(t + 1, 1, h)
                weigh(t, 0)
                for h in range(3, 8):
                    pair_scores(t + 1, 1, h)
                keep_x2(t, 0)
                if isinstance(g, int) or True:
                    more(g)

            def more(g):
                t = 2 * g
                if isinstance(g, int):
                    if g + 1 < NG:
                        stage_x1(t + 2, 0)
                        for h in range(4):
                            pair_scores(t + 2, 0, h)
                        stage_x1(t + 3, 1)
                    return
                stage_x1(t + 2, 0)
                for h in range(4):
                    pair_scores(t + 2, 0, h)
                stage_x1(t + 3, 1)

            turn(0, True, False, False)
            turn(1, True, True, False)
            with pool.Fori(2, NG - 1) as g:
                turn(g, True, True, True)
            turn(NG - 1, True, True, True)
            turn(NG, False, True, True)

        @block.tensor
        def _(pe):
            def mm(o, l, r, start=True, stop=True):
                return pe.matmul(o, l, r, start=start, stop=stop)

            pe.wait_ge(ld_a, 16)
            pe.wait_ge(ld_c, 16)
            pe.wait_ge(pool_setup, 4)
            mm(bank(7, 0, B), C("wc1c"), C("csT")).then_inc(pe_setup, 1)
            mm(bank(6, 0, B), C("we1T"), C("csT")).then_inc(pe_setup, 1)
            pe.wait_ge(act_setup, 1)
            mm(banks[0:B, 1, 0:P], thT[:, 0:B], A("we2T")).then_inc(pe_setup, 1)
            pe.wait_ge(dve_setup, DVE_SETUP.index("f4b") + 1)
            pe.transpose(bank(0, 0, B), field_b[0:B, :], A("ident")[0:B, 0:B]).then_inc(pe_setup, 1)
            pe.wait_ge(dve_setup, DVE_SETUP.index("fpT") + 1)
            mm(banks[0:B, 6, 0:P], fpT, A("peT")).then_inc(pe_setup, 1)
            pe.wait_ge(dve_setup, DVE_SETUP.index("fa") + 1)
            pe.transpose(bank(1, 0, B), fa[0:B, :], A("ident")[0:B, 0:B]).then_inc(pe_setup, 1)
            mm(bank(7, 128, 256), ones[0:CD, :], gate_rhs[0:CD, :]).then_inc(pe_setup, 1)
            pe.wait_ge(ld_wq, 16)
            for c in range(4):
                mm(bank(2 + c), A("wo"), wq_sb[:, 512 * c:512 * c + 512]).then_inc(pe_setup, 1)

            def project(b):
                pe.wait_ge(s_x, b + 1)
                wait(pe, s_q, b)
                mm(bank(0, 0, P), A("wqT"), xTs)
                mm(bank(0, P, 2 * P), A("wkT"), xTs).then_inc(s_qk, 1)
                wait(pe, s_tanh, b)
                mm(bank(7, 0, P), xTs, A("wvT"))
                mm(bank(7, P, 2 * P), A("wc1T"), xTs).then_inc(s_proj, 1)

            def coherence(b):
                pe.wait_ge(s_tanh, b + 1)
                wait(pe, s_tl, b)
                mm(bank(1, 0, NH), thT, A("wc2T")).then_inc(s_coh, 1)

            def scores(b, r):
                pe.wait_ge(s_q, b + 1)
                pe.wait_ge(s_kh, FG * b + r + 1)
                wait(pe, s_ET, FG * (b - 1) + r + 1)
                mm(bank(2 + r), qT, k_heads[:, 512 * r:512 * r + 512]).then_inc(s_S, 1)

            def transposes(b, r):
                pe.wait_ge(s_E, FG * b + r + 1)
                for g in range(FG):
                    m = pe.transpose(banks[:, 2 + r, P * g:P * g + P], D[r][:, P * g:P * g + P], A("ident"))
                m.then_inc(s_T, 1)

            def values(b, r):
                pe.wait_ge(s_ET, FG * b + r + 1)
                for g in range(FG):
                    h = FG * r + g
                    m = mm(bank(6, 9 * h, 9 * h + 9), ET[r][:, P * g:P * g + P], v_aug[:, 9 * h:9 * h + 9])
                m.then_inc(s_pv, 1)

            def out_T(b):
                pe.wait_ge(s_os, b + 1)
                pe.transpose(bank(6, 144, 272), o_s, A("ident")).then_inc(s_oTp, 1)

            def out_proj(b):
                pe.wait_ge(s_oT, b + 1)
                mm(bank(6, 144, 272), A("woT"), oT).then_inc(s_x1p, 1)

            def attend(b, more, project_more, first=False):
                transposes(b, 0)
                transposes(b, 1)
                if not first:
                    out_T(b - 1)
                transposes(b, 2)
                transposes(b, 3)
                if not first:
                    out_proj(b - 1)
                if more:
                    scores(b + 1, 0)
                pe.wait_ge(s_v, b + 1)
                wait(pe, s_x1, b)
                mm(bank(6, 384, 512), ones, v_aug.rearrange("p (h d) -> p h d", d=9)[:, :, 0:HD]).then_inc(s_vs, 1)
                for r in range(FG):
                    values(b, r)
                    if more and r < FG - 1:
                        scores(b + 1, r + 1)
                if more:
                    coherence(b + 1)
                if project_more:
                    project(b + 2)

            pe.wait_ge(act_setup, len(ACT_SETUP))
            pe.wait_ge(dve_setup, len(DVE_SETUP))
            project(0)
            for r in range(FG):
                scores(0, r)
            coherence(0)
            project(1)
            attend(0, True, True, first=True)
            with pe.Fori(1, B - 2) as b:
                attend(b, True, True)
            attend(B - 2, True, False)
            attend(B - 1, False, False)
            out_T(B - 1)
            out_proj(B - 1)

            pe.wait_ge(dve_norm, NORM_DVE.index("mean_bc") + 1)
            mm(bank(0, 0, P), mean_bc, A("ident")).then_inc(pe_norm, 1)
            pe.wait_ge(dve_norm, NORM_DVE.index("centred") + 1)
            for t in range(B):
                m = mm(bank(6, 0, P), o_c[:, P * t:P * t + P], o_c[:, P * t:P * t + P],
                       start=(t == 0), stop=(t == B - 1))
            m.then_inc(pe_norm, 1)
            pe.wait_ge(dve_norm, NORM_DVE.index("cov") + 1)
            for c in range(4):
                mm(bank(2 + c), cov, U[:, 512 * c:512 * c + 512]).then_inc(pe_norm, 1)
            pe.wait_ge(dve_norm, NORM_DVE.index("T3") + 1)
            for c in range(16):
                m = mm(bank(7, c, c + 1), T[:, P * c:P * c + P], ones[:, 0:1])
            m.then_inc(pe_norm, 1)
            pe.wait_ge(dve_norm, NORM_DVE.index("ka") + 1)
            pe.wait_ge(ld_wqT, 16)
            for c in range(16):
                m = mm(bank(1, NK * c, NK * c + NK), wqT_sb[:, P * c:P * c + P], ka[:, NK * c:NK * c + NK])
            m.then_inc(pe_norm, 1)
            pe.wait_ge(dve_norm, NORM_DVE.index("weff") + 1)
            mm(bank(5), ones, kb, start=True, stop=False)
            mm(bank(5), x1neg, weff[:, :], start=False, stop=True).then_inc(pe_norm, 1)

            pe.wait_ge(ld_w, 16 * 8)
            pe.wait_ge(ld_l, 48)
            pe.wait_ge(dve_norm, len(NORM_DVE))

            def key_scores(t, a):
                pe.wait_ge(t_x1s, t + 1)
                wait(pe, t_sim, t)
                wait(pe, t_x2T, t - 1)
                mm(bank(6), x1s[a][:, :], weff[:, :]).then_inc(t_simp, 1)

            def expert_inputs(t, a):
                wait(pe, t_G, t)
                wait(pe, t_PT, t - 1)
                for c in range(2):
                    m = mm(bank(c), x1s[a][:, :], downT[:, 512 * c:512 * c + 512])
                m.then_inc(t_Hp, 1)

            def weights_T(t, a):
                pe.wait_ge(t_P, t + 1)
                wait(pe, t_PT, t)
                for c in range(8):
                    m = pe.transpose(banks[:, c // 4, P * (c % 4):P * (c % 4) + P], W[a][:, P * c:P * c + P], ident[:, :])
                m.then_inc(t_Tp, 1)

            def peer_out(t):
                pe.wait_ge(t_PT, t + 1)
                wait(pe, t_sim, t + 2 if not isinstance(t, int) else min(t + 2, B))
                for c in range(8):
                    m = mm(bank(6, 0, P), PT[:, P * c:P * c + P], up_sb[:, c, :], start=(c == 0), stop=(c == 7))
                m.then_inc(t_x2p, 1)

            def x2_T(t, a):
                pe.wait_ge(t_x2, t + 1)
                pe.transpose(bank(6, P, 2 * P), x2s[a][:, :], ident[:, :]).then_inc(t_trp, 1)

            def gate1(Gn):
                pe.wait_ge(t_x2T, 2 * Gn + 2)
                wait(pe, g_binit, 2 * Gn)
                for a in range(2):
                    m = mm(bank(7, 8 * a, 8 * a + 8), x2T[:, P * a:P * a + P], L("wgr"))
                m.then_inc(g_g1p, 1)

            def gate2(Gn):
                pe.wait_ge(g_cT, Gn + 1)
                for a in range(2):
                    m = mm(bank(7, 8 * a, 8 * a + 8), cT[:, P * a:P * a + P], L("wgf"))
                m.then_inc(g_g2p, 1)

            def weighted_bias(n, name):
                lo, hi = E_AT[name]
                pe.wait_ge(g_cw, n + 1)
                for a in range(2):
                    m = pe.transpose(banks[0:NE, 7, P * a:P * a + P], cw[:, a, :], ident[:, :])
                m.then_inc(g_cwTp, 1)
                pe.wait_ge(g_cwT, n + 1)
                for a in range(2):
                    m = mm(bank(7, 256 + P * a, 384 + P * a), cwT[:, P * a:P * a + P], epack[:, lo:hi])
                m.then_inc(g_bias, 1)

            def hidden1(Gn, e):
                if e == 0:
                    pe.wait_ge(t_x2T, 2 * Gn + 2)
                    wait(pe, e_g, 8 * Gn)
                wait(pe, e_r1, 8 * Gn + e)
                for m_ in range(2):
                    m = mm(bank(2, 256 * m_, 256 * m_ + 256), w1_sb[:, e, P * m_:P * m_ + P], x2T[:, :])
                m.then_inc(e_h1, 1)

            def hidden2(Gn, e):
                pe.wait_ge(e_r1, 8 * Gn + e + 1)
                wait(pe, e_r2, 8 * Gn + e)
                for n in range(2):
                    for m_ in range(2):
                        m = mm(bank(3, 256 * n, 256 * n + 256), w2_sb[:, e, m_, P * n:P * n + P], H1[e % 2][:, m_, :],
                               start=(m_ == 0), stop=(m_ == 1))
                m.then_inc(e_h2, 1)

            def outputs(Gn, n, w_, h_, e, parts):
                wait(pe, e_acc, 16 * Gn + n - 1)
                for a in range(2):
                    for c in range(parts):
                        m = mm(bank(4 + n % 2, P * a, P * a + P),
                               h_[:, c, P * a:P * a + P], w_[:, e, c, :], start=(c == 0), stop=(c == parts - 1))
                m.then_inc(e_y, 1)

            def hidden_f(Gn, e):
                if e == 0:
                    pe.wait_ge(e_r2, 8 * Gn + 8)
                wait(pe, e_g, 8 * Gn + e)
                for f in range(4):
                    m = mm(banks[:, 2 + f // 2, 256 * (f % 2):256 * (f % 2) + 256],
                           f1_sb[:, e, P * f:P * f + P], cT[:, :])
                m.then_inc(e_hf, 1)

            def step(Gn, l):
                if l < 8:
                    if l > 0:
                        pe.wait_ge(e_r2, 8 * Gn + l)
                        outputs(Gn, l - 1, w3_sb, H2[(l - 1) % 2], l - 1, 2)
                    hidden2(Gn, l)
                    if l < 7:
                        hidden1(Gn, l + 1)
                elif l == 8:
                    pe.wait_ge(e_r2, 8 * Gn + 8)
                    outputs(Gn, 7, w3_sb, H2[1], 7, 2)
                    pe.wait_ge(e_acc, 16 * Gn + 8)
                    for a in range(2):
                        m = pe.transpose(bank(7, 256 + P * a, 384 + P * a), acc[:, a, :], ident[:, :])
                    m.then_inc(g_cTp, 1)
                    gate2(Gn)
                    hidden_f(Gn, 0)
                else:
                    e = l - 9
                    if e < 7:
                        hidden_f(Gn, e + 1)
                    pe.wait_ge(e_g, 8 * Gn + e + 1)
                    outputs(Gn, 8 + e, f2_sb, HF[e % 2], e, 4)

            key_scores(0, 0)
            expert_inputs(0, 0)

            def turn(g, peer, new, old, more=True):
                t = 2 * g
                for s in range(16):
                    if s < 4 and old:
                        step(g - 2, s + 12)
                    if s >= 4 and new:
                        step(g - 1, s - 4)
                    if s == 4 and old:
                        step(g - 2, 16)
                    if new and s == 1:
                        weights_T(t - 1, 1)
                    if new and s == 2:
                        peer_out(t - 1)
                    if new and s == 3:
                        x2_T(t - 1, 1)
                        gate1(g - 1)
                        hidden1(g - 1, 0)
                    if new and s == 4:
                        weighted_bias(2 * (g - 1), "b3")
                    if new and s == 12:
                        pass
                    if new and s == 13:
                        weighted_bias(2 * (g - 1) + 1, "b2f")
                    if peer:
                        if s == 3:
                            key_scores(t + 1, 1)
                        if s == 9:
                            weights_T(t, 0)
                        if s == 10:
                            peer_out(t)
                        if s == 11:
                            x2_T(t, 0)
                        if s == 12:
                            expert_inputs(t + 1, 1)
                            if more:
                                key_scores(t + 2, 0)
                        if s == 14 and more:
                            expert_inputs(t + 2, 0)

            turn(0, True, False, False)
            turn(1, True, True, False)
            with pe.Fori(2, NG - 1) as g:
                turn(g, True, True, True)
            turn(NG - 1, True, True, True, more=False)
            turn(NG, False, True, True)
            turn(NG + 1, False, False, True)

        @block.scalar
        def _(act):
            act.wait_ge(pe_setup, 2)
            act.activation(thT[:, 0:B], bank(6, 0, B), ACT.Relu, bias=A("be1")).then_inc(act_setup, 1)
            act.wait_ge(dve_setup, DVE_SETUP.index("field_max") + 1)
            act.activation(field_a[0:B, :], banks[0:B, 6, 0:P], ACT.Exp, bias=small[0:B, 10:11],
                           accum_out=small[0:B, 11:12]).then_inc(act_setup, 1)
            for c in range(4):
                act.wait_ge(pe_setup, PE_SETUP.index("U0") + c + 1)
                act.activation(U[:, 512 * c:512 * c + 512], bank(2 + c), ACT.Copy).then_inc(act_setup, 1)

            def projected(b):
                act.wait_ge(s_qk, b + 1)
                wait(act, s_S, FG * b)
                act.activation(qT, bank(0, 0, P), ACT.Identity, bias=A("bq"))
                wait(act, s_kh, FG * b)
                act.activation(kT, bank(0, P, 2 * P), ACT.Identity, bias=A("bk")).then_inc(s_q, 1)
                act.wait_ge(s_proj, b + 1)
                wait(act, s_v, b)
                act.activation(v_stage, bank(7, 0, P), ACT.Copy).then_inc(s_vst, 1)
                wait(act, s_coh, b)
                act.activation(thT, bank(7, P, 2 * P), ACT.Tanh, bias=col(hidb, b)).then_inc(s_tanh, 1)

            def exps(b, r):
                act.wait_ge(s_D, FG * b + r + 1)
                act.activation(D[r], D[r], ACT.Exp, scale=float(HD) ** -0.5).then_inc(s_E, 1)

            def probs_T(b, r):
                act.wait_ge(s_T, FG * b + r + 1)
                wait(act, s_pv, FG * (b - 1) + r + 1)
                act.activation(ET[r], bank(2 + r), ACT.Copy).then_inc(s_ET, 1)

            def out_T(b):
                act.wait_ge(s_oTp, b + 1)
                wait(act, s_x1p, b)
                act.activation(oT, bank(6, 144, 272), ACT.Copy, accum_out=col(o_sum, b)).then_inc(s_oT, 1)

            def out_x1(b):
                act.wait_ge(s_x1p, b + 1)
                act.activation(cols(x1T_all, b), bank(6, 144, 272), ACT.Identity, bias=A("bout"),
                               accum_out=col(x1_sum, b)).then_inc(s_x1, 1)

            def attend(b, more, project_more, first=False):
                probs_T(b, 0)
                probs_T(b, 1)
                if not first:
                    out_T(b - 1)
                probs_T(b, 2)
                probs_T(b, 3)
                if not first:
                    out_x1(b - 1)
                act.wait_ge(s_tl, b + 1)
                wait(act, s_cden, b)
                act.activation(ec, tl, ACT.Exp, scale=-1.0).then_inc(s_ec, 1)
                if more:
                    for r in range(FG):
                        exps(b + 1, r)
                if project_more:
                    projected(b + 2)

            act.wait_ge(dve_setup, len(DVE_SETUP))
            projected(0)
            for r in range(FG):
                exps(0, r)
            projected(1)
            attend(0, True, True, first=True)
            with act.Fori(1, B - 2) as b:
                attend(b, True, True)
            attend(B - 2, True, False)
            attend(B - 1, False, False)
            out_T(B - 1)
            out_x1(B - 1)

            def exp_pairs(t, a, h):
                hs, slot = 8 * t + h, 8 * a + h
                act.wait_ge(h_S, hs + 1)
                if h == 0:
                    act.wait_ge(t_top, t + 1)
                wait(act, h_w, hs - RING + 1)
                act.activation(E[slot % RING], S[slot % RING], ACT.Exp, bias=neg_max[a][:, h:h + 1]).then_inc(h_E, 1)

            def exp_top(t):
                act.wait_ge(t_top, t + 1)
                wait(act, t_zs, t)
                act.activation(etop[:, :, :], dtop[:, :, :], ACT.Exp).then_inc(t_ez, 1)

            def expert_inputs(t, a):
                act.wait_ge(t_Hp, t + 1)
                wait(act, t_P, t - 1)
                act.activation(G[a], banks[:, 0:2, :].rearrange("p c n -> p (c n)"),
                               ACT.Gelu_apprx_tanh).then_inc(t_G, 1)

            def weights_T(t):
                act.wait_ge(t_Tp, t + 1)
                wait(act, t_x2p, t)
                act.activation(PT[:, :], banks[:, 0:2, :].rearrange("p c n -> p (c n)"), ACT.Copy).then_inc(t_PT, 1)

            def squares(t, a):
                act.wait_ge(t_x2, t + 1)
                wait(act, t_ssq, t)
                wait(act, g_msq, t // 2 if isinstance(t, int) else halves(t))
                act.activation(square[:, :], x2s[a][:, :], ACT.Square, accum_out=ssq[:, a:a + 1]).then_inc(t_ssq, 1)

            def x2_T(t, a, Gn):
                act.wait_ge(t_trp, t + 1)
                wait(act, e_h1, 8 * Gn)
                act.activation(x2T[:, P * a:P * a + P], bank(6, P, 2 * P), ACT.Copy).then_inc(t_x2T, 1)

            def step(Gn, l):
                if l < 8:
                    e = l
                    hidden1(Gn, e) if e == 0 else None
                    act.wait_ge(e_h2, 8 * Gn + e + 1)
                    wait(act, e_y, 16 * Gn + e - 1)
                    for n in range(2):
                        m = act.activation(H2[e % 2][:, n, :], bank(3, 256 * n, 256 * n + 256), ACT.Relu,
                                           bias=L("b2", 2 * e + n, 2 * e + n + 1))
                    m.then_inc(e_r2, 1)
                    if e < 7:
                        hidden1(Gn, e + 1)
                elif l == 8:
                    act.wait_ge(g_cTp, Gn + 1)
                    wait(act, e_hf, 8 * Gn)
                    act.activation(cT[:, :], bank(7, 256, 512), ACT.Copy).then_inc(g_cT, 1)
                    act.wait_ge(g_g2p, Gn + 1)
                    act.activation(lexp[:, :, :].rearrange("p a e -> p (a e)"), bank(7, 0, 16), ACT.Exp,
                                   scale=-1.0).then_inc(g_exp2, 1)
                    hidden_f(Gn, 0)
                elif l < 16:
                    if l < 16 and l - 8 < 8:
                        hidden_f(Gn, l - 8)

            def hidden1(Gn, e):
                act.wait_ge(e_h1, 8 * Gn + e + 1)
                wait(act, e_h2, 8 * Gn + e - 1)
                for n in range(2):
                    m = act.activation(H1[e % 2][:, n, :], bank(2, 256 * n, 256 * n + 256), ACT.Relu,
                                       bias=L("b1", 2 * e + n, 2 * e + n + 1))
                m.then_inc(e_r1, 1)

            def hidden_f(Gn, e):
                act.wait_ge(e_hf, 8 * Gn + e + 1)
                wait(act, e_y, 16 * Gn + 8 + e - 1)
                for f in range(4):
                    m = act.activation(HF[e % 2][:, f, :], banks[:, 2 + f // 2, 256 * (f % 2):256 * (f % 2) + 256],
                                       ACT.Gelu_apprx_tanh, bias=L("bf", 4 * e + f, 4 * e + f + 1))
                m.then_inc(e_g, 1)

            act.wait_ge(dve_norm, len(NORM_DVE))
            act.wait_ge(ld_l, 48)
            expert_inputs(0, 0)
            exp_top(0)
            for h in range(4):
                exp_pairs(0, 0, h)

            EXPS = {3: [4, 5], 4: [6], 5: [7], 6: [8], 7: [9], 8: [10], 9: [11], 10: [12, 13], 11: [14, 15]}

            def turn(g, peer, new, old, more=True):
                t = 2 * g
                for s in range(16):
                    if s < 4 and old:
                        step(g - 2, s + 12)
                    if s == 1 and new:
                        weights_T(t - 1)
                    if s == 2 and new:
                        act.wait_ge(t_x2, t)
                        wait(act, t_ssq, t - 1)
                        act.activation(square[:, :], x2s[1][:, :], ACT.Square, accum_out=ssq[:, 1:2]).then_inc(t_ssq, 1)
                    if s == 3 and new:
                        x2_T(t - 1, 1, g - 1)
                        hidden1(g - 1, 0)
                    if s == 3 and new:
                        act.wait_ge(gate, 3)
                        act.activation(lexp[:, :, :], lg[:, :, :], ACT.Exp).then_inc(g_exp1, 1)
                    if peer:
                        if s == 5:
                            exp_top(t + 1)
                        for h in EXPS.get(s, []):
                            exp_pairs(t + h // 8, h // 8, h % 8)
                    if s >= 4 and new:
                        Gn, l = g - 1, s - 4
                        if l < 8:
                            act.wait_ge(e_h2, 8 * Gn + l + 1)
                            wait(act, e_y, 16 * Gn + l - 1)
                            for n in range(2):
                                m = act.activation(H2[l % 2][:, n, :], bank(3, 256 * n, 256 * n + 256), ACT.Relu,
                                                   bias=L("b2", 2 * l + n, 2 * l + n + 1))
                            m.then_inc(e_r2, 1)
                            if l < 7:
                                hidden1(Gn, l + 1)
                        else:
                            step(Gn, l)
                    if peer:
                        if s == 9:
                            weights_T(t)
                        if s == 11:
                            act.wait_ge(t_x2, t + 1)
                            wait(act, t_ssq, t)
                            wait(act, g_msq, g)
                            act.activation(square[:, :], x2s[0][:, :], ACT.Square, accum_out=ssq[:, 0:1]).then_inc(t_ssq, 1)
                            x2_T(t, 0, g)
                        if s == 12:
                            expert_inputs(t + 1, 1)
                        if more and s == 14:
                            expert_inputs(t + 2, 0)
                        if more and s == 15:
                            exp_top(t + 2)
                            for h in range(4):
                                exp_pairs(t + 2, 0, h)

            turn(0, True, False, False)
            turn(1, True, True, False)
            with act.Fori(2, NG - 1) as g:
                turn(g, True, True, True)
            turn(NG - 1, True, True, True, more=False)
            turn(NG, False, True, True)
            turn(NG + 1, False, False, True)

        @block.vector
        def _(v):
            def setup_done(name):
                v.wait_ge(dve_setup, DVE_SETUP.index(name) + 1)

            v.memset(small, 0.0).then_inc(dve_setup, 1)
            v.wait_ge(ld_a, 16)
            v.wait_ge(ld_c, 16)
            v.wait_ge(ld_r, 16)
            cs = C("csT").unsqueeze(2).broadcast_to([CD, B, NE])
            gg = C("ggW").unsqueeze(1).broadcast_to([CD, B, NE])
            v.tensor_tensor(gate_rhs[0:CD, :].rearrange("p (b o) -> p b o", b=B), cs, gg, ALU.mult).then_inc(dve_setup, 1)
            v.wait_ge(pe_setup, 1)
            v.tensor_scalar(hidb, bank(7, 0, B), A("bc1"), None, ALU.add).then_inc(dve_setup, 1)
            v.wait_ge(pe_setup, 3)
            v.tensor_tensor(field_a[0:B, :], banks[0:B, 1, 0:P], R("be2", B), ALU.add).then_inc(dve_setup, 1)
            setup_done("f2")
            v.bn_stats(small[0:B, 0:6], field_a[0:B, :]).then_inc(dve_setup, 1)
            setup_done("stats")
            v.bn_aggr(small[0:B, 6:8], small[0:B, 0:6]).then_inc(dve_setup, 1)
            setup_done("aggr")
            v.tensor_scalar(small[0:B, 8:9], small[0:B, 7:8], 1e-5, None, ALU.add).then_inc(dve_setup, 1)
            v.wait_ge(pool_setup, 5)
            v.tensor_scalar(field_b[0:B, :], field_a[0:B, :], small[0:B, 6:7], small[0:B, 9:10],
                            ALU.subtract, ALU.mult).then_inc(dve_setup, 1)
            setup_done("f3")
            v.tensor_tensor(field_a[0:B, :], field_b[0:B, :], R("ln_g", B), ALU.mult).then_inc(dve_setup, 1)
            setup_done("f4g")
            v.tensor_tensor(field_b[0:B, :], field_a[0:B, :], R("ln_b", B), ALU.add).then_inc(dve_setup, 1)
            v.wait_ge(pe_setup, PE_SETUP.index("fpT") + 1)
            v.tensor_copy(fpT, bank(0, 0, B)).then_inc(dve_setup, 1)
            v.wait_ge(pe_setup, PE_SETUP.index("field_scores") + 1)
            v.tensor_reduce(small[0:B, 10:11], banks[0:B, 6, 0:P], AX_X, ALU.max, negate=True).then_inc(dve_setup, 1)
            v.wait_ge(act_setup, 2)
            v.reciprocal(small[0:B, 12:13], small[0:B, 11:12]).then_inc(dve_setup, 1)
            setup_done("fa_recip")
            v.tensor_scalar(fa[0:B, :], field_a[0:B, :], small[0:B, 12:13], FIELD, ALU.mult, ALU.mult).then_inc(dve_setup, 1)
            v.wait_ge(pe_setup, PE_SETUP.index("faT") + 1)
            v.tensor_copy(fas, bank(1, 0, B)).then_inc(dve_setup, 1)
            v.tensor_tensor(gate_rows, R("wgb"), R("ggb"), ALU.add).then_inc(dve_setup, 1)
            setup_done("gate_rows")
            v.wait_ge(pe_setup, PE_SETUP.index("gate_bias") + 1)
            v.tensor_tensor(gate_bias[:, :, :], bank(7, P, 2 * P).rearrange("p (b o) -> p b o", b=B),
                            gate_rows.unsqueeze(1).broadcast_to([P, B, NE]), ALU.add).then_inc(dve_setup, 1)
            v.wait_ge(ld_l, 48)
            v.tensor_scalar(L("wgr"), L("wgr"), L("rms"), None, ALU.mult).then_inc(dve_setup, 1)

            quarter = lambda ap: ap.rearrange("p (g n) -> p g n", g=FG)

            def row_max(b, r):
                v.wait_ge(s_S, FG * b + r + 1)
                v.tensor_reduce(mx4[:, FG * r:FG * r + FG], quarter(bank(2 + r)), AX_X, ALU.max).then_inc(s_mx, 1)

            def minus_max(b, r):
                v.wait_ge(s_mx, FG * b + r + 1)
                wait(v, s_T, FG * (b - 1) + r + 1)
                v.tensor_tensor(quarter(D[r]), quarter(bank(2 + r)),
                                mx4[:, FG * r:FG * r + FG].unsqueeze(2).broadcast_to([P, FG, P]),
                                ALU.subtract).then_inc(s_D, 1)

            def shifted_scores(b):
                row_max(b, 0)
                row_max(b, 1)
                minus_max(b, 0)
                row_max(b, 2)
                minus_max(b, 1)
                row_max(b, 3)
                minus_max(b, 2)
                minus_max(b, 3)

            def attend(b, more):
                v.wait_ge(s_coh, b + 1)
                wait(v, s_ec, b)
                v.tensor_tensor(tl, bank(1, 0, NH), R("bc2"), ALU.add).then_inc(s_tl, 1)
                if more:
                    shifted_scores(b + 1)
                v.wait_ge(s_ec, b + 1)
                v.tensor_scalar(cden, ec, 1e-8 / (1 - FIELD), (1 + 1e-8) / (1 - FIELD), ALU.mult, ALU.add).then_inc(s_cden, 1)
                v.wait_ge(s_pv, FG * b + FG)
                v.wait_ge(s_cden, b + 1)
                o9 = bank(6, 0, 144).rearrange("p (h d) -> p h d", d=9)
                v.tensor_tensor(zden.unsqueeze(2), o9[:, :, HD:HD + 1], cden.unsqueeze(2), ALU.mult).then_inc(s_zd, 1)
                v.wait_ge(s_zd, b + 1)
                v.reciprocal(rz_att, zden).then_inc(s_rz, 1)
                v.wait_ge(s_rz, b + 1)
                v.tensor_tensor(o_n.rearrange("p (h d) -> p h d", d=HD), o9[:, :, 0:HD],
                                rz_att.unsqueeze(2).broadcast_to([P, NH, HD]), ALU.mult).then_inc(s_on, 1)
                v.wait_ge(s_on, b + 1)
                v.wait_ge(s_vs, b + 1)
                wait(v, s_oTp, b)
                wait(v, s_ostore, b)
                v.scalar_tensor_tensor(o_s, bank(6, 384, 512), col(fas, b), o_n, ALU.mult, ALU.add).then_inc(s_os, 1)

            v.wait_ge(pool_setup, 5)
            setup_done("wgr")
            shifted_scores(0)
            attend(0, True)
            with v.Fori(1, B - 1) as b:
                attend(b, True)
            attend(B - 1, False)

            def norm_done(name):
                v.wait_ge(dve_norm, NORM_DVE.index(name) + 1)

            v.wait_ge(s_x1, B)
            v.wait_ge(s_ostore, B)
            v.tensor_reduce(small[:, 16:17], o_sum, AX_X, ALU.add).then_inc(dve_norm, 1)
            norm_done("mean_col")
            v.tensor_scalar(mean_bc, ones, small[:, 16:17], 1.0 / TOK, ALU.mult, ALU.mult).then_inc(dve_norm, 1)
            v.tensor_reduce(small[:, 17:18], x1_sum, AX_X, ALU.add).then_inc(dve_norm, 1)
            norm_done("x1mean")
            v.tensor_scalar(x1neg, ones, small[:, 17:18], -1.0 / TOK, ALU.mult, ALU.mult).then_inc(dve_norm, 1)
            v.wait_ge(pe_norm, 1)
            v.tensor_tensor(o_c.rearrange("p (t n) -> p t n", t=B), o_all.rearrange("p (t n) -> p t n", t=B),
                            bank(0, 0, P).unsqueeze(1).broadcast_to([P, B, P]), ALU.subtract).then_inc(dve_norm, 1)
            v.wait_ge(pe_norm, 2)
            v.tensor_scalar(cov, bank(6, 0, P), 1.0 / TOK, None, ALU.mult).then_inc(dve_norm, 1)
            for c in range(4):
                v.wait_ge(pe_norm, NORM_PE.index("CU0") + c + 1)
                v.tensor_tensor(T[:, 512 * c:512 * c + 512], bank(2 + c), U[:, 512 * c:512 * c + 512],
                                ALU.mult).then_inc(dve_norm, 1)
            v.wait_ge(pe_norm, NORM_PE.index("var") + 1)
            v.tensor_scalar(small[:, 0:B], bank(7, 0, B), 1e-5, None, ALU.add).then_inc(dve_norm, 1)
            v.wait_ge(pool_norm, 1)
            v.tensor_tensor(scale_a, rstd, A("gamma"), ALU.mult).then_inc(dve_norm, 1)
            norm_done("scale")
            k3 = lambda ap: ap.rearrange("p (c k) -> p c k", k=NK)
            v.tensor_tensor(k3(ka), k3(A("keysT")), scale_a.unsqueeze(2).broadcast_to([P, 16, NK]), ALU.mult).then_inc(dve_norm, 1)
            v.tensor_tensor(k3(kb), k3(A("keysT")), A("beta").unsqueeze(2).broadcast_to([P, 16, NK]), ALU.mult).then_inc(dve_norm, 1)
            v.wait_ge(pe_norm, NORM_PE.index("weff") + 1)
            v.tensor_copy(weff[:, :], bank(1)).then_inc(dve_norm, 1)
            v.wait_ge(pe_norm, NORM_PE.index("sim_bias") + 1)
            v.tensor_copy(sim_bias[:, :], bank(5)).then_inc(dve_norm, 1)
            norm_done("sim_bias")

            def top_pairs(t, a):
                v.wait_ge(t_simp, t + 1)
                wait(v, h_S, 8 * t - 8)
                v.tensor_tensor(sim[a][:, :, :].rearrange("p c k -> p (c k)"), bank(6), sim_bias[:, :],
                                ALU.add).then_inc(topk, 1)
                v.wait_ge(topk, 1)
                for c in range(16):
                    m = v.max(top_keys[:, c, :], sim[a][:, c, :])
                m.then_inc(topk, 1)
                v.wait_ge(topk, 2)
                v.tensor_tensor(pairs[:, :, :, :],
                                top_keys[:, 0:PH, :].unsqueeze(3).broadcast_to([P, PH, 8, 8]),
                                top_keys[:, PH:16, :].unsqueeze(2).broadcast_to([P, PH, 8, 8]), ALU.add).then_inc(topk, 1)
                v.wait_ge(topk, 3)
                for h in range(PH):
                    m = v.max(top[a][:, h, :], pairs[:, h, :, :].rearrange("p a b -> p (a b)"))
                m.then_inc(topk, 1)
                v.wait_ge(topk, 4)
                v.sem_clear(topk)
                wait(v, h_E, 8 * t - 8)
                v.tensor_scalar(neg_max[a][:, :].unsqueeze(2), top[a][:, :, 0:1], -1.0, None, ALU.mult).then_inc(t_sim, 1)
                wait(v, t_ez, t)
                v.tensor_tensor(dtop[:, :, :], top[a][:, :, :], top[a][:, :, 0:1].broadcast_to([P, PH, 8]),
                                ALU.subtract).then_inc(t_top, 1)

            def top_sums(t, a):
                v.wait_ge(t_ez, t + 1)
                v.tensor_reduce(zsum[:, :], etop[:, :, :], AX_X, ALU.add).then_inc(t_zs, 1)
                v.wait_ge(t_zs, t + 1)
                v.reciprocal(rz[a][:, :], zsum[:, :]).then_inc(t_rz, 1)

            def mask(t, a, h):
                hs, slot = 8 * t + h, (8 * a + h) % RING
                v.wait_ge(h_E, hs + 1)
                v.scalar_tensor_tensor(E[slot], S[slot], top[a][:, h, 7:8], E[slot], ALU.is_ge, ALU.mult).then_inc(h_me, 1)

            def add_weights(t, a, h):
                hs, slot = 8 * t + h, (8 * a + h) % RING
                v.wait_ge(h_me, hs + 1)
                if h == 0:
                    v.wait_ge(t_rz, t + 1)
                    wait(v, t_Tp, t - 1)
                    v.tensor_scalar(W[a], E[slot], rz[a][:, 0:1], None, ALU.mult).then_inc(h_w, 1)
                else:
                    v.wait_ge(h_w, hs)
                    v.scalar_tensor_tensor(W[a], E[slot], rz[a][:, h:h + 1], W[a], ALU.mult, ALU.add).then_inc(h_w, 1)

            def add_peer(t, a):
                v.wait_ge(t_x2p, t + 1)
                wait(v, t_xst, t - 1)
                wait(v, t_ssq, t - 1)
                wait(v, t_trp, t - 1)
                v.tensor_tensor(x2s[a][:, :], bank(6, 0, P), tile_of(x_all, t), ALU.add).then_inc(t_x2, 1)

            def pick_two(n):
                for a in range(2):
                    m = v.max(best[:, a, :], prob[:, a, :])
                m.then_inc(gate, 1)
                v.wait_ge(gate, 7)
                for a in range(2):
                    m = v.max_index(besti[:, a, :], best[:, a, :], prob[:, a, :])
                m.then_inc(gate, 1)
                v.wait_ge(gate, 8)
                v.tensor_copy(bestf[:, :, :], besti[:, :, :]).then_inc(gate, 1)
                v.wait_ge(gate, 9)
                wait(v, g_cwTp, n)
                wait(v, e_acc, 8 * n)
                for a in range(2):
                    v.scalar_tensor_tensor(pick[:, a, :], iota8[:, :], bestf[:, a, 0:1], prob[:, a, :], ALU.is_equal, ALU.mult)
                for a in range(2):
                    m = v.scalar_tensor_tensor(cw[:, a, :], iota8[:, :], bestf[:, a, 1:2], prob[:, a, :], ALU.is_equal, ALU.mult)
                m.then_inc(gate, 1)
                v.wait_ge(gate, 10)
                v.tensor_tensor(cw[:, :, :], cw[:, :, :], pick[:, :, :], ALU.add).then_inc(g_cw, 1)
                v.sem_clear(gate)

            def mean_square(Gn):
                v.wait_ge(t_ssq, 2 * Gn + 2)
                wait(v, g_rms, Gn)
                v.tensor_scalar(msq[:, :], ssq[:, :], 1.0 / P, 1e-6, ALU.mult, ALU.add).then_inc(g_msq, 1)

            def gate1(Gn):
                v.wait_ge(g_rms, Gn + 1)
                v.wait_ge(g_g1p, Gn + 1)
                wait(v, g_exp1, Gn)
                for a in range(2):
                    m = v.scalar_tensor_tensor(lg[:, a, :], bank(7, 8 * a, 8 * a + 8), rms[:, a:a + 1],
                                               tile_of(gate_bias, 2 * Gn + a), ALU.mult, ALU.add)
                    m.then_inc(g_lg, 1)
                v.wait_ge(g_lg, 2 * Gn + 2)
                v.tensor_reduce(lmax[:, :], lg[:, :, :], AX_X, ALU.max).then_inc(gate, 2)
                v.wait_ge(gate, 2)
                v.tensor_tensor(lg[:, :, :], lg[:, :, :], lmax[:, :].unsqueeze(2).broadcast_to([P, 2, NE]),
                                ALU.subtract).then_inc(gate, 1)

            def gate1_pick(Gn):
                v.wait_ge(g_exp1, Gn + 1)
                v.tensor_reduce(lsum[:, :], lexp[:, :, :], AX_X, ALU.add).then_inc(gate, 1)
                v.wait_ge(gate, 4)
                v.reciprocal(lmax[:, :], lsum[:, :]).then_inc(gate, 1)
                v.wait_ge(gate, 5)
                v.tensor_tensor(prob[:, :, :], lexp[:, :, :], lmax[:, :].unsqueeze(2).broadcast_to([P, 2, NE]),
                                ALU.mult).then_inc(gate, 1)
                v.wait_ge(gate, 6)
                pick_two(2 * Gn)

            def gate2(Gn):
                v.wait_ge(g_exp2, Gn + 1)
                v.tensor_scalar(lg[:, :, :], lexp[:, :, :], 1.0, None, ALU.add).then_inc(gate, 5)
                v.wait_ge(gate, 5)
                v.reciprocal(prob[:, :, :], lg[:, :, :]).then_inc(gate, 1)
                v.wait_ge(gate, 6)
                pick_two(2 * Gn + 1)

            def weights_T(n):
                v.wait_ge(g_cwTp, n + 1)
                wait(v, g_bias, n)
                v.tensor_copy(cwT[:, :], banks[0:NE, 7, 0:2 * P]).then_inc(g_cwT, 1)

            def init1(Gn):
                v.wait_ge(g_bias, 2 * Gn + 1)
                v.tensor_copy(acc[:, :, :], bank(7, 256, 512).rearrange("p (a n) -> p a n", a=2)).then_inc(g_binit, 1)

            def init2(Gn):
                v.wait_ge(g_bias, 2 * Gn + 2)
                wait(v, g_out, 32 * Gn)
                v.wait_ge(t_xst, 2 * Gn + 2)
                for a in range(2):
                    m = v.tensor_tensor(acc_f[:, a, :], bank(7, 256 + P * a, 384 + P * a), tile_of(x_all, 2 * Gn + a), ALU.add)
                m.then_inc(g_binit, 1)

            def add_expert(Gn, n):
                e = n % 8
                if e == 0:
                    v.wait_ge(g_binit, 2 * Gn + 1 + n // 8)
                    v.wait_ge(g_cw, 2 * Gn + 1 + n // 8)
                else:
                    v.wait_ge(e_acc, 16 * Gn + n)
                v.wait_ge(e_y, 16 * Gn + n + 1)
                dst = acc if n < 8 else acc_f
                for a in range(2):
                    m = v.scalar_tensor_tensor(dst[:, a, :], bank(4 + n % 2, P * a, P * a + P),
                                               cw[:, a, e:e + 1], dst[:, a, :], ALU.mult, ALU.add)
                m.then_inc(e_acc, 1)

            top_pairs(0, 0)

            def turn(g, peer, new, old, more=True):
                t = 2 * g
                for s in range(16):
                    if peer:
                        if s == 0:
                            top_sums(t, 0)
                        mask(t + s // 8, s // 8, s % 8)
                    if s == 0:
                        if new:
                            add_weights(t - 1, 1, 7)
                    elif peer:
                        add_weights(t + (s - 1) // 8, (s - 1) // 8, (s - 1) % 8)
                    if s < 4 and old:
                        add_expert(g - 2, s + 11)
                    if s == 2 and new:
                        add_peer(t - 1, 1)
                    if s == 3 and new:
                        mean_square(g - 1)
                        gate1(g - 1)
                    if s == 4:
                        if old:
                            add_expert(g - 2, 15)
                        if new:
                            gate1_pick(g - 1)
                            weights_T(2 * (g - 1))
                            init1(g - 1)
                    if new and s >= 5 and s <= 12:
                        add_expert(g - 1, s - 5)
                    if new and s == 13:
                        gate2(g - 1)
                        weights_T(2 * (g - 1) + 1)
                        init2(g - 1)
                        add_expert(g - 1, 8)
                    if new and s >= 14:
                        add_expert(g - 1, s - 5)
                    if peer:
                        if s == 3:
                            top_pairs(t + 1, 1)
                        if s == 6:
                            top_sums(t + 1, 1)
                        if s == 10:
                            add_peer(t, 0)
                        if s == 13 and more:
                            top_pairs(t + 2, 0)

            turn(0, True, False, False)
            turn(1, True, True, False)
            with v.Fori(2, NG - 1) as g:
                turn(g, True, True, True)
            turn(NG - 1, True, True, True, more=False)
            turn(NG, False, True, True)
            turn(NG + 1, False, False, True)


def kernel(**inputs):
    import numpy as _np
    import concourse.bacc as _bacc
    from concourse import mybir as _mybir
    from concourse.bass_utils import run_bass_kernel_spmd as _run

    i = {k: _np.asarray(v) for k, v in inputs.items()}
    c0, f0, c1, f1 = (lambda n, p=p: i[p + n] for p in ("L0_cond_", "L0_ffn_", "L1_cond_", "L1_ffn_"))
    f32 = _np.float32

    def side(parts, widths):
        return _np.concatenate([_np.reshape(parts[n], (-1, w)) for n, w in widths.items()], axis=1)

    WT = c0("Wqkv").T
    bqkv = c0("bqkv")
    pos = _np.arange(P, dtype=f32)
    inv = _np.power(f32(10000.0), _np.repeat(_np.arange(0, P, 2, dtype=f32) / f32(P), 2))
    pe = _np.sin(pos[:, None] / inv[None, :]).astype(f32)
    pA = side(dict(
        wqT=WT[:, 0:P], wkT=WT[:, P:2 * P], wvT=WT[:, 2 * P:], bq=bqkv[0:P], bk=bqkv[P:2 * P],
        head_of=_np.repeat(_np.eye(NH, dtype=f32), HD, axis=0),
        woT=c0("Wout").T, wo=c0("Wout"), wc1T=c0("Wc1")[:, :P].T, wc2T=c0("Wc2").T, we2T=c0("We2").T,
        peT=pe.T, ident=_np.eye(P, dtype=f32), bout=c0("bout"), bc1=c0("bc1"), be1=c0("be1"),
        gamma=f0("bn_gamma").reshape(16, P).T, beta=f0("bn_beta").reshape(16, P).T,
        keysT=f0("keys").transpose(3, 2, 0, 1)), COLS_A)
    pL = side(dict(
        b1=c1("b1").reshape(16, P).T, b2=c1("b2").reshape(16, P).T, bf=f1("b1").reshape(32, P).T,
        wgr=c1("wg_W"), rms=c1("rms_w"), wgf=f1("Wg")), COLS_L)
    pC = side(dict(wc1c=c0("Wc1")[:, P:].T, csT=i["cond_256"].T, we1T=c0("We1").T, ggW=c1("gg_W")), COLS_C)
    pR = side(dict(bv=bqkv[2 * P:], bc2=c0("bc2"), be2=c0("be2"), ln_g=c0("ln_g"), ln_b=c0("ln_b"),
                   wgb=c1("wg_b"), ggb=c1("gg_b")), COLS_R)
    p8 = side(dict(b3=c1("b3"), b2f=f1("b2")), COLS_8)
    x = i["x"]
    w_q = f0("w_q")
    arrays = dict(
        xtok=x, xT=x.reshape(TOK, P).T, pA=pA, pL=pL, pC=pC, pR=pR, p8=p8, wq=w_q,
        wqT=w_q.reshape(P, 16, P).transpose(2, 1, 0).reshape(P, 16 * P),
        down=f0("down_embed").T, up=f0("up_embed"), w1=c1("W1"), w2=c1("W2"), w3=c1("W3"),
        f1=f1("W1"), f2=f1("W2"))
    nc = _bacc.Bacc("TRN2", target_bir_lowering=False, num_devices=1)
    maps, args = {}, []
    for name, a in arrays.items():
        a = _np.ascontiguousarray(a)
        maps[f"in_{name}"] = a
        args.append(nc.dram_tensor(f"in_{name}", a.shape, _mybir.dt.from_np(a.dtype), kind="ExternalInput").ap())
    args.append(nc.dram_tensor("out_x", (B, P, P), F32, kind="ExternalOutput").ap())
    program(nc, *args)
    r = _run(nc, [maps], core_ids=[0])
    return r.results[0]["out_x"]
```

```python
from contextlib import ExitStack

import numpy as np

import concourse.bass as bass
from concourse import mybir

F32 = mybir.dt.float32
U32 = mybir.dt.uint32
ALU = mybir.AluOpType
ACT = mybir.ActivationFunctionType
AX_X = mybir.AxisListType.X

P = 128
B = 16
NH, HD = 16, 8
CD = 32
FG = 4
FIELD = 0.3 * 0.7
PH = 8
NK = 32
NE = 8
M1 = 256
FF = 512
NG = B // 2
TOK = B * P
RING = 8

COLS_A = dict(wqT=128, wkT=128, wvT=128, bq=1, bk=1, head_of=16, woT=128, wo=128, wc1T=128, wc2T=16,
              we2T=128, peT=128, ident=128, bout=1, bc1=1, be1=1, gamma=16, beta=16, keysT=512)
COLS_L = dict(b1=16, b2=16, bf=32, wgr=8, rms=1, wgf=8)
COLS_C = dict(wc1c=128, csT=16, we1T=128, ggW=8)
COLS_R = dict(bv=128, bc2=16, be2=128, ln_g=128, ln_b=128, wgb=8, ggb=8)
COLS_8 = dict(b3=128, b2f=128)


def columns(widths):
    at, n = {}, 0
    for name, w in widths.items():
        at[name] = (n, n + w)
        n += w
    return at, n


PE_SETUP = ["hid_bias", "field1", "field2", "fpT", "field_scores", "faT", "gate_bias",
            "U0", "U1", "U2", "U3"]
DVE_SETUP = ["consts", "gate_rhs", "hid_bias", "f2", "stats", "aggr", "vareps", "f3", "f4g", "f4b", "fpT",
             "field_max", "fa_recip", "fa", "faT", "gate_rows", "gate_bias", "wgr"]
ACT_SETUP = ["field1", "field_exp", "U0", "U1", "U2", "U3"]
NORM_PE = ["mean_row", "cov", "CU0", "CU1", "CU2", "CU3", "var", "weff", "sim_bias"]
NORM_DVE = ["mean_col", "mean_bc", "x1mean", "x1neg", "centred", "cov", "T0", "T1", "T2", "T3",
            "vareps", "scale", "ka", "kb", "weff", "sim_bias"]


def program(nc, xtok, xT, pA, pL, pC, pR, p8, wq, wqT, down, up, w1, w2, w3, f1, f2, out):
    A_AT, A_N = columns(COLS_A)
    L_AT, L_N = columns(COLS_L)
    C_AT, C_N = columns(COLS_C)
    R_AT, R_N = columns(COLS_R)
    E_AT, E_N = columns(COLS_8)
    ds = bass.ds

    with ExitStack() as ctx:
        def sb(name, shape, dt=F32):
            return ctx.enter_context(nc.sbuf_tensor(name, shape, dt))

        def sem(name):
            return ctx.enter_context(nc.semaphore(name))

        x_all = sb("x_all", [P, B, P])
        x1T_all = sb("x1T_all", [P, TOK])
        downT = sb("downT", [P, NK * NK])
        up_sb = sb("up_sb", [P, PH, P])
        w1_sb = sb("w1_sb", [P, NE, M1])
        w2_sb = sb("w2_sb", [P, NE, 2, M1])
        w3_sb = sb("w3_sb", [P, NE, 2, P])
        f1_sb = sb("f1_sb", [P, NE, FF])
        f2_sb = sb("f2_sb", [P, NE, 4, P])
        lpack = sb("lpack", [P, L_N])
        epack = sb("epack", [NE, E_N])
        ident = sb("ident", [P, P])
        weff = sb("weff", [P, 512])
        sim_bias = sb("sim_bias", [P, 512])
        gate_bias = sb("gate_bias", [P, B, NE])
        iota8 = sb("iota8", [P, NE])
        mhalf = sb("mhalf", [P, B])

        def L(name, a=0, b=None):
            lo, hi = L_AT[name]
            return lpack[:, lo + a:hi if b is None else lo + b]

        region = sb("region", [P, 2 * RING, 1024])
        flat = region[:, :, :].rearrange("p a n -> p (a n)")
        used = [0]

        def part(n):
            used[0] += n
            assert used[0] <= 2 * RING * 1024
            return flat[:, used[0] - n:used[0]]

        wq_sb = part(2048)
        wqT_sb = part(2048)
        U = part(2048)
        o_all = part(TOK)
        qT, kT = part(P), part(P)
        k_heads = part(2048)
        apack = part(A_N)
        v_aug = part(NH * 9)
        xTs, thT, o_s, oT = part(P), part(P), part(P), part(P)
        cpack = part(C_N)
        rows = part(R_N)
        gate_rhs, gate_rows, ones = part(P), part(NE), part(P)
        hidb, fas = part(B), part(B)
        mx4 = part(16)
        tl, ec, cden, zden, rz_att = part(NH), part(NH), part(NH), part(NH), part(NH)
        o_n = part(P)
        v_stage = part(P)
        field_a, field_b, fpT, fa = part(P), part(P), part(B), part(P)
        small = part(32)
        o_sum, x1_sum = part(B), part(B)
        mean_bc, x1neg = part(P), part(P)
        cov = part(P)
        rstd, scale_a = part(B), part(B)
        ka, kb = k_heads[:, 0:512], k_heads[:, 512:1024]

        def A(name, a=0, b=None):
            lo, hi = A_AT[name]
            return apack[:, lo + a:hi if b is None else lo + b]

        def C(name):
            lo, hi = C_AT[name]
            return cpack[0:CD, lo:hi]

        def R(name, rows_=P):
            lo, hi = R_AT[name]
            return rows[0:rows_, lo:hi]

        S = [region[:, n, :] for n in range(RING)]
        E = [region[:, RING + n, :] for n in range(RING)]

        x1s = [sb(f"x1s{a}", [P, P]) for a in range(2)]
        sim = [sb(f"sim{a}", [P, 16, NK]) for a in range(2)]
        top_keys = sb("top_keys", [P, 16, 8])
        pairs = sb("pairs", [P, PH, 8, 8])
        top = [sb(f"top{a}", [P, PH, 8]) for a in range(2)]
        neg_max = [sb(f"neg_max{a}", [P, PH]) for a in range(2)]
        dtop = sb("dtop", [P, PH, 8])
        etop = sb("etop", [P, PH, 8])
        zsum = sb("zsum", [P, PH])
        rz = [sb(f"rz{a}", [P, PH]) for a in range(2)]
        W_both = sb("W_both", [P, 2048])
        G_both = sb("G_both", [P, 2048])
        W = [W_both[:, 1024 * a:1024 * a + 1024] for a in range(2)]
        G = [G_both[:, 1024 * a:1024 * a + 1024] for a in range(2)]
        D = [W_both[:, 512 * r:512 * r + 512] for r in range(FG)]
        ET = [G_both[:, 512 * r:512 * r + 512] for r in range(FG)]
        o_c, T = W_both[:, :], G_both[:, :]
        PT = sb("PT", [P, 1024])
        x2s = [sb(f"x2s{a}", [P, P]) for a in range(2)]
        x2T = sb("x2T", [P, 2 * P])
        square = sb("square", [P, P])
        ssq = sb("ssq", [P, 2])
        msq = sb("msq", [P, 2])
        rms = sb("rms", [P, 2])
        HF = [sb(f"HF_{n}", [P, 4, 256]) for n in range(2)]
        H1 = [HF[0][:, 2 * n:2 * n + 2, :] for n in range(2)]
        H2 = [sb(f"H2_{n}", [P, 2, 256]) for n in range(2)]
        acc = sb("acc", [P, 2, P])
        cT = sb("cT", [P, 2 * P])
        acc_f = sb("acc_f", [P, 2, P])
        lg = sb("lg", [P, 2, NE])
        lmax = sb("lmax", [P, 2])
        lexp = sb("lexp", [P, 2, NE])
        lsum = sb("lsum", [P, 2])
        prob = sb("prob", [P, 2, NE])
        best = sb("best", [P, 2, 8])
        besti = sb("besti", [P, 2, 8], U32)
        bestf = sb("bestf", [P, 2, 8])
        pick = sb("pick", [P, 2, NE])
        cw = sb("cw", [P, 2, NE])
        cwT = sb("cwT", [NE, 2 * P])

        banks = ctx.enter_context(nc.psum_tensor("banks", [P, 8, 512], F32))

        def bank(n, a=0, b=512):
            return banks[:, n, a:b]

        ld_a, ld_c, ld_r, ld_x, ld_wq, ld_wqT = (sem(n) for n in ("ld_a", "ld_c", "ld_r", "ld_x", "ld_wq", "ld_wqT"))
        ld_w, ld_l, ld_xtok = sem("ld_w"), sem("ld_l"), sem("ld_xtok")
        pe_setup, dve_setup, act_setup, pool_setup = sem("pe_setup"), sem("dve_setup"), sem("act_setup"), sem("pool_setup")
        s_proj, s_v, s_hid, s_coh = sem("s_proj"), sem("s_v"), sem("s_hid"), sem("s_coh")
        s_tanh, s_tl, s_ec, s_cden = sem("s_tanh"), sem("s_tl"), sem("s_ec"), sem("s_cden")
        s_qk, s_q, s_kh = sem("s_qk"), sem("s_q"), sem("s_kh")
        s_vst, s_x = sem("s_vst"), sem("s_x")
        s_S, s_mx, s_D, s_E, s_T, s_ET, s_pv = (sem("att_" + n) for n in ("S", "mx", "D", "E", "T", "ET", "pv"))
        s_vs = sem("s_vs")
        s_zd, s_rz, s_on, s_os, s_ostore = sem("s_zd"), sem("s_rzatt"), sem("s_on"), sem("s_os"), sem("s_ostore")
        s_oTp, s_oT, s_x1p, s_x1 = sem("s_oTp"), sem("s_oT"), sem("s_x1p"), sem("s_x1")
        pe_norm, dve_norm, pool_norm = sem("pe_norm"), sem("dve_norm"), sem("pool_norm")

        t_x1s, t_simp, t_simr, t_sim = sem("t_x1s"), sem("t_simp"), sem("t_simr"), sem("t_sim")
        topk = sem("topk")
        t_top, t_ez, t_zs, t_rz, t_Hp, t_G = (sem("t_" + n) for n in ("top", "ez", "zs", "rz", "Hp", "G"))
        h_S, h_E, h_me, h_w = sem("h_S"), sem("h_E"), sem("h_me"), sem("h_w")
        t_P, t_Tp, t_PT, t_x2p, t_x2, t_xst, t_ssq, t_trp, t_x2T = (
            sem("t_" + n) for n in ("P", "Tp", "PT", "x2p", "x2", "xst", "ssq", "trp", "x2T"))
        e_h1, e_r1, e_h2, e_r2, e_hf, e_g = (sem("e_" + n) for n in ("h1", "r1", "h2", "r2", "hf", "g"))
        e_y, e_acc = sem("e_y"), sem("e_acc")
        g_msq, g_rms, g_g1p, g_lg, g_exp1, g_g2p, g_exp2 = (
            sem("g_" + n) for n in ("msq", "rms", "g1p", "lg", "exp1", "g2p", "exp2"))
        gate = sem("gate")
        g_cw, g_cwTp, g_cwT, g_bias, g_badd, g_cTp, g_cT = (
            sem("g_" + n) for n in ("cw", "cwTp", "cwT", "bias", "badd", "cTp", "cT"))
        g_out = sem("g_out")

        def wait(eng, s, value):
            if not isinstance(value, int) or value > 0:
                eng.wait_ge(s, value)

        def col(ap, i):
            return ap[:, ds(i, 1)] if not isinstance(i, int) else ap[:, i:i + 1]

        def cols(ap, i, n=P):
            return ap[:, ds(i * n, n)] if not isinstance(i, int) else ap[:, i * n:(i + 1) * n]

        def tile_of(ap, t):
            if isinstance(t, int):
                return ap[:, t, :]
            return ap[:, ds(t, 1), :].rearrange("p a n -> p (a n)")

        block = ctx.enter_context(nc.Block())

        @block.sync
        def _(sp):
            sp.dma_start(apack, pA).then_inc(ld_a, 16)
            sp.dma_start(cpack[0:CD, :], pC).then_inc(ld_c, 16)
            sp.dma_start(rows, pR.broadcast_to([P, R_N])).then_inc(ld_r, 16)
            sp.dma_start(x1T_all[:, :], xT).then_inc(ld_x, 16)
            sp.dma_start(lpack[:, :], pL).then_inc(ld_l, 16)
            sp.dma_start(ident[:, :], pA[:, A_AT["ident"][0]:A_AT["ident"][1]]).then_inc(ld_l, 16)
            sp.dma_start(epack[:, :], p8).then_inc(ld_l, 16)
            sp.dma_start(wq_sb, wq).then_inc(ld_wq, 16)
            sp.dma_start(wqT_sb, wqT).then_inc(ld_wqT, 16)
            for dst, src in ((downT[:, :], down), (x_all[:, :, :], xtok.rearrange("b s e -> s b e")),
                             (up_sb[:, :, :], up.rearrange("(c p) d -> p c d", p=P)),
                             (w1_sb[:, :, :], w1.rearrange("e h m -> h e m")),
                             (w2_sb[:, :, :, :].rearrange("p e c n -> p (e c) n"),
                              w2.rearrange("e (c p) n -> p (e c) n", p=P)),
                             (w3_sb[:, :, :, :].rearrange("p e c n -> p (e c) n"),
                              w3.rearrange("e (c p) n -> p (e c) n", p=P)),
                             (f1_sb[:, :, :], f1.rearrange("e d f -> d e f")),
                             (f2_sb[:, :, :, :].rearrange("p e c n -> p (e c) n"),
                              f2.rearrange("e (c p) n -> p (e c) n", p=P))):
                sp.dma_start(dst, src).then_inc(ld_w, 16)

            def store(Gn):
                sp.wait_ge(e_acc, 16 * Gn + 16)
                for a in range(2):
                    sp.dma_start(out[ds(2 * Gn + a, 1), :, :].rearrange("a s e -> s (a e)"),
                                 acc_f[:, a, :]).then_inc(g_out, 16)

            with sp.Fori(0, NG) as Gn:
                store(Gn)
            sp.wait_ge(g_out, 32 * NG)

        @block.gpsimd
        def _(pool):
            pool.memset(mhalf[:, :], -0.5).then_inc(pool_setup, 1)
            pool.memset(ones, 1.0).then_inc(pool_setup, 1)
            pool.memset(v_aug, 1.0).then_inc(pool_setup, 1)
            pool.iota(iota8[:, :], [[1, NE]], base=0, channel_multiplier=0,
                      allow_small_or_imprecise_dtypes=True).then_inc(pool_setup, 1)
            pool.wait_ge(pool_setup, 4)
            pool.wait_ge(dve_setup, DVE_SETUP.index("vareps") + 1)
            pool.tensor_tensor(small[0:B, 9:10], small[0:B, 8:9], mhalf[0:B, 0:1], ALU.pow).then_inc(pool_setup, 1)
            heads = lambda ap: ap.rearrange("p (h d) -> p h d", h=NH)

            def values(b):
                pool.wait_ge(s_vst, b + 1)
                wait(pool, s_pv, FG * b)
                wait(pool, s_vs, b)
                pool.tensor_tensor(heads(v_aug)[:, :, 0:HD], heads(v_stage), heads(R("bv")), ALU.add).then_inc(s_v, 1)

            def keep_output(b):
                pool.wait_ge(s_os, b + 1)
                pool.tensor_copy(cols(o_all, b), o_s).then_inc(s_ostore, 1)

            def stage_x(b):
                wait(pool, s_proj, b)
                pool.tensor_copy(xTs, cols(x1T_all, b)).then_inc(s_x, 1)

            def head_keys(b):
                pool.wait_ge(s_q, b + 1)
                for r in range(FG):
                    wait(pool, s_S, FG * (b - 1) + r + 1)
                    pool.tensor_tensor(k_heads[:, 512 * r:512 * r + 512].rearrange("p (g n) -> p g n", g=FG),
                                       kT.unsqueeze(1).broadcast_to([P, FG, P]),
                                       A("head_of", FG * r, FG * r + FG).unsqueeze(2).broadcast_to([P, FG, P]),
                                       ALU.mult).then_inc(s_kh, 1)

            pool.wait_ge(ld_x, 16)
            stage_x(0)
            pool.wait_ge(ld_r, 16)
            pool.wait_ge(ld_a, 16)
            head_keys(0)
            values(0)
            stage_x(1)
            head_keys(1)
            stage_x(2)

            def attend(b, more):
                values(b + 1)
                head_keys(b + 2)
                keep_output(b)
                if more:
                    stage_x(b + 3)

            attend(0, True)
            with pool.Fori(1, B - 3) as b:
                attend(b, True)
            attend(B - 3, False)
            values(B - 1)
            keep_output(B - 2)
            keep_output(B - 1)
            pool.wait_ge(dve_norm, NORM_DVE.index("vareps") + 1)
            pool.tensor_tensor(rstd, small[:, 0:B], mhalf[:, :], ALU.pow).then_inc(pool_norm, 1)

            def stage_x1(t, a):
                wait(pool, t_Hp, 2 * t - 2)
                pool.tensor_copy(x1s[a][:, :], cols(x1T_all, t)).then_inc(t_x1s, 1)

            def pair_scores(t, a, h):
                hs, slot = 8 * t + h, h
                if h == 0:
                    pool.wait_ge(t_simr, t + 1)
                wait(pool, h_me, hs - RING + 1)
                pool.tensor_tensor(
                    S[slot].rearrange("p (i j) -> p i j", i=NK),
                    sim[a][:, h, :].unsqueeze(2).broadcast_to([P, NK, NK]),
                    sim[a][:, PH + h, :].unsqueeze(1).broadcast_to([P, NK, NK]),
                    ALU.add).then_inc(h_S, 1)

            def weigh(t, a):
                pool.wait_ge(h_w, 8 * t + 8)
                pool.wait_ge(t_G, t + 1)
                pool.tensor_tensor(W[a], W[a], G[a], ALU.mult).then_inc(t_P, 1)

            def keep_x2(t, a):
                pool.wait_ge(t_x2, t + 1)
                pool.tensor_copy(tile_of(x_all, t), x2s[a][:, :]).then_inc(t_xst, 1)

            pool.wait_ge(s_x1, B)
            pool.wait_ge(dve_norm, len(NORM_DVE))
            stage_x1(0, 0)
            stage_x1(1, 1)

            def turn(g, peer, new, more=True):
                t = 2 * g
                if peer and new:
                    pair_scores(t, 0, 7)
                if new:
                    weigh(t - 1, 1)
                if more:
                    stage_x1(t + 2, 0)
                if new:
                    keep_x2(t - 1, 1)
                    pool.wait_ge(g_msq, g)
                    pool.tensor_tensor(rms[:, :], msq[:, :], mhalf[:, 0:2], ALU.pow).then_inc(g_rms, 1)
                if not peer:
                    return
                for h in range(8):
                    pair_scores(t + 1, 1, h)
                weigh(t, 0)
                if more:
                    pair_scores(t + 2, 0, 0)
                    pair_scores(t + 2, 0, 1)
                keep_x2(t, 0)
                if more:
                    for h in range(2, 5):
                        pair_scores(t + 2, 0, h)
                    stage_x1(t + 3, 1)
                    for h in range(5, 7):
                        pair_scores(t + 2, 0, h)

            for h in range(8):
                pair_scores(0, 0, h)
            turn(0, True, False)
            with pool.Fori(1, NG - 1) as g:
                turn(g, True, True)
            turn(NG - 1, True, True, more=False)
            turn(NG, False, True, more=False)

        @block.tensor
        def _(pe):
            def mm(o, l, r, start=True, stop=True):
                return pe.matmul(o, l, r, start=start, stop=stop)

            pe.wait_ge(ld_a, 16)
            pe.wait_ge(ld_c, 16)
            pe.wait_ge(pool_setup, 4)
            mm(bank(7, 0, B), C("wc1c"), C("csT")).then_inc(pe_setup, 1)
            mm(bank(6, 0, B), C("we1T"), C("csT")).then_inc(pe_setup, 1)
            pe.wait_ge(act_setup, 1)
            mm(banks[0:B, 1, 0:P], thT[:, 0:B], A("we2T")).then_inc(pe_setup, 1)
            pe.wait_ge(dve_setup, DVE_SETUP.index("f4b") + 1)
            pe.transpose(bank(0, 0, B), field_b[0:B, :], A("ident")[0:B, 0:B]).then_inc(pe_setup, 1)
            pe.wait_ge(dve_setup, DVE_SETUP.index("fpT") + 1)
            mm(banks[0:B, 6, 0:P], fpT, A("peT")).then_inc(pe_setup, 1)
            pe.wait_ge(dve_setup, DVE_SETUP.index("fa") + 1)
            pe.transpose(bank(1, 0, B), fa[0:B, :], A("ident")[0:B, 0:B]).then_inc(pe_setup, 1)
            mm(bank(7, 128, 256), ones[0:CD, :], gate_rhs[0:CD, :]).then_inc(pe_setup, 1)
            pe.wait_ge(ld_wq, 16)
            for c in range(4):
                mm(bank(2 + c), A("wo"), wq_sb[:, 512 * c:512 * c + 512]).then_inc(pe_setup, 1)

            def project(b):
                pe.wait_ge(s_x, b + 1)
                wait(pe, s_q, b)
                mm(bank(0, 0, P), A("wqT"), xTs)
                mm(bank(0, P, 2 * P), A("wkT"), xTs).then_inc(s_qk, 1)
                wait(pe, s_tanh, b)
                mm(bank(7, 0, P), xTs, A("wvT"))
                mm(bank(7, P, 2 * P), A("wc1T"), xTs).then_inc(s_proj, 1)

            def coherence(b):
                pe.wait_ge(s_tanh, b + 1)
                wait(pe, s_tl, b)
                mm(bank(1, 0, NH), thT, A("wc2T")).then_inc(s_coh, 1)

            def scores(b, r):
                pe.wait_ge(s_q, b + 1)
                pe.wait_ge(s_kh, FG * b + r + 1)
                wait(pe, s_ET, FG * (b - 1) + r + 1)
                mm(bank(2 + r), qT, k_heads[:, 512 * r:512 * r + 512]).then_inc(s_S, 1)

            def transposes(b, r):
                pe.wait_ge(s_E, FG * b + r + 1)
                for g in range(FG):
                    m = pe.transpose(banks[:, 2 + r, P * g:P * g + P], D[r][:, P * g:P * g + P], A("ident"))
                m.then_inc(s_T, 1)

            def values(b, r):
                pe.wait_ge(s_ET, FG * b + r + 1)
                for g in range(FG):
                    h = FG * r + g
                    m = mm(bank(6, 9 * h, 9 * h + 9), ET[r][:, P * g:P * g + P], v_aug[:, 9 * h:9 * h + 9])
                m.then_inc(s_pv, 1)

            def out_T(b):
                pe.wait_ge(s_os, b + 1)
                pe.transpose(bank(6, 144, 272), o_s, A("ident")).then_inc(s_oTp, 1)

            def out_proj(b):
                pe.wait_ge(s_oT, b + 1)
                mm(bank(6, 144, 272), A("woT"), oT).then_inc(s_x1p, 1)

            def attend(b, more, project_more, first=False):
                transposes(b, 0)
                transposes(b, 1)
                if not first:
                    out_T(b - 1)
                transposes(b, 2)
                transposes(b, 3)
                if not first:
                    out_proj(b - 1)
                if more:
                    scores(b + 1, 0)
                pe.wait_ge(s_v, b + 1)
                wait(pe, s_x1, b)
                mm(bank(6, 384, 512), ones, v_aug.rearrange("p (h d) -> p h d", d=9)[:, :, 0:HD]).then_inc(s_vs, 1)
                for r in range(FG):
                    values(b, r)
                    if more and r < FG - 1:
                        scores(b + 1, r + 1)
                if more:
                    coherence(b + 1)
                if project_more:
                    project(b + 2)

            pe.wait_ge(act_setup, len(ACT_SETUP))
            pe.wait_ge(dve_setup, len(DVE_SETUP))
            project(0)
            for r in range(FG):
                scores(0, r)
            coherence(0)
            project(1)
            attend(0, True, True, first=True)
            with pe.Fori(1, B - 2) as b:
                attend(b, True, True)
            attend(B - 2, True, False)
            attend(B - 1, False, False)
            out_T(B - 1)
            out_proj(B - 1)

            pe.wait_ge(dve_norm, NORM_DVE.index("mean_bc") + 1)
            mm(bank(0, 0, P), mean_bc, A("ident")).then_inc(pe_norm, 1)
            pe.wait_ge(dve_norm, NORM_DVE.index("centred") + 1)
            for t in range(B):
                m = mm(bank(6, 0, P), o_c[:, P * t:P * t + P], o_c[:, P * t:P * t + P],
                       start=(t == 0), stop=(t == B - 1))
            m.then_inc(pe_norm, 1)
            pe.wait_ge(dve_norm, NORM_DVE.index("cov") + 1)
            for c in range(4):
                mm(bank(2 + c), cov, U[:, 512 * c:512 * c + 512]).then_inc(pe_norm, 1)
            pe.wait_ge(dve_norm, NORM_DVE.index("T3") + 1)
            for c in range(16):
                m = mm(bank(7, c, c + 1), T[:, P * c:P * c + P], ones[:, 0:1])
            m.then_inc(pe_norm, 1)
            pe.wait_ge(dve_norm, NORM_DVE.index("ka") + 1)
            pe.wait_ge(ld_wqT, 16)
            for c in range(16):
                m = mm(bank(1, NK * c, NK * c + NK), wqT_sb[:, P * c:P * c + P], ka[:, NK * c:NK * c + NK])
            m.then_inc(pe_norm, 1)
            pe.wait_ge(dve_norm, NORM_DVE.index("weff") + 1)
            mm(bank(5), ones, kb, start=True, stop=False)
            mm(bank(5), x1neg, weff[:, :], start=False, stop=True).then_inc(pe_norm, 1)

            pe.wait_ge(ld_w, 16 * 8)
            pe.wait_ge(ld_l, 48)
            pe.wait_ge(dve_norm, len(NORM_DVE))

            def key_scores(t, a):
                pe.wait_ge(t_x1s, t + 1)
                wait(pe, t_simr, t)
                wait(pe, t_x2T, t - 2)
                mm(bank(6), x1s[a][:, :], weff[:, :]).then_inc(t_simp, 1)

            def expert_inputs(t, a, c):
                if c == 0:
                    wait(pe, t_G, t)
                    wait(pe, t_PT, t - 1)
                mm(bank(c), x1s[a][:, :], downT[:, 512 * c:512 * c + 512]).then_inc(t_Hp, 1)

            def weights_T(t, a):
                pe.wait_ge(t_P, t + 1)
                if a == 1:
                    pe.wait_ge(t_G, t + 2 if not isinstance(t, int) else min(t + 2, B))
                wait(pe, t_PT, t)
                for c in range(8):
                    m = pe.transpose(banks[:, c // 4, P * (c % 4):P * (c % 4) + P], W[a][:, P * c:P * c + P], ident[:, :])
                m.then_inc(t_Tp, 1)

            def peer_out(t):
                pe.wait_ge(t_PT, t + 1)
                wait(pe, t_x2T, t)
                wait(pe, t_simr, t + 3 if not isinstance(t, int) else min(t + 3, B))
                for c in range(8):
                    m = mm(bank(6, 0, P), PT[:, P * c:P * c + P], up_sb[:, c, :], start=(c == 0), stop=(c == 7))
                m.then_inc(t_x2p, 1)

            def x2_T(t, a):
                pe.wait_ge(t_x2, t + 1)
                pe.transpose(bank(6, P, 2 * P), x2s[a][:, :], ident[:, :]).then_inc(t_trp, 1)

            def gate1(Gn):
                pe.wait_ge(t_x2T, 2 * Gn + 2)
                wait(pe, g_badd, 2 * Gn)
                for a in range(2):
                    m = mm(bank(7, 8 * a, 8 * a + 8), x2T[:, P * a:P * a + P], L("wgr"))
                m.then_inc(g_g1p, 1)

            def gate2(Gn):
                pe.wait_ge(g_cT, Gn + 1)
                for a in range(2):
                    m = mm(bank(7, 8 * a, 8 * a + 8), cT[:, P * a:P * a + P], L("wgf"))
                m.then_inc(g_g2p, 1)

            def weights_cwT(n):
                pe.wait_ge(g_cw, n + 1)
                for a in range(2):
                    m = pe.transpose(banks[0:NE, 7, P * a:P * a + P], cw[:, a, :], ident[:, :])
                m.then_inc(g_cwTp, 1)

            def weighted_bias(n, name):
                lo, hi = E_AT[name]
                pe.wait_ge(g_cwT, n + 1)
                for a in range(2):
                    m = mm(bank(7, 256 + P * a, 384 + P * a), cwT[:, P * a:P * a + P], epack[:, lo:hi])
                m.then_inc(g_bias, 1)

            def hidden1(Gn, e):
                if e == 0:
                    pe.wait_ge(t_x2T, 2 * Gn + 2)
                    wait(pe, e_g, 16 * Gn)
                wait(pe, e_r1, 8 * Gn + e)
                for m_ in range(2):
                    m = mm(bank(2, 256 * m_, 256 * m_ + 256), w1_sb[:, e, P * m_:P * m_ + P], x2T[:, :])
                m.then_inc(e_h1, 1)

            def hidden2(Gn, e):
                pe.wait_ge(e_r1, 8 * Gn + e + 1)
                wait(pe, e_r2, 8 * Gn + e)
                for n in range(2):
                    for m_ in range(2):
                        m = mm(bank(3, 256 * n, 256 * n + 256), w2_sb[:, e, m_, P * n:P * n + P], H1[e % 2][:, m_, :],
                               start=(m_ == 0), stop=(m_ == 1))
                m.then_inc(e_h2, 1)

            def outputs(Gn, n, w_, h_, e, parts):
                wait(pe, e_acc, 16 * Gn + n - 1)
                for a in range(2):
                    for c in range(parts):
                        m = mm(bank(4 + n % 2, P * a, P * a + P),
                               h_[:, c, P * a:P * a + P], w_[:, e, c, :], start=(c == 0), stop=(c == parts - 1))
                m.then_inc(e_y, 1)

            def hidden_f(Gn, e):
                for b in range(2):
                    if e == 0:
                        pe.wait_ge((e_r1, e_r2)[b], 8 * Gn + 8)
                    else:
                        pe.wait_ge(e_g, 16 * Gn + 2 * e - 1 + b)
                    for f in range(2 * b, 2 * b + 2):
                        m = mm(bank(2 + b, 256 * (f % 2), 256 * (f % 2) + 256), f1_sb[:, e, P * f:P * f + P], cT[:, :])
                    m.then_inc(e_hf, 1)

            def sum_T(Gn):
                pe.wait_ge(e_acc, 16 * Gn + 8)
                for a in range(2):
                    m = pe.transpose(bank(7, P * a, P * a + P), acc[:, a, :], ident[:, :])
                m.then_inc(g_cTp, 1)

            def outputs1(Gn, e):
                pe.wait_ge(e_r2, 8 * Gn + e + 1)
                outputs(Gn, e, w3_sb, H2[e % 2], e, 2)

            def outputs2(Gn, e):
                pe.wait_ge(e_g, 16 * Gn + 2 * e + 2)
                outputs(Gn, 8 + e, f2_sb, HF[e % 2], e, 4)

            key_scores(0, 0)
            expert_inputs(0, 0, 0)
            expert_inputs(0, 0, 1)
            key_scores(1, 1)

            def turn(g, peer, new, old, more=True):
                t, G1, G2 = 2 * g, g - 1, g - 2
                for s in range(16):
                    if s < 4 and old:
                        hidden_f(G2, s + 4)
                    if s == 3 and new:
                        x2_T(t - 1, 1)
                    if s < 4 and old:
                        outputs2(G2, s + 3)
                    if s == 0 and old:
                        weights_cwT(2 * G2 + 1)
                    if s == 2 and old:
                        weighted_bias(2 * G2 + 1, "b2f")
                    if s == 1 and new:
                        weights_T(t - 1, 1)
                    if s == 2 and new:
                        peer_out(t - 1)
                    if s == 4 and new:
                        gate1(G1)
                        hidden1(G1, 0)
                    if s == 4 and old:
                        outputs2(G2, 7)
                    if s == 8 and more:
                        key_scores(t + 2, 0)
                    if 4 <= s < 12 and new:
                        e = s - 4
                        if e < 7:
                            hidden1(G1, e + 1)
                        if e >= 2:
                            outputs1(G1, e - 2)
                        hidden2(G1, e)
                        if e == 7:
                            outputs1(G1, 6)
                    if s == 8 and new:
                        weights_cwT(2 * G1)
                    if s == 10 and new:
                        weighted_bias(2 * G1, "b3")
                    if s == 9 and peer:
                        weights_T(t, 0)
                    if s == 10 and peer:
                        peer_out(t)
                    if s == 12:
                        if new:
                            outputs1(G1, 7)
                        if peer:
                            x2_T(t, 0)
                            expert_inputs(t + 1, 1, 0)
                        if new:
                            sum_T(G1)
                        if peer:
                            expert_inputs(t + 1, 1, 1)
                        if new:
                            gate2(G1)
                            hidden_f(G1, 0)
                    if s == 13 and more:
                        key_scores(t + 3, 1)
                    if s > 12 and new:
                        hidden_f(G1, s - 12)
                        outputs2(G1, s - 13)
                    if s == 14 and more:
                        expert_inputs(t + 2, 0, 0)
                        expert_inputs(t + 2, 0, 1)

            turn(0, True, False, False)
            turn(1, True, True, False)
            with pe.Fori(2, NG - 1) as g:
                turn(g, True, True, True)
            turn(NG - 1, True, True, True, more=False)
            turn(NG, False, True, True, more=False)
            turn(NG + 1, False, False, True, more=False)

        @block.scalar
        def _(act):
            act.wait_ge(pe_setup, 2)
            act.activation(thT[:, 0:B], bank(6, 0, B), ACT.Relu, bias=A("be1")).then_inc(act_setup, 1)
            act.wait_ge(dve_setup, DVE_SETUP.index("field_max") + 1)
            act.activation(field_a[0:B, :], banks[0:B, 6, 0:P], ACT.Exp, bias=small[0:B, 10:11],
                           accum_out=small[0:B, 11:12]).then_inc(act_setup, 1)
            for c in range(4):
                act.wait_ge(pe_setup, PE_SETUP.index("U0") + c + 1)
                act.activation(U[:, 512 * c:512 * c + 512], bank(2 + c), ACT.Copy).then_inc(act_setup, 1)

            def projected(b):
                act.wait_ge(s_qk, b + 1)
                wait(act, s_S, FG * b)
                act.activation(qT, bank(0, 0, P), ACT.Identity, bias=A("bq"))
                wait(act, s_kh, FG * b)
                act.activation(kT, bank(0, P, 2 * P), ACT.Identity, bias=A("bk")).then_inc(s_q, 1)
                act.wait_ge(s_proj, b + 1)
                wait(act, s_v, b)
                act.activation(v_stage, bank(7, 0, P), ACT.Copy).then_inc(s_vst, 1)
                wait(act, s_coh, b)
                act.activation(thT, bank(7, P, 2 * P), ACT.Tanh, bias=col(hidb, b)).then_inc(s_tanh, 1)

            def exps(b, r):
                act.wait_ge(s_D, FG * b + r + 1)
                act.activation(D[r], D[r], ACT.Exp, scale=float(HD) ** -0.5).then_inc(s_E, 1)

            def probs_T(b, r):
                act.wait_ge(s_T, FG * b + r + 1)
                wait(act, s_pv, FG * (b - 1) + r + 1)
                act.activation(ET[r], bank(2 + r), ACT.Copy).then_inc(s_ET, 1)

            def out_T(b):
                act.wait_ge(s_oTp, b + 1)
                wait(act, s_x1p, b)
                act.activation(oT, bank(6, 144, 272), ACT.Copy, accum_out=col(o_sum, b)).then_inc(s_oT, 1)

            def out_x1(b):
                act.wait_ge(s_x1p, b + 1)
                act.activation(cols(x1T_all, b), bank(6, 144, 272), ACT.Identity, bias=A("bout"),
                               accum_out=col(x1_sum, b)).then_inc(s_x1, 1)

            def attend(b, more, project_more, first=False):
                probs_T(b, 0)
                probs_T(b, 1)
                if not first:
                    out_T(b - 1)
                probs_T(b, 2)
                probs_T(b, 3)
                if not first:
                    out_x1(b - 1)
                act.wait_ge(s_tl, b + 1)
                wait(act, s_cden, b)
                act.activation(ec, tl, ACT.Exp, scale=-1.0).then_inc(s_ec, 1)
                if more:
                    for r in range(FG):
                        exps(b + 1, r)
                if project_more:
                    projected(b + 2)

            act.wait_ge(dve_setup, len(DVE_SETUP))
            projected(0)
            for r in range(FG):
                exps(0, r)
            projected(1)
            attend(0, True, True, first=True)
            with act.Fori(1, B - 2) as b:
                attend(b, True, True)
            attend(B - 2, True, False)
            attend(B - 1, False, False)
            out_T(B - 1)
            out_x1(B - 1)

            def exp_pairs(t, a, h):
                hs, slot = 8 * t + h, h
                act.wait_ge(h_S, hs + 1)
                if h == 0:
                    act.wait_ge(t_top, t + 1)
                wait(act, h_w, hs - RING + 1)
                act.activation(E[slot], S[slot], ACT.Exp, bias=neg_max[a][:, h:h + 1]).then_inc(h_E, 1)

            def exp_top(t):
                act.wait_ge(t_top, t + 1)
                wait(act, t_zs, t)
                act.activation(etop[:, :, :], dtop[:, :, :], ACT.Exp).then_inc(t_ez, 1)

            def expert_inputs(t, a):
                act.wait_ge(t_Hp, 2 * t + 2)
                wait(act, t_P, t - 1)
                act.activation(G[a], banks[:, 0:2, :].rearrange("p c n -> p (c n)"),
                               ACT.Gelu_apprx_tanh).then_inc(t_G, 1)

            def weights_T(t):
                act.wait_ge(t_Tp, t + 1)
                wait(act, t_x2p, t)
                act.activation(PT[:, :], banks[:, 0:2, :].rearrange("p c n -> p (c n)"), ACT.Copy).then_inc(t_PT, 1)

            def squares(t, a):
                act.wait_ge(t_x2, t + 1)
                wait(act, t_ssq, t)
                act.activation(square[:, :], x2s[a][:, :], ACT.Square, accum_out=ssq[:, a:a + 1]).then_inc(t_ssq, 1)

            def x2_T(t, a, Gn):
                act.wait_ge(t_trp, t + 1)
                wait(act, e_h1, 8 * Gn)
                act.activation(x2T[:, P * a:P * a + P], bank(6, P, 2 * P), ACT.Copy).then_inc(t_x2T, 1)

            def hidden2(Gn, e):
                act.wait_ge(e_h2, 8 * Gn + e + 1)
                wait(act, e_y, 16 * Gn + e - 1)
                for n in range(2):
                    m = act.activation(H2[e % 2][:, n, :], bank(3, 256 * n, 256 * n + 256), ACT.Relu,
                                       bias=L("b2", 2 * e + n, 2 * e + n + 1))
                m.then_inc(e_r2, 1)

            def sum_T(Gn):
                act.wait_ge(g_cTp, Gn + 1)
                wait(act, e_hf, 16 * Gn)
                act.activation(cT[:, :], bank(7, 0, 256), ACT.Copy).then_inc(g_cT, 1)

            def gate1_exp(Gn):
                act.wait_ge(g_lg, Gn + 1)
                act.activation(lexp[:, :, :], lg[:, :, :], ACT.Exp).then_inc(g_exp1, 1)

            def gate2_exp(Gn):
                act.wait_ge(g_g2p, Gn + 1)
                act.activation(lexp[:, :, :].rearrange("p a e -> p (a e)"), bank(7, 0, 16), ACT.Exp,
                               scale=-1.0).then_inc(g_exp2, 1)

            def hidden1(Gn, e):
                act.wait_ge(e_h1, 8 * Gn + e + 1)
                wait(act, e_h2, 8 * Gn + e - 1)
                for n in range(2):
                    m = act.activation(H1[e % 2][:, n, :], bank(2, 256 * n, 256 * n + 256), ACT.Relu,
                                       bias=L("b1", 2 * e + n, 2 * e + n + 1))
                m.then_inc(e_r1, 1)

            def hidden_f(Gn, e):
                for b in range(2):
                    act.wait_ge(e_hf, 16 * Gn + 2 * e + b + 1)
                    if b == 0:
                        wait(act, e_y, 16 * Gn + 8 + e - 1)
                    for f in range(2 * b, 2 * b + 2):
                        m = act.activation(HF[e % 2][:, f, :], bank(2 + b, 256 * (f % 2), 256 * (f % 2) + 256),
                                           ACT.Gelu_apprx_tanh, bias=L("bf", 4 * e + f, 4 * e + f + 1))
                    m.then_inc(e_g, 1)

            act.wait_ge(dve_norm, len(NORM_DVE))
            act.wait_ge(ld_l, 48)
            expert_inputs(0, 0)
            exp_top(0)
            for h in range(4):
                exp_pairs(0, 0, h)

            EXPS = {4: [5], 5: [6, 7], 6: [8], 7: [9, 10], 8: [11, 12], 9: [13], 10: [14, 15], 11: [16, 17],
                    12: [18, 19]}

            def turn(g, peer, new, old, more=True):
                t, G1, G2 = 2 * g, g - 1, g - 2
                for s in range(16):
                    if s < 4 and old:
                        hidden_f(G2, s + 4)
                    if s == 1 and new:
                        weights_T(t - 1)
                    if s == 3 and new:
                        x2_T(t - 1, 1, G1)
                        squares(t - 1, 1)
                    if s == 4 and peer:
                        exp_pairs(t, 0, 4)
                    if s == 4 and new:
                        hidden1(G1, 0)
                    if s == 4 and peer:
                        exp_top(t + 1)
                    if 4 <= s < 11 and new:
                        hidden1(G1, s - 3)
                    if s == 5 and new:
                        gate1_exp(G1)
                    if s == 11 and more:
                        exp_top(t + 2)
                    if peer:
                        for h in EXPS.get(s, []):
                            if h < 16 or more:
                                exp_pairs(t + h // 8, h // 8 % 2, h % 8)
                    if 4 <= s < 12 and new:
                        hidden2(G1, s - 4)
                    if s == 9 and peer:
                        weights_T(t)
                    if s == 12 and peer:
                        x2_T(t, 0, g)
                        wait(act, g_msq, g)
                        squares(t, 0)
                    if s == 12 and new:
                        sum_T(G1)
                        gate2_exp(G1)
                    if s >= 12 and new:
                        hidden_f(G1, s - 12)
                    if s == 12 and peer:
                        expert_inputs(t + 1, 1)
                    if s == 14 and more:
                        expert_inputs(t + 2, 0)

            turn(0, True, False, False)
            turn(1, True, True, False)
            with act.Fori(2, NG - 1) as g:
                turn(g, True, True, True)
            turn(NG - 1, True, True, True, more=False)
            turn(NG, False, True, True, more=False)
            turn(NG + 1, False, False, True, more=False)

        @block.vector
        def _(v):
            def setup_done(name):
                v.wait_ge(dve_setup, DVE_SETUP.index(name) + 1)

            v.memset(small, 0.0).then_inc(dve_setup, 1)
            v.wait_ge(ld_a, 16)
            v.wait_ge(ld_c, 16)
            v.wait_ge(ld_r, 16)
            cs = C("csT").unsqueeze(2).broadcast_to([CD, B, NE])
            gg = C("ggW").unsqueeze(1).broadcast_to([CD, B, NE])
            v.tensor_tensor(gate_rhs[0:CD, :].rearrange("p (b o) -> p b o", b=B), cs, gg, ALU.mult).then_inc(dve_setup, 1)
            v.wait_ge(pe_setup, 1)
            v.tensor_scalar(hidb, bank(7, 0, B), A("bc1"), None, ALU.add).then_inc(dve_setup, 1)
            v.wait_ge(pe_setup, 3)
            v.tensor_tensor(field_a[0:B, :], banks[0:B, 1, 0:P], R("be2", B), ALU.add).then_inc(dve_setup, 1)
            setup_done("f2")
            v.bn_stats(small[0:B, 0:6], field_a[0:B, :]).then_inc(dve_setup, 1)
            setup_done("stats")
            v.bn_aggr(small[0:B, 6:8], small[0:B, 0:6]).then_inc(dve_setup, 1)
            setup_done("aggr")
            v.tensor_scalar(small[0:B, 8:9], small[0:B, 7:8], 1e-5, None, ALU.add).then_inc(dve_setup, 1)
            v.wait_ge(pool_setup, 5)
            v.tensor_scalar(field_b[0:B, :], field_a[0:B, :], small[0:B, 6:7], small[0:B, 9:10],
                            ALU.subtract, ALU.mult).then_inc(dve_setup, 1)
            setup_done("f3")
            v.tensor_tensor(field_a[0:B, :], field_b[0:B, :], R("ln_g", B), ALU.mult).then_inc(dve_setup, 1)
            setup_done("f4g")
            v.tensor_tensor(field_b[0:B, :], field_a[0:B, :], R("ln_b", B), ALU.add).then_inc(dve_setup, 1)
            v.wait_ge(pe_setup, PE_SETUP.index("fpT") + 1)
            v.tensor_copy(fpT, bank(0, 0, B)).then_inc(dve_setup, 1)
            v.wait_ge(pe_setup, PE_SETUP.index("field_scores") + 1)
            v.tensor_reduce(small[0:B, 10:11], banks[0:B, 6, 0:P], AX_X, ALU.max, negate=True).then_inc(dve_setup, 1)
            v.wait_ge(act_setup, 2)
            v.reciprocal(small[0:B, 12:13], small[0:B, 11:12]).then_inc(dve_setup, 1)
            setup_done("fa_recip")
            v.tensor_scalar(fa[0:B, :], field_a[0:B, :], small[0:B, 12:13], FIELD, ALU.mult, ALU.mult).then_inc(dve_setup, 1)
            v.wait_ge(pe_setup, PE_SETUP.index("faT") + 1)
            v.tensor_copy(fas, bank(1, 0, B)).then_inc(dve_setup, 1)
            v.tensor_tensor(gate_rows, R("wgb"), R("ggb"), ALU.add).then_inc(dve_setup, 1)
            setup_done("gate_rows")
            v.wait_ge(pe_setup, PE_SETUP.index("gate_bias") + 1)
            v.tensor_tensor(gate_bias[:, :, :], bank(7, P, 2 * P).rearrange("p (b o) -> p b o", b=B),
                            gate_rows.unsqueeze(1).broadcast_to([P, B, NE]), ALU.add).then_inc(dve_setup, 1)
            v.wait_ge(ld_l, 48)
            v.tensor_scalar(L("wgr"), L("wgr"), L("rms"), None, ALU.mult).then_inc(dve_setup, 1)

            quarter = lambda ap: ap.rearrange("p (g n) -> p g n", g=FG)

            def row_max(b, r):
                v.wait_ge(s_S, FG * b + r + 1)
                v.tensor_reduce(mx4[:, FG * r:FG * r + FG], quarter(bank(2 + r)), AX_X, ALU.max).then_inc(s_mx, 1)

            def minus_max(b, r):
                v.wait_ge(s_mx, FG * b + r + 1)
                wait(v, s_T, FG * (b - 1) + r + 1)
                v.tensor_tensor(quarter(D[r]), quarter(bank(2 + r)),
                                mx4[:, FG * r:FG * r + FG].unsqueeze(2).broadcast_to([P, FG, P]),
                                ALU.subtract).then_inc(s_D, 1)

            def shifted_scores(b):
                row_max(b, 0)
                row_max(b, 1)
                minus_max(b, 0)
                row_max(b, 2)
                minus_max(b, 1)
                row_max(b, 3)
                minus_max(b, 2)
                minus_max(b, 3)

            def attend(b, more):
                v.wait_ge(s_coh, b + 1)
                wait(v, s_ec, b)
                v.tensor_tensor(tl, bank(1, 0, NH), R("bc2"), ALU.add).then_inc(s_tl, 1)
                if more:
                    shifted_scores(b + 1)
                v.wait_ge(s_ec, b + 1)
                v.tensor_scalar(cden, ec, 1e-8 / (1 - FIELD), (1 + 1e-8) / (1 - FIELD), ALU.mult, ALU.add).then_inc(s_cden, 1)
                v.wait_ge(s_pv, FG * b + FG)
                v.wait_ge(s_cden, b + 1)
                o9 = bank(6, 0, 144).rearrange("p (h d) -> p h d", d=9)
                v.tensor_tensor(zden.unsqueeze(2), o9[:, :, HD:HD + 1], cden.unsqueeze(2), ALU.mult).then_inc(s_zd, 1)
                v.wait_ge(s_zd, b + 1)
                v.reciprocal(rz_att, zden).then_inc(s_rz, 1)
                v.wait_ge(s_rz, b + 1)
                v.tensor_tensor(o_n.rearrange("p (h d) -> p h d", d=HD), o9[:, :, 0:HD],
                                rz_att.unsqueeze(2).broadcast_to([P, NH, HD]), ALU.mult).then_inc(s_on, 1)
                v.wait_ge(s_on, b + 1)
                v.wait_ge(s_vs, b + 1)
                wait(v, s_oTp, b)
                wait(v, s_ostore, b)
                v.scalar_tensor_tensor(o_s, bank(6, 384, 512), col(fas, b), o_n, ALU.mult, ALU.add).then_inc(s_os, 1)

            v.wait_ge(pool_setup, 5)
            setup_done("wgr")
            shifted_scores(0)
            attend(0, True)
            with v.Fori(1, B - 1) as b:
                attend(b, True)
            attend(B - 1, False)

            def norm_done(name):
                v.wait_ge(dve_norm, NORM_DVE.index(name) + 1)

            v.wait_ge(s_x1, B)
            v.wait_ge(s_ostore, B)
            v.tensor_reduce(small[:, 16:17], o_sum, AX_X, ALU.add).then_inc(dve_norm, 1)
            norm_done("mean_col")
            v.tensor_scalar(mean_bc, ones, small[:, 16:17], 1.0 / TOK, ALU.mult, ALU.mult).then_inc(dve_norm, 1)
            v.tensor_reduce(small[:, 17:18], x1_sum, AX_X, ALU.add).then_inc(dve_norm, 1)
            norm_done("x1mean")
            v.tensor_scalar(x1neg, ones, small[:, 17:18], -1.0 / TOK, ALU.mult, ALU.mult).then_inc(dve_norm, 1)
            v.wait_ge(pe_norm, 1)
            v.tensor_tensor(o_c.rearrange("p (t n) -> p t n", t=B), o_all.rearrange("p (t n) -> p t n", t=B),
                            bank(0, 0, P).unsqueeze(1).broadcast_to([P, B, P]), ALU.subtract).then_inc(dve_norm, 1)
            v.wait_ge(pe_norm, 2)
            v.tensor_scalar(cov, bank(6, 0, P), 1.0 / TOK, None, ALU.mult).then_inc(dve_norm, 1)
            for c in range(4):
                v.wait_ge(pe_norm, NORM_PE.index("CU0") + c + 1)
                v.tensor_tensor(T[:, 512 * c:512 * c + 512], bank(2 + c), U[:, 512 * c:512 * c + 512],
                                ALU.mult).then_inc(dve_norm, 1)
            v.wait_ge(pe_norm, NORM_PE.index("var") + 1)
            v.tensor_scalar(small[:, 0:B], bank(7, 0, B), 1e-5, None, ALU.add).then_inc(dve_norm, 1)
            v.wait_ge(pool_norm, 1)
            v.tensor_tensor(scale_a, rstd, A("gamma"), ALU.mult).then_inc(dve_norm, 1)
            norm_done("scale")
            k3 = lambda ap: ap.rearrange("p (c k) -> p c k", k=NK)
            v.tensor_tensor(k3(ka), k3(A("keysT")), scale_a.unsqueeze(2).broadcast_to([P, 16, NK]), ALU.mult).then_inc(dve_norm, 1)
            v.tensor_tensor(k3(kb), k3(A("keysT")), A("beta").unsqueeze(2).broadcast_to([P, 16, NK]), ALU.mult).then_inc(dve_norm, 1)
            v.wait_ge(pe_norm, NORM_PE.index("weff") + 1)
            v.tensor_copy(weff[:, :], bank(1)).then_inc(dve_norm, 1)
            v.wait_ge(pe_norm, NORM_PE.index("sim_bias") + 1)
            v.tensor_copy(sim_bias[:, :], bank(5)).then_inc(dve_norm, 1)
            norm_done("sim_bias")

            def key_sums(t, a):
                v.wait_ge(t_simp, t + 1)
                wait(v, h_S, 8 * t - 8)
                v.tensor_tensor(sim[a][:, :, :].rearrange("p c k -> p (c k)"), bank(6), sim_bias[:, :],
                                ALU.add).then_inc(topk, 1)

            def top_keys_of(t, a):
                v.wait_ge(topk, 1)
                v.max(top_keys[:, 0, :], sim[a][:, 0, :]).then_inc(t_simr, 1)
                for c in range(1, 16):
                    m = v.max(top_keys[:, c, :], sim[a][:, c, :])
                m.then_inc(topk, 1)

            def pair_sums():
                v.wait_ge(topk, 2)
                v.tensor_tensor(pairs[:, :, :, :],
                                top_keys[:, 0:PH, :].unsqueeze(3).broadcast_to([P, PH, 8, 8]),
                                top_keys[:, PH:16, :].unsqueeze(2).broadcast_to([P, PH, 8, 8]), ALU.add).then_inc(topk, 1)

            def top_pairs(t, a):
                v.wait_ge(topk, 3)
                for h in range(PH):
                    m = v.max(top[a][:, h, :], pairs[:, h, :, :].rearrange("p a b -> p (a b)"))
                m.then_inc(topk, 1)
                v.wait_ge(topk, 4)
                v.sem_clear(topk)
                wait(v, h_E, 8 * t - 8)
                v.tensor_scalar(neg_max[a][:, :].unsqueeze(2), top[a][:, :, 0:1], -1.0, None, ALU.mult).then_inc(t_sim, 1)
                wait(v, t_ez, t)
                v.tensor_tensor(dtop[:, :, :], top[a][:, :, :], top[a][:, :, 0:1].broadcast_to([P, PH, 8]),
                                ALU.subtract).then_inc(t_top, 1)

            def top_sums(t, a):
                v.wait_ge(t_ez, t + 1)
                v.tensor_reduce(zsum[:, :], etop[:, :, :], AX_X, ALU.add).then_inc(t_zs, 1)
                v.wait_ge(t_zs, t + 1)
                v.reciprocal(rz[a][:, :], zsum[:, :]).then_inc(t_rz, 1)

            def mask(t, a, h):
                hs, slot = 8 * t + h, h
                v.wait_ge(h_E, hs + 1)
                v.scalar_tensor_tensor(E[slot], S[slot], top[a][:, h, 7:8], E[slot], ALU.is_ge, ALU.mult).then_inc(h_me, 1)

            def add_weights(t, a, h):
                hs, slot = 8 * t + h, h
                v.wait_ge(h_me, hs + 1)
                if h == 0:
                    v.wait_ge(t_rz, t + 1)
                    wait(v, t_Tp, t - 1)
                    v.tensor_scalar(W[a], E[slot], rz[a][:, 0:1], None, ALU.mult).then_inc(h_w, 1)
                else:
                    v.wait_ge(h_w, hs)
                    v.scalar_tensor_tensor(W[a], E[slot], rz[a][:, h:h + 1], W[a], ALU.mult, ALU.add).then_inc(h_w, 1)

            def add_peer(t, a):
                v.wait_ge(t_x2p, t + 1)
                wait(v, t_xst, t - 1)
                wait(v, t_ssq, t - 1)
                wait(v, t_trp, t - 1)
                v.tensor_tensor(x2s[a][:, :], bank(6, 0, P), tile_of(x_all, t), ALU.add).then_inc(t_x2, 1)

            def mean_square(Gn):
                v.wait_ge(t_ssq, 2 * Gn + 2)
                wait(v, g_rms, Gn)
                v.tensor_scalar(msq[:, :], ssq[:, :], 1.0 / P, 1e-6, ALU.mult, ALU.add).then_inc(g_msq, 1)

            def logits(Gn):
                v.wait_ge(g_rms, Gn + 1)
                v.wait_ge(g_g1p, Gn + 1)
                wait(v, g_exp1, Gn)
                for a in range(2):
                    m = v.scalar_tensor_tensor(lg[:, a, :], bank(7, 8 * a, 8 * a + 8), rms[:, a:a + 1],
                                               tile_of(gate_bias, 2 * Gn + a), ALU.mult, ALU.add)
                m.then_inc(gate, 1)

            def logit_max():
                v.wait_ge(gate, 1)
                v.tensor_reduce(lmax[:, :], lg[:, :, :], AX_X, ALU.max).then_inc(gate, 1)

            def minus_logit_max():
                v.wait_ge(gate, 2)
                v.tensor_tensor(lg[:, :, :], lg[:, :, :], lmax[:, :].unsqueeze(2).broadcast_to([P, 2, NE]),
                                ALU.subtract).then_inc(g_lg, 1)

            def exp_sum(Gn):
                v.wait_ge(g_exp1, Gn + 1)
                v.tensor_reduce(lsum[:, :], lexp[:, :, :], AX_X, ALU.add).then_inc(gate, 2)

            def exp_recip():
                v.wait_ge(gate, 4)
                v.reciprocal(lmax[:, :], lsum[:, :]).then_inc(gate, 1)

            def probabilities():
                v.wait_ge(gate, 5)
                v.tensor_tensor(prob[:, :, :], lexp[:, :, :], lmax[:, :].unsqueeze(2).broadcast_to([P, 2, NE]),
                                ALU.mult).then_inc(gate, 1)

            def sigmoid_den(Gn):
                v.wait_ge(g_exp2, Gn + 1)
                v.tensor_scalar(lg[:, :, :], lexp[:, :, :], 1.0, None, ALU.add).then_inc(gate, 5)

            def sigmoid():
                v.wait_ge(gate, 5)
                v.reciprocal(prob[:, :, :], lg[:, :, :]).then_inc(gate, 1)

            def two_best():
                v.wait_ge(gate, 6)
                for a in range(2):
                    m = v.max(best[:, a, :], prob[:, a, :])
                m.then_inc(gate, 1)

            def two_best_at():
                v.wait_ge(gate, 7)
                for a in range(2):
                    m = v.max_index(besti[:, a, :], best[:, a, :], prob[:, a, :])
                m.then_inc(gate, 1)

            def index_values():
                v.wait_ge(gate, 8)
                v.tensor_copy(bestf[:, :, :], besti[:, :, :]).then_inc(gate, 1)

            def picks(n):
                v.wait_ge(gate, 9)
                wait(v, g_cwTp, n)
                wait(v, e_acc, 8 * n)
                for a in range(2):
                    v.scalar_tensor_tensor(pick[:, a, :], iota8[:, :], bestf[:, a, 0:1], prob[:, a, :], ALU.is_equal, ALU.mult)
                for a in range(2):
                    m = v.scalar_tensor_tensor(cw[:, a, :], iota8[:, :], bestf[:, a, 1:2], prob[:, a, :], ALU.is_equal, ALU.mult)
                m.then_inc(gate, 1)

            def gate_weights():
                v.wait_ge(gate, 10)
                v.sem_clear(gate)
                v.tensor_tensor(cw[:, :, :], cw[:, :, :], pick[:, :, :], ALU.add).then_inc(g_cw, 1)

            def weights_T(n):
                v.wait_ge(g_cwTp, n + 1)
                wait(v, g_bias, n)
                v.tensor_copy(cwT[:, :], banks[0:NE, 7, 0:2 * P]).then_inc(g_cwT, 1)

            def add_bias(Gn, layer):
                dst = (acc, acc_f)[layer]
                v.wait_ge(g_bias, 2 * Gn + layer + 1)
                v.wait_ge(e_acc, 16 * Gn + 8 * layer + 5)
                v.tensor_tensor(dst[:, :, :], bank(7, 256, 512).rearrange("p (a n) -> p a n", a=2), dst[:, :, :],
                                ALU.add).then_inc(g_badd, 1)

            def add_expert(Gn, n):
                e, layer = n % 8, n // 8
                v.wait_ge(e_y, 16 * Gn + n + 1)
                if n == 0:
                    wait(v, g_cTp, Gn)
                if n == 8:
                    wait(v, g_out, 32 * Gn)
                    v.wait_ge(t_xst, 2 * Gn + 2)
                if e == 0:
                    v.wait_ge(g_cw, 2 * Gn + 1 + layer)
                elif e == 5:
                    v.wait_ge(g_badd, 2 * Gn + 1 + layer)
                else:
                    v.wait_ge(e_acc, 16 * Gn + n)
                dst = (acc, acc_f)[layer]
                for a in range(2):
                    y, w_ = bank(4 + n % 2, P * a, P * a + P), cw[:, a, e:e + 1]
                    if n == 0:
                        m = v.tensor_scalar(dst[:, a, :], y, w_, None, ALU.mult)
                    else:
                        base = tile_of(x_all, 2 * Gn + a) if n == 8 else dst[:, a, :]
                        m = v.scalar_tensor_tensor(dst[:, a, :], y, w_, base, ALU.mult, ALU.add)
                m.then_inc(e_acc, 1)

            key_sums(0, 0)
            top_keys_of(0, 0)
            pair_sums()
            top_pairs(0, 0)
            key_sums(1, 1)
            top_keys_of(1, 1)
            top_sums(0, 0)

            ADDS = {6: [0], 7: [1], 8: [2], 9: [3], 10: [4], 11: [5], 12: [7], 14: [8], 15: [9]}
            OLD_ADDS = {0: [10], 1: [11], 2: [12], 3: [13], 4: [14, 15]}

            def turn(g, peer, new, old, more=True):
                t, G1, G2 = 2 * g, g - 1, g - 2
                for s in range(16):
                    if s == 12:
                        if peer:
                            add_weights(t + 1, 1, 3)
                        if new:
                            add_expert(G1, 6)
                    if s == 4 and peer:
                        top_pairs(t + 1, 1)
                    if s == 4 and new:
                        mean_square(G1)
                    if peer:
                        mask(t + s // 8, s // 8, s % 8)
                    if s == 3 and peer:
                        pair_sums()
                    if s == 3 and new:
                        add_peer(t - 1, 1)
                    if s == 11 and peer:
                        add_peer(t, 0)
                    if new:
                        if s == 6:
                            probabilities()
                            two_best()
                        if s == 9:
                            weights_T(2 * G1)
                        if s == 11:
                            add_bias(G1, 0)
                        if s == 13:
                            sigmoid_den(G1)
                            sigmoid()
                        if s == 14:
                            index_values()
                            picks(2 * G1 + 1)
                    if s == 14 and more:
                        top_keys_of(t + 3, 1)
                    if s == 3 and old:
                        add_bias(G2, 1)
                    if peer and s > 0 and s != 12:
                        add_weights(t + (s - 1) // 8, (s - 1) // 8, (s - 1) % 8)
                    if new and s == 0:
                        add_weights(t - 1, 1, 7)
                    if new:
                        if s == 4:
                            logits(G1)
                            logit_max()
                            minus_logit_max()
                        if s == 5:
                            exp_sum(G1)
                            exp_recip()
                        if s == 6:
                            two_best_at()
                            index_values()
                            picks(2 * G1)
                            gate_weights()
                        if s == 13:
                            two_best()
                            two_best_at()
                        if s == 14:
                            gate_weights()
                    if s == 1 and old:
                        weights_T(2 * G2 + 1)
                    if old:
                        for n in OLD_ADDS.get(s, []):
                            add_expert(G2, n)
                    if new:
                        for n in ADDS.get(s, []):
                            add_expert(G1, n)
                    if more:
                        if s == 9:
                            key_sums(t + 2, 0)
                            top_keys_of(t + 2, 0)
                        if s == 10:
                            pair_sums()
                            top_pairs(t + 2, 0)
                        if s == 13:
                            top_sums(t + 2, 0)
                            key_sums(t + 3, 1)
                    if peer:
                        if s == 6:
                            top_sums(t + 1, 1)

            turn(0, True, False, False)
            turn(1, True, True, False)
            with v.Fori(2, NG - 1) as g:
                turn(g, True, True, True)
            turn(NG - 1, True, True, True, more=False)
            turn(NG, False, True, True, more=False)
            turn(NG + 1, False, False, True, more=False)


def kernel(**inputs):
    import numpy as _np
    import concourse.bacc as _bacc
    from concourse import mybir as _mybir
    from concourse.bass_utils import run_bass_kernel_spmd as _run

    i = {k: _np.asarray(v) for k, v in inputs.items()}
    c0, f0, c1, f1 = (lambda n, p=p: i[p + n] for p in ("L0_cond_", "L0_ffn_", "L1_cond_", "L1_ffn_"))
    f32 = _np.float32

    def side(parts, widths):
        return _np.concatenate([_np.reshape(parts[n], (-1, w)) for n, w in widths.items()], axis=1)

    WT = c0("Wqkv").T
    bqkv = c0("bqkv")
    pos = _np.arange(P, dtype=f32)
    inv = _np.power(f32(10000.0), _np.repeat(_np.arange(0, P, 2, dtype=f32) / f32(P), 2))
    pe = _np.sin(pos[:, None] / inv[None, :]).astype(f32)
    pA = side(dict(
        wqT=WT[:, 0:P], wkT=WT[:, P:2 * P], wvT=WT[:, 2 * P:], bq=bqkv[0:P], bk=bqkv[P:2 * P],
        head_of=_np.repeat(_np.eye(NH, dtype=f32), HD, axis=0),
        woT=c0("Wout").T, wo=c0("Wout"), wc1T=c0("Wc1")[:, :P].T, wc2T=c0("Wc2").T, we2T=c0("We2").T,
        peT=pe.T, ident=_np.eye(P, dtype=f32), bout=c0("bout"), bc1=c0("bc1"), be1=c0("be1"),
        gamma=f0("bn_gamma").reshape(16, P).T, beta=f0("bn_beta").reshape(16, P).T,
        keysT=f0("keys").transpose(3, 2, 0, 1)), COLS_A)
    pL = side(dict(
        b1=c1("b1").reshape(16, P).T, b2=c1("b2").reshape(16, P).T, bf=f1("b1").reshape(32, P).T,
        wgr=c1("wg_W"), rms=c1("rms_w"), wgf=f1("Wg")), COLS_L)
    pC = side(dict(wc1c=c0("Wc1")[:, P:].T, csT=i["cond_256"].T, we1T=c0("We1").T, ggW=c1("gg_W")), COLS_C)
    pR = side(dict(bv=bqkv[2 * P:], bc2=c0("bc2"), be2=c0("be2"), ln_g=c0("ln_g"), ln_b=c0("ln_b"),
                   wgb=c1("wg_b"), ggb=c1("gg_b")), COLS_R)
    p8 = side(dict(b3=c1("b3"), b2f=f1("b2")), COLS_8)
    x = i["x"]
    w_q = f0("w_q")
    arrays = dict(
        xtok=x, xT=x.reshape(TOK, P).T, pA=pA, pL=pL, pC=pC, pR=pR, p8=p8, wq=w_q,
        wqT=w_q.reshape(P, 16, P).transpose(2, 1, 0).reshape(P, 16 * P),
        down=f0("down_embed").T, up=f0("up_embed"), w1=c1("W1"), w2=c1("W2"), w3=c1("W3"),
        f1=f1("W1"), f2=f1("W2"))
    nc = _bacc.Bacc("TRN2", target_bir_lowering=False, num_devices=1)
    maps, args = {}, []
    for name, a in arrays.items():
        a = _np.ascontiguousarray(a)
        maps[f"in_{name}"] = a
        args.append(nc.dram_tensor(f"in_{name}", a.shape, _mybir.dt.from_np(a.dtype), kind="ExternalInput").ap())
    args.append(nc.dram_tensor("out_x", (B, P, P), F32, kind="ExternalOutput").ap())
    program(nc, *args)
    r = _run(nc, [maps], core_ids=[0])
    return r.results[0]["out_x"]
```

```python
from contextlib import ExitStack

import numpy as np

import concourse.bass as bass
from concourse import mybir

F32 = mybir.dt.float32
U32 = mybir.dt.uint32
ALU = mybir.AluOpType
ACT = mybir.ActivationFunctionType
AX_X = mybir.AxisListType.X

P = 128
B = 16
NH, HD = 16, 8
CD = 32
FG = 4
FIELD = 0.3 * 0.7
PH = 8
NK = 32
NE = 8
M1 = 256
FF = 512
NG = B // 2
TOK = B * P
RING = 8

COLS_A = dict(wqT=128, wkT=128, wvT=128, bq=1, bk=1, head_of=16, woT=128, wo=128, wc1T=128, wc2T=16,
              we2T=128, peT=128, ident=128, bout=1, bc1=1, be1=1, gamma=16, beta=16, keysT=512)
COLS_L = dict(b1=16, b2=16, bf=32, wgr=8, rms=1, wgf=8)
COLS_C = dict(wc1c=128, csT=16, we1T=128, ggW=8)
COLS_R = dict(bv=128, bc2=16, be2=128, ln_g=128, ln_b=128, wgb=8, ggb=8)
COLS_8 = dict(b3=128, b2f=128)


def columns(widths):
    at, n = {}, 0
    for name, w in widths.items():
        at[name] = (n, n + w)
        n += w
    return at, n


PE_SETUP = ["hid_bias", "field1", "gate_bias", "field2", "fpT", "U0", "field_scores", "U1", "faT", "U2", "U3"]
DVE_SETUP = ["consts", "gate_rhs", "hid_bias", "gate_rows", "gate_bias", "f2", "stats", "aggr", "vareps",
             "f3", "f4g", "f4b", "fpT", "field_max", "fa_recip", "fa", "faT"]
ACT_SETUP = ["field1", "U0", "field_exp", "U1", "U2", "U3"]
NORM_PE = ["mean_row", "cov", "CU0", "CU1", "var0", "CU2", "var1", "CU3", "var2", "var3", "weff0", "weff1",
           "sim_bias"]
NORM_DVE = ["mean_col", "mean_bc", "centred0", "centred1", "centred2", "centred3", "x1mean", "x1neg", "kb", "wgr",
            "cov", "T0", "T1", "vareps0", "T2", "vareps1", "T3", "vareps2", "vareps3",
            "scale0", "ka0", "scale1", "ka1", "scale2", "ka2", "scale3", "ka3", "weff1", "sim_bias"]


def program(nc, xtok, xT, pA, pL, pC, pR, p8, wq, wqT, down, up, w1, w2, w3, f1, f2, out):
    A_AT, A_N = columns(COLS_A)
    L_AT, L_N = columns(COLS_L)
    C_AT, C_N = columns(COLS_C)
    R_AT, R_N = columns(COLS_R)
    E_AT, E_N = columns(COLS_8)
    ds = bass.ds

    with ExitStack() as ctx:
        def sb(name, shape, dt=F32):
            return ctx.enter_context(nc.sbuf_tensor(name, shape, dt))

        def sem(name):
            return ctx.enter_context(nc.semaphore(name))

        x_all = sb("x_all", [P, B, P])
        x1T_all = sb("x1T_all", [P, TOK])
        downT = sb("downT", [P, NK * NK])
        up_sb = sb("up_sb", [P, PH, P])
        w1_sb = sb("w1_sb", [P, NE, M1])
        w2_sb = sb("w2_sb", [P, NE, 2, M1])
        w3_sb = sb("w3_sb", [P, NE, 2, P])
        f1_sb = sb("f1_sb", [P, NE, FF])
        f2_sb = sb("f2_sb", [P, NE, 4, P])
        lpack = sb("lpack", [P, L_N])
        epack = sb("epack", [NE, E_N])
        ident = sb("ident", [P, P])
        weff = sb("weff", [P, 512])
        sim_bias = sb("sim_bias", [P, 512])
        gate_bias = sb("gate_bias", [P, B, NE])
        iota8 = sb("iota8", [P, NE])
        mhalf = sb("mhalf", [P, B])

        def L(name, a=0, b=None):
            lo, hi = L_AT[name]
            return lpack[:, lo + a:hi if b is None else lo + b]

        region = sb("region", [P, 2 * RING, 1024])
        flat = region[:, :, :].rearrange("p a n -> p (a n)")
        used = [0]

        def part(n):
            used[0] += n
            assert used[0] <= 2 * RING * 1024
            return flat[:, used[0] - n:used[0]]

        wq_sb = part(2048)
        wqT_sb = part(2048)
        U = part(2048)
        o_all = part(TOK)
        qT, kT = part(P), part(P)
        k_heads = part(2048)
        apack = part(A_N)
        v_aug = part(NH * 9)
        xTs, thT, o_s, oT = part(P), part(P), part(P), part(P)
        cpack = part(C_N)
        rows = part(R_N)
        gate_rhs, gate_rows, ones = part(P), part(NE), part(P)
        hidb, fas = part(B), part(B)
        mx4 = part(16)
        tl, ec, cden, zden, rz_att = part(NH), part(NH), part(NH), part(NH), part(NH)
        o_n = part(P)
        v_stage = part(P)
        field_a, field_b, fpT, fa = part(P), part(P), part(B), part(P)
        small = part(32)
        o_sum, x1_sum = part(B), part(B)
        mean_bc, x1neg = part(P), part(P)
        cov = part(P)
        rstd, scale_a = part(B), part(B)
        ka, kb = k_heads[:, 0:512], k_heads[:, 512:1024]

        def A(name, a=0, b=None):
            lo, hi = A_AT[name]
            return apack[:, lo + a:hi if b is None else lo + b]

        def C(name):
            lo, hi = C_AT[name]
            return cpack[0:CD, lo:hi]

        def R(name, rows_=P):
            lo, hi = R_AT[name]
            return rows[0:rows_, lo:hi]

        S = [region[:, n, :] for n in range(RING)]
        E = [region[:, RING + n, :] for n in range(RING)]

        x1s = [sb(f"x1s{a}", [P, P]) for a in range(2)]
        sim = [sb(f"sim{a}", [P, 16, NK]) for a in range(2)]
        top_keys = sb("top_keys", [P, 16, 8])
        pairs = sb("pairs", [P, PH, 8, 8])
        top = [sb(f"top{a}", [P, PH, 8]) for a in range(2)]
        neg_max = [sb(f"neg_max{a}", [P, PH]) for a in range(2)]
        dtop = sb("dtop", [P, PH, 8])
        etop = sb("etop", [P, PH, 8])
        zsum = sb("zsum", [P, PH])
        rz = [sb(f"rz{a}", [P, PH]) for a in range(2)]
        W_both = sb("W_both", [P, 2048])
        G_both = sb("G_both", [P, 2048])
        W = [W_both[:, 1024 * a:1024 * a + 1024] for a in range(2)]
        G = [G_both[:, 1024 * a:1024 * a + 1024] for a in range(2)]
        D = [W_both[:, 512 * r:512 * r + 512] for r in range(FG)]
        ET = [G_both[:, 512 * r:512 * r + 512] for r in range(FG)]
        o_c, T = W_both[:, :], G_both[:, :]
        PT = sb("PT", [P, 1024])
        x2s = [sb(f"x2s{a}", [P, P]) for a in range(2)]
        x2T = sb("x2T", [P, 2 * P])
        square = sb("square", [P, P])
        ssq = sb("ssq", [P, 2])
        msq = sb("msq", [P, 2])
        rms = sb("rms", [P, 2])
        HF = [sb(f"HF_{n}", [P, 4, 256]) for n in range(2)]
        H1 = [HF[0][:, 2 * n:2 * n + 2, :] for n in range(2)]
        H2 = [sb(f"H2_{n}", [P, 2, 256]) for n in range(2)]
        acc = sb("acc", [P, 2, P])
        cT = sb("cT", [P, 2 * P])
        acc_f = sb("acc_f", [P, 2, P])
        lg = sb("lg", [P, 2, NE])
        lmax = sb("lmax", [P, 2])
        lexp = sb("lexp", [P, 2, NE])
        lsum = sb("lsum", [P, 2])
        prob = sb("prob", [P, 2, NE])
        best = sb("best", [P, 2, 8])
        besti = sb("besti", [P, 2, 8], U32)
        bestf = sb("bestf", [P, 2, 8])
        pick = sb("pick", [P, 2, NE])
        cw = sb("cw", [P, 2, NE])
        cwT = sb("cwT", [NE, 2 * P])
        unused = sb("unused", [P, 1])

        banks = ctx.enter_context(nc.psum_tensor("banks", [P, 8, 512], F32))

        def bank(n, a=0, b=512):
            return banks[:, n, a:b]

        ld_a, ld_c, ld_r, ld_x0, ld_x, ld_wq, ld_wqT = (
            sem("ld_" + n) for n in ("a", "c", "r", "x0", "x", "wq", "wqT"))
        ld_w, ld_l = sem("ld_w"), sem("ld_l")
        pe_setup, dve_setup, act_setup, pool_setup = (sem(n + "_setup") for n in ("pe", "dve", "act", "pool"))
        pe_norm, dve_norm, pool_norm, act_norm = (sem(n + "_norm") for n in ("pe", "dve", "pool", "act"))
        s_x = sem("s_x")
        s_qk, s_proj = sem("s_qk"), sem("s_proj")
        s_q, s_kh = sem("s_q"), sem("s_kh")
        s_vst, s_v, s_vs = sem("s_vst"), sem("s_v"), sem("s_vs")
        s_tanh, s_coh, s_tl = sem("s_tanh"), sem("s_coh"), sem("s_tl")
        s_ec, s_cden = sem("s_ec"), sem("s_cden")
        s_S, s_mx, s_D, s_E, s_T, s_ET, s_pv = (sem("att_" + n) for n in ("S", "mx", "D", "E", "T", "ET", "pv"))
        s_zd, s_rz, s_on, s_os, s_ostore = sem("s_zd"), sem("s_rzatt"), sem("s_on"), sem("s_os"), sem("s_ostore")
        s_oTp, s_oT, s_x1p, s_x1 = sem("s_oTp"), sem("s_oT"), sem("s_x1p"), sem("s_x1")

        t_x1s, t_simp, t_simr, t_sim = sem("t_x1s"), sem("t_simp"), sem("t_simr"), sem("t_sim")
        topk = sem("topk")
        t_top, t_ez, t_zs, t_rz = (sem("t_" + n) for n in ("top", "ez", "zs", "rz"))
        t_Hp, t_G = sem("t_Hp"), sem("t_G")
        t_P, t_Tp, t_PT, t_x2p, t_x2, t_xst, t_ssq, t_trp, t_x2T = (
            sem("t_" + n) for n in ("P", "Tp", "PT", "x2p", "x2", "xst", "ssq", "trp", "x2T"))
        h_S, h_E, h_me, h_w = sem("h_S"), sem("h_E"), sem("h_me"), sem("h_w")
        e_h1, e_r1, e_h2, e_r2, e_hf, e_g = (sem("e_" + n) for n in ("h1", "r1", "h2", "r2", "hf", "g"))
        e_y, e_acc = sem("e_y"), sem("e_acc")
        g_msq, g_rms, g_g1p, g_lg, g_exp1, g_g2p, g_exp2 = (
            sem("g_" + n) for n in ("msq", "rms", "g1p", "lg", "exp1", "g2p", "exp2"))
        gate = sem("gate")
        g_cw, g_cwTp, g_cwT, g_bias, g_badd, g_cTp, g_cT = (
            sem("g_" + n) for n in ("cw", "cwTp", "cwT", "bias", "badd", "cTp", "cT"))
        tables = sem("tables")
        g_out = sem("g_out")

        def wait(eng, s, value):
            if not isinstance(value, int) or value > 0:
                eng.wait_ge(s, value)

        def col(ap, i):
            return ap[:, ds(i, 1)] if not isinstance(i, int) else ap[:, i:i + 1]

        def cols(ap, i, n=P):
            return ap[:, ds(i * n, n)] if not isinstance(i, int) else ap[:, i * n:(i + 1) * n]

        def tile_of(ap, t):
            if isinstance(t, int):
                return ap[:, t, :]
            return ap[:, ds(t, 1), :].rearrange("p a n -> p (a n)")

        block = ctx.enter_context(nc.Block())

        @block.sync
        def _(sp):
            sp.dma_start(apack, pA).then_inc(ld_a, 16)
            sp.dma_start(cpack[0:CD, :], pC).then_inc(ld_c, 16)
            sp.dma_start(x1T_all[:, 0:4 * P], xT[:, 0:4 * P]).then_inc(ld_x0, 16)
            sp.dma_start(rows, pR.broadcast_to([P, R_N])).then_inc(ld_r, 16)
            sp.dma_start(x1T_all[:, 4 * P:TOK], xT[:, 4 * P:TOK]).then_inc(ld_x, 16)
            sp.dma_start(lpack[:, :], pL).then_inc(ld_l, 16)
            sp.dma_start(ident[:, :], pA[:, A_AT["ident"][0]:A_AT["ident"][1]]).then_inc(ld_l, 16)
            sp.dma_start(epack[:, :], p8).then_inc(ld_l, 16)
            sp.dma_start(wq_sb, wq).then_inc(ld_wq, 16)
            sp.dma_start(wqT_sb, wqT).then_inc(ld_wqT, 16)
            for dst, src in ((downT[:, :], down), (x_all[:, :, :], xtok.rearrange("b s e -> s b e")),
                             (up_sb[:, :, :], up.rearrange("(c p) d -> p c d", p=P)),
                             (w1_sb[:, :, :], w1.rearrange("e h m -> h e m")),
                             (w2_sb[:, :, :, :].rearrange("p e c n -> p (e c) n"),
                              w2.rearrange("e (c p) n -> p (e c) n", p=P)),
                             (w3_sb[:, :, :, :].rearrange("p e c n -> p (e c) n"),
                              w3.rearrange("e (c p) n -> p (e c) n", p=P)),
                             (f1_sb[:, :, :], f1.rearrange("e d f -> d e f")),
                             (f2_sb[:, :, :, :].rearrange("p e c n -> p (e c) n"),
                              f2.rearrange("e (c p) n -> p (e c) n", p=P))):
                sp.dma_start(dst, src).then_inc(ld_w, 16)

            def store(Gn):
                sp.wait_ge(e_acc, 16 * Gn + 16)
                for a in range(2):
                    sp.dma_start(out[ds(2 * Gn + a, 1), :, :].rearrange("a s e -> s (a e)"),
                                 acc_f[:, a, :]).then_inc(g_out, 16)

            with sp.Fori(0, NG) as Gn:
                store(Gn)
            sp.wait_ge(g_out, 32 * NG)

        @block.gpsimd
        def _(pool):
            pool.memset(mhalf[:, :], -0.5).then_inc(pool_setup, 1)
            pool.memset(ones, 1.0).then_inc(pool_setup, 1)
            pool.memset(v_aug, 1.0).then_inc(pool_setup, 1)
            pool.iota(iota8[:, :], [[1, NE]], base=0, channel_multiplier=0,
                      allow_small_or_imprecise_dtypes=True).then_inc(pool_setup, 1)
            pool.wait_ge(ld_x0, 16)
            pool.tensor_copy(xTs, cols(x1T_all, 0)).then_inc(s_x, 1)
            pool.wait_ge(pool_setup, 4)
            pool.wait_ge(dve_setup, DVE_SETUP.index("vareps") + 1)
            pool.tensor_tensor(small[0:B, 9:10], small[0:B, 8:9], mhalf[0:B, 0:1], ALU.pow).then_inc(pool_setup, 1)
            heads = lambda ap: ap.rearrange("p (h d) -> p h d", h=NH)

            def values(b):
                pool.wait_ge(s_vst, b + 1)
                wait(pool, s_pv, FG * b)
                wait(pool, s_vs, b)
                pool.tensor_tensor(heads(v_aug)[:, :, 0:HD], heads(v_stage), heads(R("bv")), ALU.add).then_inc(s_v, 1)

            def keep_output(b):
                pool.wait_ge(s_os, b + 1)
                pool.tensor_copy(cols(o_all, b), o_s).then_inc(s_ostore, 1)

            def stage_x(b):
                wait(pool, s_proj, b)
                pool.tensor_copy(xTs, cols(x1T_all, b)).then_inc(s_x, 1)

            def head_keys(b):
                pool.wait_ge(s_q, b + 1)
                for r in range(FG):
                    wait(pool, s_S, FG * (b - 1) + r + 1)
                    pool.tensor_tensor(k_heads[:, 512 * r:512 * r + 512].rearrange("p (g n) -> p g n", g=FG),
                                       kT.unsqueeze(1).broadcast_to([P, FG, P]),
                                       A("head_of", FG * r, FG * r + FG).unsqueeze(2).broadcast_to([P, FG, P]),
                                       ALU.mult).then_inc(s_kh, 1)

            def stage_x1(t, a):
                wait(pool, t_Hp, 2 * t - 2)
                pool.tensor_copy(x1s[a][:, :], cols(x1T_all, t)).then_inc(t_x1s, 1)

            pool.wait_ge(ld_x, 16)
            pool.wait_ge(ld_r, 16)
            pool.wait_ge(ld_a, 16)
            head_keys(0)
            values(0)
            stage_x(1)
            head_keys(1)
            stage_x(2)

            def attend(b, more):
                values(b + 1)
                head_keys(b + 2)
                keep_output(b)
                if more:
                    stage_x(b + 3)

            attend(0, True)
            with pool.Fori(1, B - 3) as b:
                attend(b, True)
            attend(B - 3, False)
            pool.wait_ge(s_x1, 2)
            stage_x1(0, 0)
            stage_x1(1, 1)
            values(B - 1)
            keep_output(B - 2)
            keep_output(B - 1)

            def pair_scores(t, a, h):
                hs = 8 * t + h
                if h == 0:
                    pool.wait_ge(t_simr, t + 1)
                wait(pool, h_me, hs - RING + 1)
                pool.tensor_tensor(
                    S[h].rearrange("p (i j) -> p i j", i=NK),
                    sim[a][:, h, :].unsqueeze(2).broadcast_to([P, NK, NK]),
                    sim[a][:, PH + h, :].unsqueeze(1).broadcast_to([P, NK, NK]),
                    ALU.add).then_inc(h_S, 1)

            def weigh(t, a):
                pool.wait_ge(h_w, 8 * t + 8)
                pool.wait_ge(t_G, t + 1)
                pool.tensor_tensor(W[a], W[a], G[a], ALU.mult).then_inc(t_P, 1)

            def keep_x2(t, a):
                pool.wait_ge(t_x2, t + 1)
                pool.tensor_copy(tile_of(x_all, t), x2s[a][:, :]).then_inc(t_xst, 1)

            for c in range(4):
                pool.wait_ge(dve_norm, NORM_DVE.index(f"vareps{c}") + 1)
                pool.tensor_tensor(rstd[:, 4 * c:4 * c + 4], small[:, 4 * c:4 * c + 4], mhalf[:, 0:4],
                                   ALU.pow).then_inc(pool_norm, 1)

            def turn(g, peer, new, more=True):
                t = 2 * g
                if peer and new:
                    pair_scores(t, 0, 7)
                if new:
                    weigh(t - 1, 1)
                if more:
                    stage_x1(t + 2, 0)
                if new:
                    keep_x2(t - 1, 1)
                    pool.wait_ge(g_msq, g)
                    pool.tensor_tensor(rms[:, :], msq[:, :], mhalf[:, 0:2], ALU.pow).then_inc(g_rms, 1)
                if not peer:
                    return
                for h in range(8):
                    pair_scores(t + 1, 1, h)
                weigh(t, 0)
                if more:
                    pair_scores(t + 2, 0, 0)
                    pair_scores(t + 2, 0, 1)
                keep_x2(t, 0)
                if more:
                    for h in range(2, 5):
                        pair_scores(t + 2, 0, h)
                    stage_x1(t + 3, 1)
                    for h in range(5, 7):
                        pair_scores(t + 2, 0, h)

            for h in range(8):
                pair_scores(0, 0, h)
            turn(0, True, False)
            with pool.Fori(1, NG - 1) as g:
                turn(g, True, True)
            turn(NG - 1, True, True, more=False)
            turn(NG, False, True, more=False)

        @block.tensor
        def _(pe):
            def mm(o, l, r, start=True, stop=True):
                return pe.matmul(o, l, r, start=start, stop=stop)

            pe.wait_ge(ld_a, 16)
            pe.wait_ge(ld_c, 16)
            pe.wait_ge(pool_setup, 4)
            mm(bank(7, 0, B), C("wc1c"), C("csT")).then_inc(pe_setup, 1)
            mm(bank(6, 0, B), C("we1T"), C("csT")).then_inc(pe_setup, 1)
            pe.wait_ge(dve_setup, DVE_SETUP.index("gate_rhs") + 1)
            mm(bank(5, 0, P), ones[0:CD, :], gate_rhs[0:CD, :]).then_inc(pe_setup, 1)
            pe.wait_ge(act_setup, 1)
            mm(banks[0:B, 1, 0:P], thT[:, 0:B], A("we2T")).then_inc(pe_setup, 1)

            def project(b):
                pe.wait_ge(s_x, b + 1)
                wait(pe, s_q, b)
                mm(bank(0, 0, P), A("wqT"), xTs)
                mm(bank(0, P, 2 * P), A("wkT"), xTs).then_inc(s_qk, 1)
                wait(pe, s_tanh, b)
                mm(bank(7, 0, P), xTs, A("wvT"))
                mm(bank(7, P, 2 * P), A("wc1T"), xTs).then_inc(s_proj, 1)

            def coherence(b):
                pe.wait_ge(s_tanh, b + 1)
                wait(pe, s_tl, b)
                mm(bank(1, 0, NH), thT, A("wc2T")).then_inc(s_coh, 1)

            def scores(b, r):
                pe.wait_ge(s_q, b + 1)
                pe.wait_ge(s_kh, FG * b + r + 1)
                wait(pe, s_ET, FG * (b - 1) + r + 1)
                mm(bank(2 + r), qT, k_heads[:, 512 * r:512 * r + 512]).then_inc(s_S, 1)

            def transposes(b, r):
                pe.wait_ge(s_E, FG * b + r + 1)
                for g in range(FG):
                    m = pe.transpose(banks[:, 2 + r, P * g:P * g + P], D[r][:, P * g:P * g + P], A("ident"))
                m.then_inc(s_T, 1)

            def values(b, r):
                pe.wait_ge(s_ET, FG * b + r + 1)
                for g in range(FG):
                    h = FG * r + g
                    m = mm(bank(6, 9 * h, 9 * h + 9), ET[r][:, P * g:P * g + P], v_aug[:, 9 * h:9 * h + 9])
                m.then_inc(s_pv, 1)

            def out_T(b):
                pe.wait_ge(s_os, b + 1)
                pe.transpose(bank(6, 144, 272), o_s, A("ident")).then_inc(s_oTp, 1)

            def out_proj(b):
                pe.wait_ge(s_oT, b + 1)
                mm(bank(6, 144, 272), A("woT"), oT).then_inc(s_x1p, 1)

            def out_query(c, to):
                mm(bank(to), A("wo"), wq_sb[:, 512 * c:512 * c + 512]).then_inc(pe_setup, 1)

            def first_inputs(c):
                if c == 0:
                    pe.wait_ge(ld_w, 16 * 8)
                    pe.wait_ge(ld_l, 48)
                    pe.wait_ge(t_x1s, 1)
                    pe.wait_ge(s_q, B)
                else:
                    pe.wait_ge(s_tl, B)
                mm(bank(c), x1s[0][:, :], downT[:, 512 * c:512 * c + 512]).then_inc(t_Hp, 1)

            def attend(b, more, project_more, first=False):
                transposes(b, 0)
                transposes(b, 1)
                if not more:
                    first_inputs(0)
                if not first:
                    out_T(b - 1)
                transposes(b, 2)
                if first:
                    pe.wait_ge(s_tl, 1)
                    out_query(2, 1)
                transposes(b, 3)
                if first:
                    pe.wait_ge(s_q, 2)
                    out_query(3, 0)
                else:
                    out_proj(b - 1)
                if more:
                    scores(b + 1, 0)
                else:
                    first_inputs(1)
                pe.wait_ge(s_v, b + 1)
                wait(pe, s_x1, b)
                mm(bank(6, 384, 512), ones, v_aug.rearrange("p (h d) -> p h d", d=9)[:, :, 0:HD]).then_inc(s_vs, 1)
                for r in range(FG):
                    values(b, r)
                    if more and r < FG - 1:
                        scores(b + 1, r + 1)
                if first:
                    pe.wait_ge(act_setup, len(ACT_SETUP))
                if more:
                    coherence(b + 1)
                if project_more:
                    project(b + 2)

            pe.wait_ge(dve_setup, DVE_SETUP.index("hid_bias") + 1)
            project(0)
            pe.wait_ge(dve_setup, DVE_SETUP.index("f4b") + 1)
            pe.transpose(bank(1, 0, B), field_b[0:B, :], A("ident")[0:B, 0:B]).then_inc(pe_setup, 1)
            pe.wait_ge(ld_wq, 16)
            out_query(0, 2)
            pe.wait_ge(dve_setup, DVE_SETUP.index("fpT") + 1)
            mm(banks[0:B, 6, 0:P], fpT, A("peT")).then_inc(pe_setup, 1)
            out_query(1, 3)
            pe.wait_ge(dve_setup, DVE_SETUP.index("fa") + 1)
            pe.transpose(bank(1, 0, B), fa[0:B, :], A("ident")[0:B, 0:B]).then_inc(pe_setup, 1)
            for r in range(FG):
                if r < 2:
                    pe.wait_ge(act_setup, ACT_SETUP.index(f"U{r}") + 1)
                scores(0, r)
            pe.wait_ge(dve_setup, len(DVE_SETUP))
            coherence(0)
            project(1)
            attend(0, True, True, first=True)
            with pe.Fori(1, B - 2) as b:
                attend(b, True, True)
            attend(B - 2, True, False)
            attend(B - 1, False, False)
            out_T(B - 1)
            out_proj(B - 1)

            def wait_norm(name):
                pe.wait_ge(dve_norm, NORM_DVE.index(name) + 1)

            def cov_U(c):
                mm(bank(2 + c), cov, U[:, 512 * c:512 * c + 512]).then_inc(pe_norm, 1)

            def variance(c):
                wait_norm(f"T{c}")
                for k in range(4):
                    m = mm(bank(2 + c, k, k + 1), T[:, P * (4 * c + k):P * (4 * c + k + 1)], ones[:, 0:1])
                m.then_inc(pe_norm, 1)

            def folded_keys(c):
                wait_norm(f"ka{c}")
                for k in range(4 * c, 4 * c + 4):
                    m = mm(bank(2 + c // 2, NK * (k % 8), NK * (k % 8) + NK), wqT_sb[:, P * k:P * k + P],
                           ka[:, NK * k:NK * k + NK])
                if c % 2 == 1:
                    m.then_inc(pe_norm, 1)

            wait_norm("mean_bc")
            mm(bank(7, 0, P), mean_bc, A("ident")).then_inc(pe_norm, 1)
            pe.wait_ge(s_x1, B)
            for t in range(B):
                if t % 4 == 0:
                    wait_norm(f"centred{t // 4}")
                m = mm(bank(6, 0, P), o_c[:, P * t:P * t + P], o_c[:, P * t:P * t + P],
                       start=(t == 0), stop=(t == B - 1))
            m.then_inc(pe_norm, 1)
            wait_norm("cov")
            cov_U(0)
            cov_U(1)
            variance(0)
            cov_U(2)
            variance(1)
            cov_U(3)
            variance(2)
            mm(bank(7), ones, kb, start=True, stop=False)
            variance(3)
            pe.wait_ge(ld_wqT, 16)
            for c in range(4):
                folded_keys(c)
            pe.wait_ge(act_norm, 1)
            wait_norm("weff1")
            mm(bank(7), x1neg, weff[:, :], start=False, stop=True).then_inc(pe_norm, 1)

            def key_scores(t, a):
                pe.wait_ge(t_x1s, t + 1)
                wait(pe, t_simr, t)
                wait(pe, t_x2T, t - 2)
                mm(bank(6), x1s[a][:, :], weff[:, :]).then_inc(t_simp, 1)

            def expert_inputs(t, a, c):
                if c == 0:
                    wait(pe, t_G, t)
                    wait(pe, t_PT, t - 1)
                mm(bank(c), x1s[a][:, :], downT[:, 512 * c:512 * c + 512]).then_inc(t_Hp, 1)

            def weights_T(t, a):
                pe.wait_ge(t_P, t + 1)
                if a == 1:
                    pe.wait_ge(t_G, min(t + 2, B) if isinstance(t, int) else t + 2)
                wait(pe, t_PT, t)
                for c in range(8):
                    m = pe.transpose(bank(c // 4, P * (c % 4), P * (c % 4) + P), W[a][:, P * c:P * c + P], ident[:, :])
                m.then_inc(t_Tp, 1)

            def peer_out(t):
                pe.wait_ge(t_PT, t + 1)
                wait(pe, t_x2T, t)
                wait(pe, t_simr, min(t + 3, B) if isinstance(t, int) else t + 3)
                for c in range(8):
                    m = mm(bank(6, 0, P), PT[:, P * c:P * c + P], up_sb[:, c, :], start=(c == 0), stop=(c == 7))
                m.then_inc(t_x2p, 1)

            def x2_T(t, a):
                pe.wait_ge(t_x2, t + 1)
                pe.transpose(bank(6, P, 2 * P), x2s[a][:, :], ident[:, :]).then_inc(t_trp, 1)

            def gate1(Gn):
                pe.wait_ge(t_x2T, 2 * Gn + 2)
                wait(pe, g_badd, 2 * Gn)
                for a in range(2):
                    m = mm(bank(7, 8 * a, 8 * a + 8), x2T[:, P * a:P * a + P], L("wgr"))
                m.then_inc(g_g1p, 1)

            def gate2(Gn):
                pe.wait_ge(g_cT, Gn + 1)
                for a in range(2):
                    m = mm(bank(7, 8 * a, 8 * a + 8), cT[:, P * a:P * a + P], L("wgf"))
                m.then_inc(g_g2p, 1)

            def weights_cwT(n):
                pe.wait_ge(g_cw, n + 1)
                for a in range(2):
                    m = pe.transpose(banks[0:NE, 7, P * a:P * a + P], cw[:, a, :], ident[:, :])
                m.then_inc(g_cwTp, 1)

            def weighted_bias(n, name):
                lo, hi = E_AT[name]
                pe.wait_ge(g_cwT, n + 1)
                for a in range(2):
                    m = mm(bank(7, 256 + P * a, 384 + P * a), cwT[:, P * a:P * a + P], epack[:, lo:hi])
                m.then_inc(g_bias, 1)

            def hidden1(Gn, e):
                if e == 0:
                    pe.wait_ge(t_x2T, 2 * Gn + 2)
                    wait(pe, e_g, 16 * Gn)
                wait(pe, e_r1, 8 * Gn + e)
                for n in range(2):
                    m = mm(bank(2, 256 * n, 256 * n + 256), w1_sb[:, e, P * n:P * n + P], x2T[:, :])
                m.then_inc(e_h1, 1)

            def hidden2(Gn, e):
                pe.wait_ge(e_r1, 8 * Gn + e + 1)
                wait(pe, e_r2, 8 * Gn + e)
                for n in range(2):
                    for k in range(2):
                        m = mm(bank(3, 256 * n, 256 * n + 256), w2_sb[:, e, k, P * n:P * n + P], H1[e % 2][:, k, :],
                               start=(k == 0), stop=(k == 1))
                m.then_inc(e_h2, 1)

            def outputs(Gn, n, weights, hidden, e, parts):
                wait(pe, e_acc, 16 * Gn + n - 1)
                for a in range(2):
                    for c in range(parts):
                        m = mm(bank(4 + n % 2, P * a, P * a + P),
                               hidden[:, c, P * a:P * a + P], weights[:, e, c, :],
                               start=(c == 0), stop=(c == parts - 1))
                m.then_inc(e_y, 1)

            def hidden_f(Gn, e):
                for b in range(2):
                    if e == 0:
                        pe.wait_ge((e_r1, e_r2)[b], 8 * Gn + 8)
                    else:
                        pe.wait_ge(e_g, 16 * Gn + 2 * e - 1 + b)
                    for f in range(2 * b, 2 * b + 2):
                        m = mm(bank(2 + b, 256 * (f % 2), 256 * (f % 2) + 256), f1_sb[:, e, P * f:P * f + P], cT[:, :])
                    m.then_inc(e_hf, 1)

            def sum_T(Gn):
                pe.wait_ge(e_acc, 16 * Gn + 8)
                for a in range(2):
                    m = pe.transpose(bank(7, P * a, P * a + P), acc[:, a, :], ident[:, :])
                m.then_inc(g_cTp, 1)

            def outputs1(Gn, e):
                pe.wait_ge(e_r2, 8 * Gn + e + 1)
                outputs(Gn, e, w3_sb, H2[e % 2], e, 2)

            def outputs2(Gn, e):
                pe.wait_ge(e_g, 16 * Gn + 2 * e + 2)
                outputs(Gn, 8 + e, f2_sb, HF[e % 2], e, 4)

            key_scores(0, 0)
            key_scores(1, 1)

            def turn(g, peer, new, old, more=True):
                t, G1, G2 = 2 * g, g - 1, g - 2
                for s in range(16):
                    if s < 4 and old:
                        hidden_f(G2, s + 4)
                    if s == 3 and new:
                        x2_T(t - 1, 1)
                    if s < 4 and old:
                        outputs2(G2, s + 3)
                    if s == 0 and old:
                        weights_cwT(2 * G2 + 1)
                    if s == 2 and old:
                        weighted_bias(2 * G2 + 1, "b2f")
                    if s == 1 and new:
                        weights_T(t - 1, 1)
                    if s == 2 and new:
                        peer_out(t - 1)
                    if s == 4 and more:
                        key_scores(t + 2, 0)
                    if s == 4 and new:
                        gate1(G1)
                        hidden1(G1, 0)
                    if s == 4 and old:
                        outputs2(G2, 7)
                    if 4 <= s < 12 and new:
                        e = s - 4
                        if e < 7:
                            hidden1(G1, e + 1)
                        if e >= 2:
                            outputs1(G1, e - 2)
                        hidden2(G1, e)
                        if e == 7:
                            outputs1(G1, 6)
                    if s == 8 and new:
                        weights_cwT(2 * G1)
                    if s == 10 and new:
                        weighted_bias(2 * G1, "b3")
                    if s == 9 and peer:
                        weights_T(t, 0)
                    if s == 10 and peer:
                        peer_out(t)
                    if s == 12:
                        if peer:
                            x2_T(t, 0)
                        if new:
                            outputs1(G1, 7)
                        if peer:
                            expert_inputs(t + 1, 1, 0)
                        if new:
                            sum_T(G1)
                        if peer:
                            expert_inputs(t + 1, 1, 1)
                        if new:
                            gate2(G1)
                            hidden_f(G1, 0)
                    if s == 13 and more:
                        key_scores(t + 3, 1)
                    if s > 12 and new:
                        hidden_f(G1, s - 12)
                        outputs2(G1, s - 13)
                    if s == 14 and more:
                        expert_inputs(t + 2, 0, 0)
                        expert_inputs(t + 2, 0, 1)

            turn(0, True, False, False)
            turn(1, True, True, False)
            with pe.Fori(2, NG - 1) as g:
                turn(g, True, True, True)
            turn(NG - 1, True, True, True, more=False)
            turn(NG, False, True, True, more=False)
            turn(NG + 1, False, False, True, more=False)

        @block.scalar
        def _(act):
            act.wait_ge(pe_setup, 2)
            act.activation(thT[:, 0:B], bank(6, 0, B), ACT.Relu, bias=A("be1")).then_inc(act_setup, 1)

            def projected(b):
                act.wait_ge(s_qk, b + 1)
                wait(act, s_S, FG * b)
                act.activation(qT, bank(0, 0, P), ACT.Identity, bias=A("bq"))
                wait(act, s_kh, FG * b)
                act.activation(kT, bank(0, P, 2 * P), ACT.Identity, bias=A("bk")).then_inc(s_q, 1)
                act.wait_ge(s_proj, b + 1)
                wait(act, s_v, b)
                act.activation(v_stage, bank(7, 0, P), ACT.Copy).then_inc(s_vst, 1)
                wait(act, s_coh, b)
                act.activation(thT, bank(7, P, 2 * P), ACT.Tanh, bias=col(hidb, b)).then_inc(s_tanh, 1)

            def exps(b, r):
                act.wait_ge(s_D, FG * b + r + 1)
                act.activation(D[r], D[r], ACT.Exp, scale=float(HD) ** -0.5).then_inc(s_E, 1)

            def probs_T(b, r):
                act.wait_ge(s_T, FG * b + r + 1)
                wait(act, s_pv, FG * (b - 1) + r + 1)
                act.activation(ET[r], bank(2 + r), ACT.Copy).then_inc(s_ET, 1)

            def out_T(b):
                act.wait_ge(s_oTp, b + 1)
                wait(act, s_x1p, b)
                act.activation(oT, bank(6, 144, 272), ACT.Copy, accum_out=col(o_sum, b)).then_inc(s_oT, 1)

            def out_x1(b):
                act.wait_ge(s_x1p, b + 1)
                act.activation(cols(x1T_all, b), bank(6, 144, 272), ACT.Identity, bias=A("bout"),
                               accum_out=col(x1_sum, b)).then_inc(s_x1, 1)

            def out_query(c):
                act.wait_ge(pe_setup, PE_SETUP.index(f"U{c}") + 1)
                act.activation(U[:, 512 * c:512 * c + 512], bank((2, 3, 1, 0)[c]), ACT.Copy).then_inc(act_setup, 1)

            def attend(b, more, project_more, first=False):
                probs_T(b, 0)
                probs_T(b, 1)
                if not first:
                    out_T(b - 1)
                probs_T(b, 2)
                probs_T(b, 3)
                if first:
                    out_query(2)
                    out_query(3)
                else:
                    out_x1(b - 1)
                act.wait_ge(s_tl, b + 1)
                wait(act, s_cden, b)
                act.activation(ec, tl, ACT.Exp, scale=-1.0).then_inc(s_ec, 1)
                if more:
                    for r in range(FG):
                        exps(b + 1, r)
                if project_more:
                    projected(b + 2)

            act.wait_ge(pe_setup, PE_SETUP.index("field2") + 1)
            projected(0)
            out_query(0)
            act.wait_ge(dve_setup, DVE_SETUP.index("field_max") + 1)
            act.activation(field_a[0:B, :], banks[0:B, 6, 0:P], ACT.Exp, bias=small[0:B, 10:11],
                           accum_out=small[0:B, 11:12]).then_inc(act_setup, 1)
            out_query(1)
            for r in range(FG):
                exps(0, r)
            projected(1)
            attend(0, True, True, first=True)
            with act.Fori(1, B - 2) as b:
                attend(b, True, True)
            attend(B - 2, True, False)
            attend(B - 1, False, False)
            out_T(B - 1)
            out_x1(B - 1)

            def exp_pairs(t, a, h):
                hs = 8 * t + h
                act.wait_ge(h_S, hs + 1)
                if h == 0:
                    act.wait_ge(t_top, t + 1)
                wait(act, h_w, hs - RING + 1)
                act.activation(E[h], S[h], ACT.Exp, bias=neg_max[a][:, h:h + 1]).then_inc(h_E, 1)

            def first_weights(t, a):
                act.wait_ge(h_me, 8 * t + 1)
                act.wait_ge(t_rz, t + 1)
                act.wait_ge(h_w, 8 * t)
                wait(act, t_Tp, t - 1)
                act.activation(W[a], E[0], ACT.Copy, scale=rz[a][:, 0:1]).then_inc(h_w, 1)

            def exp_top(t):
                act.wait_ge(t_top, t + 1)
                wait(act, t_zs, t)
                act.activation(etop[:, :, :], dtop[:, :, :], ACT.Exp).then_inc(t_ez, 1)

            def expert_inputs(t, a):
                act.wait_ge(t_Hp, 2 * t + 2)
                wait(act, t_P, t - 1)
                act.activation(G[a], banks[:, 0:2, :].rearrange("p c n -> p (c n)"),
                               ACT.Gelu_apprx_tanh).then_inc(t_G, 1)

            def weights_T(t):
                act.wait_ge(t_Tp, t + 1)
                wait(act, t_x2p, t)
                act.activation(PT[:, :], banks[:, 0:2, :].rearrange("p c n -> p (c n)"), ACT.Copy).then_inc(t_PT, 1)

            def load_table(function, n):
                wait(act, tables, n)
                act.activation(unused[:, :], ident[:, 0:1], function).then_inc(tables, 1)

            def squares(t, a):
                act.wait_ge(t_x2, t + 1)
                wait(act, t_ssq, t)
                act.activation(square[:, :], x2s[a][:, :], ACT.Square, accum_out=ssq[:, a:a + 1]).then_inc(t_ssq, 1)

            def x2_T(t, a, Gn):
                act.wait_ge(t_trp, t + 1)
                wait(act, e_h1, 8 * Gn)
                act.activation(x2T[:, P * a:P * a + P], bank(6, P, 2 * P), ACT.Copy).then_inc(t_x2T, 1)

            def hidden2(Gn, e):
                act.wait_ge(e_h2, 8 * Gn + e + 1)
                wait(act, e_y, 16 * Gn + e - 1)
                for n in range(2):
                    m = act.activation(H2[e % 2][:, n, :], bank(3, 256 * n, 256 * n + 256), ACT.Relu,
                                       bias=L("b2", 2 * e + n, 2 * e + n + 1))
                m.then_inc(e_r2, 1)

            def sum_T(Gn):
                act.wait_ge(g_cTp, Gn + 1)
                wait(act, e_hf, 16 * Gn)
                act.activation(cT[:, :], bank(7, 0, 256), ACT.Copy).then_inc(g_cT, 1)

            def gate1_exp(Gn):
                act.wait_ge(g_lg, Gn + 1)
                act.activation(lexp[:, :, :], lg[:, :, :], ACT.Exp).then_inc(g_exp1, 1)

            def gate2_exp(Gn):
                act.wait_ge(g_g2p, Gn + 1)
                act.activation(lexp[:, :, :].rearrange("p a e -> p (a e)"), bank(7, 0, 16), ACT.Exp,
                               scale=-1.0).then_inc(g_exp2, 1)

            def hidden1(Gn, e):
                act.wait_ge(e_h1, 8 * Gn + e + 1)
                wait(act, e_h2, 8 * Gn + e - 1)
                for n in range(2):
                    m = act.activation(H1[e % 2][:, n, :], bank(2, 256 * n, 256 * n + 256), ACT.Relu,
                                       bias=L("b1", 2 * e + n, 2 * e + n + 1))
                m.then_inc(e_r1, 1)

            def hidden_f(Gn, e):
                for b in range(2):
                    act.wait_ge(e_hf, 16 * Gn + 2 * e + b + 1)
                    if b == 0:
                        wait(act, e_y, 16 * Gn + 8 + e - 1)
                    for f in range(2 * b, 2 * b + 2):
                        m = act.activation(HF[e % 2][:, f, :], bank(2 + b, 256 * (f % 2), 256 * (f % 2) + 256),
                                           ACT.Gelu_apprx_tanh, bias=L("bf", 4 * e + f, 4 * e + f + 1))
                    m.then_inc(e_g, 1)

            act.wait_ge(ld_l, 48)
            load_table(ACT.Gelu_apprx_tanh, 0)
            act.wait_ge(pe_norm, NORM_PE.index("var3") + 1)
            expert_inputs(0, 0)
            act.wait_ge(pe_norm, NORM_PE.index("weff0") + 1)
            act.activation(weff[:, 0:256], bank(2, 0, 256), ACT.Copy).then_inc(act_norm, 1)
            load_table(ACT.Exp, 1)
            exp_top(0)
            for h in range(4):
                exp_pairs(0, 0, h)

            EXPS = {4: [5], 5: [6, 7], 6: [8], 7: [9, 10], 8: [11, 12], 9: [13], 10: [14, 15], 11: [16, 17],
                    12: [18, 19]}

            def turn(g, peer, new, old, more=True):
                t, G1, G2 = 2 * g, g - 1, g - 2
                for s in range(16):
                    if s < 4 and old:
                        hidden_f(G2, s + 4)
                    if s == 1 and new:
                        weights_T(t - 1)
                    if s == 3 and new:
                        x2_T(t - 1, 1, G1)
                        squares(t - 1, 1)
                    if s == 4 and peer:
                        exp_pairs(t, 0, 4)
                    if s == 4 and new:
                        hidden1(G1, 0)
                    if s == 4 and peer:
                        exp_top(t + 1)
                    if 4 <= s < 11 and new:
                        hidden1(G1, s - 3)
                    if s == 5 and new:
                        gate1_exp(G1)
                    if s == 11 and more:
                        exp_top(t + 2)
                    if peer:
                        for h in EXPS.get(s, []):
                            if h < 16 or more:
                                exp_pairs(t + h // 8, h // 8 % 2, h % 8)
                    if s == 9 and peer:
                        first_weights(t + 1, 1)
                    if 4 <= s < 12 and new:
                        hidden2(G1, s - 4)
                    if s == 9 and peer:
                        weights_T(t)
                    if s == 12 and peer:
                        x2_T(t, 0, g)
                        wait(act, g_msq, g)
                        squares(t, 0)
                    if s == 12 and new:
                        sum_T(G1)
                        gate2_exp(G1)
                        load_table(ACT.Gelu_apprx_tanh, g + 1)
                    if s >= 12 and new:
                        hidden_f(G1, s - 12)
                    if s == 12 and peer:
                        expert_inputs(t + 1, 1)
                    if s == 14 and more:
                        expert_inputs(t + 2, 0)

            turn(0, True, False, False)
            turn(1, True, True, False)
            with act.Fori(2, NG - 1) as g:
                turn(g, True, True, True)
            turn(NG - 1, True, True, True, more=False)
            turn(NG, False, True, True, more=False)
            turn(NG + 1, False, False, True, more=False)

        @block.vector
        def _(v):
            def setup_done(name):
                v.wait_ge(dve_setup, DVE_SETUP.index(name) + 1)

            v.memset(small, 0.0).then_inc(dve_setup, 1)
            v.wait_ge(ld_a, 16)
            v.wait_ge(ld_c, 16)
            v.wait_ge(ld_r, 16)
            cs = C("csT").unsqueeze(2).broadcast_to([CD, B, NE])
            gg = C("ggW").unsqueeze(1).broadcast_to([CD, B, NE])
            v.tensor_tensor(gate_rhs[0:CD, :].rearrange("p (b o) -> p b o", b=B), cs, gg, ALU.mult).then_inc(dve_setup, 1)
            v.wait_ge(pe_setup, 1)
            v.tensor_scalar(hidb, bank(7, 0, B), A("bc1"), None, ALU.add).then_inc(dve_setup, 1)
            v.tensor_tensor(gate_rows, R("wgb"), R("ggb"), ALU.add).then_inc(dve_setup, 1)
            setup_done("gate_rows")
            v.wait_ge(pe_setup, PE_SETUP.index("gate_bias") + 1)
            v.tensor_tensor(gate_bias[:, :, :], bank(5, 0, P).rearrange("p (b o) -> p b o", b=B),
                            gate_rows.unsqueeze(1).broadcast_to([P, B, NE]), ALU.add).then_inc(dve_setup, 1)
            v.wait_ge(pe_setup, PE_SETUP.index("field2") + 1)
            v.tensor_tensor(field_a[0:B, :], banks[0:B, 1, 0:P], R("be2", B), ALU.add).then_inc(dve_setup, 1)
            setup_done("f2")
            v.bn_stats(small[0:B, 0:6], field_a[0:B, :]).then_inc(dve_setup, 1)
            setup_done("stats")
            v.bn_aggr(small[0:B, 6:8], small[0:B, 0:6]).then_inc(dve_setup, 1)
            setup_done("aggr")
            v.tensor_scalar(small[0:B, 8:9], small[0:B, 7:8], 1e-5, None, ALU.add).then_inc(dve_setup, 1)
            v.wait_ge(pool_setup, 5)
            v.tensor_scalar(field_b[0:B, :], field_a[0:B, :], small[0:B, 6:7], small[0:B, 9:10],
                            ALU.subtract, ALU.mult).then_inc(dve_setup, 1)
            setup_done("f3")
            v.tensor_tensor(field_a[0:B, :], field_b[0:B, :], R("ln_g", B), ALU.mult).then_inc(dve_setup, 1)
            setup_done("f4g")
            v.tensor_tensor(field_b[0:B, :], field_a[0:B, :], R("ln_b", B), ALU.add).then_inc(dve_setup, 1)
            v.wait_ge(pe_setup, PE_SETUP.index("fpT") + 1)
            v.tensor_copy(fpT, bank(1, 0, B)).then_inc(dve_setup, 1)
            v.wait_ge(pe_setup, PE_SETUP.index("field_scores") + 1)
            v.tensor_reduce(small[0:B, 10:11], banks[0:B, 6, 0:P], AX_X, ALU.max, negate=True).then_inc(dve_setup, 1)
            v.wait_ge(act_setup, ACT_SETUP.index("field_exp") + 1)
            v.reciprocal(small[0:B, 12:13], small[0:B, 11:12]).then_inc(dve_setup, 1)
            setup_done("fa_recip")
            v.tensor_scalar(fa[0:B, :], field_a[0:B, :], small[0:B, 12:13], FIELD, ALU.mult, ALU.mult).then_inc(dve_setup, 1)
            v.wait_ge(pe_setup, PE_SETUP.index("faT") + 1)
            v.tensor_copy(fas, bank(1, 0, B)).then_inc(dve_setup, 1)

            quarter = lambda ap: ap.rearrange("p (g n) -> p g n", g=FG)

            def row_max(b, r):
                v.wait_ge(s_S, FG * b + r + 1)
                v.tensor_reduce(mx4[:, FG * r:FG * r + FG], quarter(bank(2 + r)), AX_X, ALU.max).then_inc(s_mx, 1)

            def minus_max(b, r):
                v.wait_ge(s_mx, FG * b + r + 1)
                wait(v, s_T, FG * (b - 1) + r + 1)
                v.tensor_tensor(quarter(D[r]), quarter(bank(2 + r)),
                                mx4[:, FG * r:FG * r + FG].unsqueeze(2).broadcast_to([P, FG, P]),
                                ALU.subtract).then_inc(s_D, 1)

            def shifted_scores(b):
                row_max(b, 0)
                row_max(b, 1)
                minus_max(b, 0)
                row_max(b, 2)
                minus_max(b, 1)
                row_max(b, 3)
                minus_max(b, 2)
                minus_max(b, 3)

            def attend(b, more):
                v.wait_ge(s_coh, b + 1)
                wait(v, s_ec, b)
                v.tensor_tensor(tl, bank(1, 0, NH), R("bc2"), ALU.add).then_inc(s_tl, 1)
                if more:
                    shifted_scores(b + 1)
                v.wait_ge(s_ec, b + 1)
                v.tensor_scalar(cden, ec, 1e-8 / (1 - FIELD), (1 + 1e-8) / (1 - FIELD), ALU.mult, ALU.add).then_inc(s_cden, 1)
                v.wait_ge(s_pv, FG * b + FG)
                v.wait_ge(s_cden, b + 1)
                o9 = bank(6, 0, 144).rearrange("p (h d) -> p h d", d=9)
                v.tensor_tensor(zden.unsqueeze(2), o9[:, :, HD:HD + 1], cden.unsqueeze(2), ALU.mult).then_inc(s_zd, 1)
                v.wait_ge(s_zd, b + 1)
                v.reciprocal(rz_att, zden).then_inc(s_rz, 1)
                v.wait_ge(s_rz, b + 1)
                v.tensor_tensor(o_n.rearrange("p (h d) -> p h d", d=HD), o9[:, :, 0:HD],
                                rz_att.unsqueeze(2).broadcast_to([P, NH, HD]), ALU.mult).then_inc(s_on, 1)
                v.wait_ge(s_on, b + 1)
                v.wait_ge(s_vs, b + 1)
                wait(v, s_oTp, b)
                wait(v, s_ostore, b)
                v.scalar_tensor_tensor(o_s, bank(6, 384, 512), col(fas, b), o_n, ALU.mult, ALU.add).then_inc(s_os, 1)

            v.wait_ge(pool_setup, 5)
            setup_done("faT")
            shifted_scores(0)
            attend(0, True)
            with v.Fori(1, B - 1) as b:
                attend(b, True)
            attend(B - 1, False)

            def norm_done(name):
                v.wait_ge(dve_norm, NORM_DVE.index(name) + 1)

            v.wait_ge(s_oT, B)
            v.tensor_reduce(small[:, 16:17], o_sum, AX_X, ALU.add).then_inc(dve_norm, 1)
            norm_done("mean_col")
            v.tensor_scalar(mean_bc, ones, small[:, 16:17], 1.0 / TOK, ALU.mult, ALU.mult).then_inc(dve_norm, 1)
            v.wait_ge(s_ostore, B)
            v.wait_ge(pe_norm, NORM_PE.index("mean_row") + 1)
            for c in range(4):
                four = lambda ap: ap[:, 512 * c:512 * c + 512].rearrange("p (t n) -> p t n", t=4)
                v.tensor_tensor(four(o_c), four(o_all), bank(7, 0, P).unsqueeze(1).broadcast_to([P, 4, P]),
                                ALU.subtract).then_inc(dve_norm, 1)
            v.wait_ge(s_x1, B)
            v.tensor_reduce(small[:, 17:18], x1_sum, AX_X, ALU.add).then_inc(dve_norm, 1)
            norm_done("x1mean")
            v.tensor_scalar(x1neg, ones, small[:, 17:18], -1.0 / TOK, ALU.mult, ALU.mult).then_inc(dve_norm, 1)
            k3 = lambda ap: ap.rearrange("p (c k) -> p c k", k=NK)
            v.tensor_tensor(k3(kb), k3(A("keysT")), A("beta").unsqueeze(2).broadcast_to([P, 16, NK]), ALU.mult).then_inc(dve_norm, 1)
            v.wait_ge(ld_l, 48)
            v.tensor_scalar(L("wgr"), L("wgr"), L("rms"), None, ALU.mult).then_inc(dve_norm, 1)
            v.wait_ge(pe_norm, NORM_PE.index("cov") + 1)
            v.tensor_scalar(cov, bank(6, 0, P), 1.0 / TOK, None, ALU.mult).then_inc(dve_norm, 1)

            def products(c):
                v.wait_ge(pe_norm, NORM_PE.index(f"CU{c}") + 1)
                v.tensor_tensor(T[:, 512 * c:512 * c + 512], bank(2 + c), U[:, 512 * c:512 * c + 512],
                                ALU.mult).then_inc(dve_norm, 1)

            def variance(c):
                v.wait_ge(pe_norm, NORM_PE.index(f"var{c}") + 1)
                v.tensor_scalar(small[:, 4 * c:4 * c + 4], bank(2 + c, 0, 4), 1e-5, None, ALU.add).then_inc(dve_norm, 1)

            def scaled_keys(c):
                v.wait_ge(pool_norm, c + 1)
                v.tensor_tensor(scale_a[:, 4 * c:4 * c + 4], rstd[:, 4 * c:4 * c + 4], A("gamma", 4 * c, 4 * c + 4),
                                ALU.mult).then_inc(dve_norm, 1)
                norm_done(f"scale{c}")
                v.tensor_tensor(k3(ka[:, P * c:P * c + P]), k3(A("keysT", P * c, P * c + P)),
                                scale_a[:, 4 * c:4 * c + 4].unsqueeze(2).broadcast_to([P, 4, NK]), ALU.mult).then_inc(dve_norm, 1)

            products(0)
            products(1)
            variance(0)
            products(2)
            variance(1)
            products(3)
            variance(2)
            variance(3)
            for c in range(4):
                scaled_keys(c)
            v.wait_ge(pe_norm, NORM_PE.index("weff1") + 1)
            v.tensor_copy(weff[:, 256:512], bank(3, 0, 256)).then_inc(dve_norm, 1)
            v.wait_ge(pe_norm, NORM_PE.index("sim_bias") + 1)
            v.tensor_copy(sim_bias[:, :], bank(7)).then_inc(dve_norm, 1)
            norm_done("sim_bias")

            def key_sums(t, a):
                v.wait_ge(t_simp, t + 1)
                wait(v, h_S, 8 * t - 8)
                v.tensor_tensor(sim[a][:, :, :].rearrange("p c k -> p (c k)"), bank(6), sim_bias[:, :],
                                ALU.add).then_inc(topk, 1)

            def top_keys_of(t, a):
                v.wait_ge(topk, 1)
                v.max(top_keys[:, 0, :], sim[a][:, 0, :]).then_inc(t_simr, 1)
                for c in range(1, 16):
                    m = v.max(top_keys[:, c, :], sim[a][:, c, :])
                m.then_inc(topk, 1)

            def pair_sums():
                v.wait_ge(topk, 2)
                v.tensor_tensor(pairs[:, :, :, :],
                                top_keys[:, 0:PH, :].unsqueeze(3).broadcast_to([P, PH, 8, 8]),
                                top_keys[:, PH:16, :].unsqueeze(2).broadcast_to([P, PH, 8, 8]), ALU.add).then_inc(topk, 1)

            def top_pairs(t, a):
                v.wait_ge(topk, 3)
                for h in range(PH):
                    m = v.max(top[a][:, h, :], pairs[:, h, :, :].rearrange("p a b -> p (a b)"))
                m.then_inc(topk, 1)
                v.wait_ge(topk, 4)
                v.sem_clear(topk)
                wait(v, h_E, 8 * t - 8)
                v.tensor_scalar(neg_max[a][:, :].unsqueeze(2), top[a][:, :, 0:1], -1.0, None, ALU.mult).then_inc(t_sim, 1)
                wait(v, t_ez, t)
                v.tensor_tensor(dtop[:, :, :], top[a][:, :, :], top[a][:, :, 0:1].broadcast_to([P, PH, 8]),
                                ALU.subtract).then_inc(t_top, 1)

            def top_sums(t, a):
                v.wait_ge(t_ez, t + 1)
                v.tensor_reduce(zsum[:, :], etop[:, :, :], AX_X, ALU.add).then_inc(t_zs, 1)
                v.wait_ge(t_zs, t + 1)
                v.reciprocal(rz[a][:, :], zsum[:, :]).then_inc(t_rz, 1)

            def mask(t, a, h):
                hs = 8 * t + h
                v.wait_ge(h_E, hs + 1)
                v.scalar_tensor_tensor(E[h], S[h], top[a][:, h, 7:8], E[h], ALU.is_ge, ALU.mult).then_inc(h_me, 1)

            def add_weights(t, a, h):
                hs = 8 * t + h
                v.wait_ge(h_me, hs + 1)
                if h == 0:
                    v.wait_ge(t_rz, t + 1)
                    wait(v, t_Tp, t - 1)
                    v.tensor_scalar(W[a], E[h], rz[a][:, 0:1], None, ALU.mult).then_inc(h_w, 1)
                else:
                    v.wait_ge(h_w, hs)
                    v.scalar_tensor_tensor(W[a], E[h], rz[a][:, h:h + 1], W[a], ALU.mult, ALU.add).then_inc(h_w, 1)

            def add_peer(t, a):
                v.wait_ge(t_x2p, t + 1)
                wait(v, t_xst, t - 1)
                wait(v, t_ssq, t - 1)
                wait(v, t_trp, t - 1)
                v.tensor_tensor(x2s[a][:, :], bank(6, 0, P), tile_of(x_all, t), ALU.add).then_inc(t_x2, 1)

            def mean_square(Gn):
                v.wait_ge(t_ssq, 2 * Gn + 2)
                wait(v, g_rms, Gn)
                v.tensor_scalar(msq[:, :], ssq[:, :], 1.0 / P, 1e-6, ALU.mult, ALU.add).then_inc(g_msq, 1)

            def logits(Gn):
                v.wait_ge(g_rms, Gn + 1)
                v.wait_ge(g_g1p, Gn + 1)
                wait(v, g_exp1, Gn)
                for a in range(2):
                    m = v.scalar_tensor_tensor(lg[:, a, :], bank(7, 8 * a, 8 * a + 8), rms[:, a:a + 1],
                                               tile_of(gate_bias, 2 * Gn + a), ALU.mult, ALU.add)
                m.then_inc(gate, 1)

            def logit_max():
                v.wait_ge(gate, 1)
                v.tensor_reduce(lmax[:, :], lg[:, :, :], AX_X, ALU.max).then_inc(gate, 1)

            def minus_logit_max():
                v.wait_ge(gate, 2)
                v.tensor_tensor(lg[:, :, :], lg[:, :, :], lmax[:, :].unsqueeze(2).broadcast_to([P, 2, NE]),
                                ALU.subtract).then_inc(g_lg, 1)

            def exp_sum(Gn):
                v.wait_ge(g_exp1, Gn + 1)
                v.tensor_reduce(lsum[:, :], lexp[:, :, :], AX_X, ALU.add).then_inc(gate, 2)

            def exp_recip():
                v.wait_ge(gate, 4)
                v.reciprocal(lmax[:, :], lsum[:, :]).then_inc(gate, 1)

            def probabilities():
                v.wait_ge(gate, 5)
                v.tensor_tensor(prob[:, :, :], lexp[:, :, :], lmax[:, :].unsqueeze(2).broadcast_to([P, 2, NE]),
                                ALU.mult).then_inc(gate, 1)

            def sigmoid_den(Gn):
                v.wait_ge(g_exp2, Gn + 1)
                v.tensor_scalar(lg[:, :, :], lexp[:, :, :], 1.0, None, ALU.add).then_inc(gate, 5)

            def sigmoid():
                v.wait_ge(gate, 5)
                v.reciprocal(prob[:, :, :], lg[:, :, :]).then_inc(gate, 1)

            def two_best():
                v.wait_ge(gate, 6)
                for a in range(2):
                    m = v.max(best[:, a, :], prob[:, a, :])
                m.then_inc(gate, 1)

            def two_best_at():
                v.wait_ge(gate, 7)
                for a in range(2):
                    m = v.max_index(besti[:, a, :], best[:, a, :], prob[:, a, :])
                m.then_inc(gate, 1)

            def index_values():
                v.wait_ge(gate, 8)
                v.tensor_copy(bestf[:, :, :], besti[:, :, :]).then_inc(gate, 1)

            def picks(n):
                v.wait_ge(gate, 9)
                wait(v, g_cwTp, n)
                wait(v, e_acc, 8 * n)
                for a in range(2):
                    v.scalar_tensor_tensor(pick[:, a, :], iota8[:, :], bestf[:, a, 0:1], prob[:, a, :], ALU.is_equal, ALU.mult)
                for a in range(2):
                    m = v.scalar_tensor_tensor(cw[:, a, :], iota8[:, :], bestf[:, a, 1:2], prob[:, a, :], ALU.is_equal, ALU.mult)
                m.then_inc(gate, 1)

            def gate_weights():
                v.wait_ge(gate, 10)
                v.sem_clear(gate)
                v.tensor_tensor(cw[:, :, :], cw[:, :, :], pick[:, :, :], ALU.add).then_inc(g_cw, 1)

            def weights_T(n):
                v.wait_ge(g_cwTp, n + 1)
                wait(v, g_bias, n)
                v.tensor_copy(cwT[:, :], banks[0:NE, 7, 0:2 * P]).then_inc(g_cwT, 1)

            def add_bias(Gn, layer):
                dst = (acc, acc_f)[layer]
                v.wait_ge(g_bias, 2 * Gn + layer + 1)
                v.wait_ge(e_acc, 16 * Gn + 8 * layer + 5)
                v.tensor_tensor(dst[:, :, :], bank(7, 256, 512).rearrange("p (a n) -> p a n", a=2), dst[:, :, :],
                                ALU.add).then_inc(g_badd, 1)

            def add_expert(Gn, n):
                e, layer = n % 8, n // 8
                v.wait_ge(e_y, 16 * Gn + n + 1)
                if n == 0:
                    wait(v, g_cTp, Gn)
                if n == 8:
                    wait(v, g_out, 32 * Gn)
                    v.wait_ge(t_xst, 2 * Gn + 2)
                if e == 0:
                    v.wait_ge(g_cw, 2 * Gn + 1 + layer)
                elif e == 5:
                    v.wait_ge(g_badd, 2 * Gn + 1 + layer)
                else:
                    v.wait_ge(e_acc, 16 * Gn + n)
                dst = (acc, acc_f)[layer]
                for a in range(2):
                    y, weight = bank(4 + n % 2, P * a, P * a + P), cw[:, a, e:e + 1]
                    if n == 0:
                        m = v.tensor_scalar(dst[:, a, :], y, weight, None, ALU.mult)
                    else:
                        base = tile_of(x_all, 2 * Gn + a) if n == 8 else dst[:, a, :]
                        m = v.scalar_tensor_tensor(dst[:, a, :], y, weight, base, ALU.mult, ALU.add)
                m.then_inc(e_acc, 1)

            key_sums(0, 0)
            top_keys_of(0, 0)
            pair_sums()
            top_pairs(0, 0)
            key_sums(1, 1)
            top_keys_of(1, 1)
            top_sums(0, 0)

            ADDS = {6: [0], 7: [1], 8: [2], 9: [3], 10: [4], 11: [5], 14: [8], 15: [9]}
            OLD_ADDS = {0: [10], 1: [11], 2: [12], 3: [13], 4: [14, 15]}

            def turn(g, peer, new, old, more=True):
                t, G1, G2 = 2 * g, g - 1, g - 2
                for s in range(16):
                    if s == 12:
                        if peer:
                            add_weights(t + 1, 1, 3)
                        if new:
                            add_expert(G1, 6)
                            add_expert(G1, 7)
                    if s == 4 and peer:
                        top_pairs(t + 1, 1)
                    if s == 4 and new:
                        mean_square(G1)
                    if s == 4 and more:
                        key_sums(t + 2, 0)
                        top_keys_of(t + 2, 0)
                    if peer:
                        mask(t + s // 8, s // 8, s % 8)
                    if s == 3 and peer:
                        pair_sums()
                    if s == 3 and new:
                        add_peer(t - 1, 1)
                    if s == 11 and peer:
                        add_peer(t, 0)
                    if new:
                        if s == 6:
                            probabilities()
                            two_best()
                        if s == 9:
                            weights_T(2 * G1)
                        if s == 11:
                            add_bias(G1, 0)
                        if s == 13:
                            sigmoid_den(G1)
                            sigmoid()
                        if s == 14:
                            index_values()
                            picks(2 * G1 + 1)
                    if s == 14 and more:
                        top_keys_of(t + 3, 1)
                    if s == 3 and old:
                        add_bias(G2, 1)
                    if peer and s not in (0, 9, 12):
                        add_weights(t + (s - 1) // 8, (s - 1) // 8, (s - 1) % 8)
                    if new and s == 0:
                        add_weights(t - 1, 1, 7)
                    if new:
                        if s == 4:
                            logits(G1)
                            logit_max()
                            minus_logit_max()
                        if s == 5:
                            exp_sum(G1)
                            exp_recip()
                        if s == 6:
                            two_best_at()
                            index_values()
                            picks(2 * G1)
                            gate_weights()
                        if s == 13:
                            two_best()
                            two_best_at()
                        if s == 14:
                            gate_weights()
                    if s == 1 and old:
                        weights_T(2 * G2 + 1)
                    if old:
                        for n in OLD_ADDS.get(s, []):
                            add_expert(G2, n)
                    if new:
                        for n in ADDS.get(s, []):
                            add_expert(G1, n)
                    if more:
                        if s == 9:
                            pair_sums()
                        if s == 10:
                            top_pairs(t + 2, 0)
                        if s == 13:
                            top_sums(t + 2, 0)
                            key_sums(t + 3, 1)
                    if peer:
                        if s == 6:
                            top_sums(t + 1, 1)

            turn(0, True, False, False)
            turn(1, True, True, False)
            with v.Fori(2, NG - 1) as g:
                turn(g, True, True, True)
            turn(NG - 1, True, True, True, more=False)
            turn(NG, False, True, True, more=False)
            turn(NG + 1, False, False, True, more=False)


def kernel(**inputs):
    import numpy as _np
    import concourse.bacc as _bacc
    from concourse import mybir as _mybir
    from concourse.bass_utils import run_bass_kernel_spmd as _run

    i = {k: _np.asarray(v) for k, v in inputs.items()}
    c0, f0, c1, f1 = (lambda n, p=p: i[p + n] for p in ("L0_cond_", "L0_ffn_", "L1_cond_", "L1_ffn_"))
    f32 = _np.float32

    def side(parts, widths):
        return _np.concatenate([_np.reshape(parts[n], (-1, w)) for n, w in widths.items()], axis=1)

    WT = c0("Wqkv").T
    bqkv = c0("bqkv")
    pos = _np.arange(P, dtype=f32)
    inv = _np.power(f32(10000.0), _np.repeat(_np.arange(0, P, 2, dtype=f32) / f32(P), 2))
    pe = _np.sin(pos[:, None] / inv[None, :]).astype(f32)
    pA = side(dict(
        wqT=WT[:, 0:P], wkT=WT[:, P:2 * P], wvT=WT[:, 2 * P:], bq=bqkv[0:P], bk=bqkv[P:2 * P],
        head_of=_np.repeat(_np.eye(NH, dtype=f32), HD, axis=0),
        woT=c0("Wout").T, wo=c0("Wout"), wc1T=c0("Wc1")[:, :P].T, wc2T=c0("Wc2").T, we2T=c0("We2").T,
        peT=pe.T, ident=_np.eye(P, dtype=f32), bout=c0("bout"), bc1=c0("bc1"), be1=c0("be1"),
        gamma=f0("bn_gamma").reshape(16, P).T, beta=f0("bn_beta").reshape(16, P).T,
        keysT=f0("keys").transpose(3, 2, 0, 1)), COLS_A)
    pL = side(dict(
        b1=c1("b1").reshape(16, P).T, b2=c1("b2").reshape(16, P).T, bf=f1("b1").reshape(32, P).T,
        wgr=c1("wg_W"), rms=c1("rms_w"), wgf=f1("Wg")), COLS_L)
    pC = side(dict(wc1c=c0("Wc1")[:, P:].T, csT=i["cond_256"].T, we1T=c0("We1").T, ggW=c1("gg_W")), COLS_C)
    pR = side(dict(bv=bqkv[2 * P:], bc2=c0("bc2"), be2=c0("be2"), ln_g=c0("ln_g"), ln_b=c0("ln_b"),
                   wgb=c1("wg_b"), ggb=c1("gg_b")), COLS_R)
    p8 = side(dict(b3=c1("b3"), b2f=f1("b2")), COLS_8)
    x = i["x"]
    w_q = f0("w_q")
    arrays = dict(
        xtok=x, xT=x.reshape(TOK, P).T, pA=pA, pL=pL, pC=pC, pR=pR, p8=p8, wq=w_q,
        wqT=w_q.reshape(P, 16, P).transpose(2, 1, 0).reshape(P, 16 * P),
        down=f0("down_embed").T, up=f0("up_embed"), w1=c1("W1"), w2=c1("W2"), w3=c1("W3"),
        f1=f1("W1"), f2=f1("W2"))
    nc = _bacc.Bacc("TRN2", target_bir_lowering=False, num_devices=1)
    maps, args = {}, []
    for name, a in arrays.items():
        a = _np.ascontiguousarray(a)
        maps[f"in_{name}"] = a
        args.append(nc.dram_tensor(f"in_{name}", a.shape, _mybir.dt.from_np(a.dtype), kind="ExternalInput").ap())
    args.append(nc.dram_tensor("out_x", (B, P, P), F32, kind="ExternalOutput").ap())
    program(nc, *args)
    r = _run(nc, [maps], core_ids=[0])
    return r.results[0]["out_x"]
```
